# Optimizing a Trainium2 kernel written in Bass

```python
import numpy as np
import jax
import jax.numpy as jnp

def _softmax(x, axis=-1):
    return jax.nn.softmax(x, axis=axis)

def _gelu(x):
    return jax.nn.gelu(x, approximate=True)

def _silu(x):
    return jax.nn.silu(x)

def _sigmoid(x):
    return jax.nn.sigmoid(x)

def _layernorm(x, axis=-1, eps=1e-05):
    m = jnp.mean(x, axis=axis, keepdims=True)
    v = jnp.var(x, axis=axis, keepdims=True)
    return (x - m) / jnp.sqrt(v + eps)

def _scatter_add(tgt, idx, src, axis=0):
    return tgt.at[idx].add(src)

def _segment_sum(src, seg, n):
    return jax.ops.segment_sum(src, seg, n)
kernel_name = 'mk_gps_d2_gnn_r8_f279df'

def setup_inputs(seed: int=0):
    np.random.seed(seed)
    _w = jnp.asarray

    def _rec_inputs():
        import jax
        import jax.numpy as jnp
        _gk = jax.random.key(seed)
        x = -0.0002117 + 1 * jax.random.normal(jax.random.fold_in(_gk, 1), (6250, 256), jnp.float32)
        _s = jax.random.randint(jax.random.fold_in(_gk, 2), (50000,), 0, 6250, jnp.int32)
        _d = jax.random.randint(jax.random.fold_in(_gk, 3), (50000,), 0, 6250, jnp.int32)
        _loop = jnp.arange(6250, dtype=jnp.int32)
        src = jnp.concatenate([_s, _d, _loop])
        dst = jnp.concatenate([_d, _s, _loop])
        _o = jnp.argsort(dst, stable=True)
        src = src[_o]
        dst = dst[_o]
        return (x, src, dst)
    x, src, dst = _rec_inputs()

    def _L0_gnn_setup():
        import jax, jax.numpy as jnp
        import numpy as np
        N_NODES = 12500
        key = jax.random.key(seed)
        ks = jax.random.split(key, 5)
        features = jax.random.normal(ks[0], (N_NODES, 256), dtype=jnp.float32)
        src = jax.random.randint(ks[1], (200000,), 0, N_NODES, dtype=jnp.int32)
        dst = jax.random.randint(ks[2], (200000,), 0, N_NODES, dtype=jnp.int32)
        W_gcn = jax.random.normal(ks[3], (256, 64), dtype=jnp.float32) * (1.0 / np.sqrt(256))
        b_gcn = jnp.zeros((64,), dtype=jnp.float32)
        W_out = jax.random.normal(ks[4], (64, 256), dtype=jnp.float32) * (1.0 / np.sqrt(64))
        b_out = jnp.zeros((256,), dtype=jnp.float32)
        return {'features': features, 'src': src, 'dst': dst, 'W_gcn': W_gcn, 'b_gcn': b_gcn, 'W_out': W_out, 'b_out': b_out}
    _L0_gnn_all = _L0_gnn_setup()
    _L0_gnn_in = {k: v for k, v in _L0_gnn_all.items() if k in ('W_gcn', 'b_gcn', 'W_out', 'b_out')}
    del _L0_gnn_all

    def _L0_mix_setup():
        import jax, jax.numpy as jnp
        import numpy as np
        MIDC = 256
        HEADS = 8
        HEADC = MIDC // HEADS
        EPS = 1e-05

        def _ln(x, gamma, beta):
            mu = jnp.mean(x, axis=-1, keepdims=True)
            var = jnp.var(x, axis=-1, keepdims=True)
            return (x - mu) * jax.lax.rsqrt(var + EPS) * gamma + beta
        key = jax.random.key(seed)
        ks = jax.random.split(key, 8)
        B, HW, C = (8, 512, MIDC)
        s = 1.0 / np.sqrt(C)
        return {'x': jax.random.normal(ks[0], (B, HW, C), jnp.float32), 'w_qkv': jax.random.normal(ks[1], (C, 3 * C), jnp.float32) * s, 'b_qkv': jnp.zeros((3 * C,), jnp.float32), 'kln_g': jnp.ones((HEADC,), jnp.float32), 'kln_b': jnp.zeros((HEADC,), jnp.float32), 'vln_g': jnp.ones((HEADC,), jnp.float32), 'vln_b': jnp.zeros((HEADC,), jnp.float32), 'w1': jax.random.normal(ks[2], (C, C), jnp.float32) * s, 'b1': jnp.zeros((C,), jnp.float32), 'w2': jax.random.normal(ks[3], (C, C), jnp.float32) * s, 'b2': jnp.zeros((C,), jnp.float32)}
    _L0_mix_all = _L0_mix_setup()
    _L0_mix_in = {k: v for k, v in _L0_mix_all.items() if k in ('w_qkv', 'b_qkv', 'kln_g', 'kln_b', 'vln_g', 'vln_b', 'w1', 'b1', 'w2', 'b2')}
    del _L0_mix_all

    def _L0_ffn_setup():
        import jax, jax.numpy as jnp
        import numpy as np
        BN_EPS = 0.001

        def _bn(h, g, b, m, v):
            return g * (h - m) * jax.lax.rsqrt(v + BN_EPS) + b
        key = jax.random.key(seed)
        ks = jax.random.split(key, 8)
        B, F, Df = (256, 64, 256)
        E, H, D = (8, 256, 256)
        s1 = 1.0 / np.sqrt(Df)
        s2 = 1.0 / np.sqrt(H)
        return {'x': jax.random.normal(ks[0], (B, F, Df), jnp.float32), 'Wr': jax.random.normal(ks[1], (Df, E), jnp.float32) * s1, 'br': jnp.zeros((E,), jnp.float32), 'W1': jax.random.normal(ks[2], (E, Df, H), jnp.float32) * s1, 'b1': jnp.zeros((E, H), jnp.float32), 'g1': jnp.ones((E, H), jnp.float32), 'be1': jnp.zeros((E, H), jnp.float32), 'm1': jnp.zeros((E, H), jnp.float32), 'v1': jnp.ones((E, H), jnp.float32), 'W2': jax.random.normal(ks[3], (E, H, H), jnp.float32) * s2, 'b2': jnp.zeros((E, H), jnp.float32), 'g2': jnp.ones((E, H), jnp.float32), 'be2': jnp.zeros((E, H), jnp.float32), 'm2': jnp.zeros((E, H), jnp.float32), 'v2': jnp.ones((E, H), jnp.float32), 'Wo': jax.random.normal(ks[4], (E, H, D), jnp.float32) * s2, 'bo': jnp.zeros((E, D), jnp.float32)}
    _L0_ffn_all = _L0_ffn_setup()
    _L0_ffn_in = {k: v for k, v in _L0_ffn_all.items() if k in ('Wr', 'br', 'W1', 'b1', 'g1', 'be1', 'm1', 'v1', 'W2', 'b2', 'g2', 'be2', 'm2', 'v2', 'Wo', 'bo')}
    del _L0_ffn_all

    def _L1_gnn_setup():
        import jax, jax.numpy as jnp
        import numpy as np
        N_NODES = 6250
        N_EDGES = 100000
        IN_CH = 256
        OUT_CH = 32
        HEADS = 8
        NEG_SLOPE = 0.2
        key = jax.random.key(seed)
        k1, k2, k3, k4, k5, k6 = jax.random.split(key, 6)
        x = jax.random.normal(k1, (N_NODES, IN_CH), dtype=jnp.float32)
        edge_index = jax.random.randint(k2, (2, N_EDGES), 0, N_NODES, dtype=jnp.int64)
        W = jax.random.normal(k3, (IN_CH, HEADS * OUT_CH), dtype=jnp.float32) / np.sqrt(IN_CH)
        att_src = jax.random.normal(k4, (HEADS, OUT_CH), dtype=jnp.float32) / np.sqrt(OUT_CH)
        att_dst = jax.random.normal(k5, (HEADS, OUT_CH), dtype=jnp.float32) / np.sqrt(OUT_CH)
        bias = jax.random.normal(k6, (HEADS * OUT_CH,), dtype=jnp.float32) * 0.02
        return {'x': x, 'edge_index': edge_index, 'W': W, 'att_src': att_src, 'att_dst': att_dst, 'bias': bias}
    _L1_gnn_all = _L1_gnn_setup()
    _L1_gnn_in = {k: v for k, v in _L1_gnn_all.items() if k in ('W', 'att_src', 'att_dst', 'bias')}
    del _L1_gnn_all

    def _L1_mix_setup():
        import jax, jax.numpy as jnp
        import numpy as np
        HEADS = 8
        DIM_HEAD = 64
        EPS = 1e-05

        def _inst_norm(t):
            mu = jnp.mean(t, axis=-1, keepdims=True)
            var = jnp.var(t, axis=-1, keepdims=True)
            return (t - mu) / jnp.sqrt(var + EPS)
        key = jax.random.key(seed)
        k1, k2, k3, k4 = jax.random.split(key, 4)
        b, n, dim = (4, 1024, 256)
        inner = HEADS * DIM_HEAD
        x = jax.random.normal(k1, (b, n, dim), dtype=jnp.float32)
        w_qkv = jax.random.normal(k2, (dim, 3 * inner), dtype=jnp.float32) * (1.0 / DIM_HEAD)
        w_out = jax.random.normal(k3, (inner, dim), dtype=jnp.float32) * dim ** (-0.5)
        b_out = jax.random.normal(k4, (dim,), dtype=jnp.float32) * 0.01
        return {'x': x, 'w_qkv': w_qkv, 'w_out': w_out, 'b_out': b_out}
    _L1_mix_all = _L1_mix_setup()
    _L1_mix_in = {k: v for k, v in _L1_mix_all.items() if k in ('w_qkv', 'w_out', 'b_out')}
    del _L1_mix_all

    def _L1_ffn_setup():
        import jax, jax.numpy as jnp
        import numpy as np
        B, N, D = (16, 512, 256)
        NUM_EXPERTS, TOP_K, HEADS = (4, 2, 4)
        N_EDGES = 131072
        LN_EPS = 1e-05

        def _layernorm(x, g, b):
            mu = x.mean(-1, keepdims=True)
            var = ((x - mu) ** 2).mean(-1, keepdims=True)
            return (x - mu) * jax.lax.rsqrt(var + LN_EPS) * g + b

        def _forward(x, edge_index, W_gat, att_src, att_dst, b_gat, ln_gamma, ln_beta, W1, b1, W2, b2):
            Bc, Nc, Dc = x.shape
            M = Bc * Nc
            x_flat = x.reshape(M, Dc)
            h = (x_flat @ W_gat).reshape(M, HEADS, NUM_EXPERTS)
            loops = jnp.arange(M, dtype=edge_index.dtype)
            src = jnp.concatenate([edge_index[0], loops])
            dst = jnp.concatenate([edge_index[1], loops])
            a_src = (h * att_src).sum(-1)
            a_dst = (h * att_dst).sum(-1)
            e = jax.nn.leaky_relu(a_src[src] + a_dst[dst], negative_slope=0.2)
            e_max = jax.ops.segment_max(e, dst, num_segments=M)
            ee = jnp.exp(e - e_max[dst])
            denom = jax.ops.segment_sum(ee, dst, num_segments=M)
            alpha = ee / (denom[dst] + 1e-16)
            msg = h[src] * alpha[:, :, None]
            agg = jax.ops.segment_sum(msg, dst, num_segments=M).reshape(M, HEADS * NUM_EXPERTS) + b_gat
            scores = _layernorm(agg, ln_gamma, ln_beta).reshape(M, HEADS, NUM_EXPERTS).mean(1)
            scores = scores.reshape(Bc, Nc, NUM_EXPERTS)
            topk_s, topk_i = jax.lax.top_k(scores, TOP_K)
            w = jax.nn.softmax(topk_s, axis=-1)
            out = jnp.zeros_like(x)
            for ei in range(NUM_EXPERTS):
                g = jnp.where(topk_i == ei, w, 0.0).sum(-1)
                hh = jax.nn.gelu(x @ W1[ei] + b1[ei], approximate=False)
                out = out + g[..., None] * (hh @ W2[ei] + b2[ei])
            return out
        key = jax.random.key(seed)
        ks = jax.random.split(key, 8)
        s = 0.05
        return {'x': jax.random.normal(ks[0], (B, N, D), jnp.float32), 'W_gat': jax.random.normal(ks[1], (D, HEADS * NUM_EXPERTS), jnp.float32) * s, 'att_src': jax.random.normal(ks[2], (HEADS, NUM_EXPERTS), jnp.float32) * s, 'att_dst': jax.random.normal(ks[3], (HEADS, NUM_EXPERTS), jnp.float32) * s, 'b_gat': jnp.zeros((HEADS * NUM_EXPERTS,), jnp.float32), 'ln_gamma': jnp.ones((HEADS * NUM_EXPERTS,), jnp.float32), 'ln_beta': jnp.zeros((HEADS * NUM_EXPERTS,), jnp.float32), 'W1': jax.random.normal(ks[4], (NUM_EXPERTS, D, 2 * D), jnp.float32) * s, 'b1': jnp.zeros((NUM_EXPERTS, 2 * D), jnp.float32), 'W2': jax.random.normal(ks[5], (NUM_EXPERTS, 2 * D, D), jnp.float32) * s, 'b2': jnp.zeros((NUM_EXPERTS, D), jnp.float32), 'edge_index': jax.random.randint(ks[6], (2, N_EDGES), 0, B * N, jnp.int32)}
    _L1_ffn_all = _L1_ffn_setup()
    _L1_ffn_in = {k: v for k, v in _L1_ffn_all.items() if k in ('W_gat', 'att_src', 'att_dst', 'b_gat', 'ln_gamma', 'ln_beta', 'W1', 'b1', 'W2', 'b2', 'edge_index')}
    del _L1_ffn_all
    return {'x': x, 'src': src, 'dst': dst, 'L0_gnn_W_gcn': _L0_gnn_in['W_gcn'], 'L0_gnn_b_gcn': _L0_gnn_in['b_gcn'], 'L0_gnn_W_out': _L0_gnn_in['W_out'], 'L0_gnn_b_out': _L0_gnn_in['b_out'], 'L0_mix_w_qkv': _L0_mix_in['w_qkv'], 'L0_mix_b_qkv': _L0_mix_in['b_qkv'], 'L0_mix_kln_g': _L0_mix_in['kln_g'], 'L0_mix_kln_b': _L0_mix_in['kln_b'], 'L0_mix_vln_g': _L0_mix_in['vln_g'], 'L0_mix_vln_b': _L0_mix_in['vln_b'], 'L0_mix_w1': _L0_mix_in['w1'], 'L0_mix_b1': _L0_mix_in['b1'], 'L0_mix_w2': _L0_mix_in['w2'], 'L0_mix_b2': _L0_mix_in['b2'], 'L0_ffn_Wr': _L0_ffn_in['Wr'], 'L0_ffn_br': _L0_ffn_in['br'], 'L0_ffn_W1': _L0_ffn_in['W1'], 'L0_ffn_b1': _L0_ffn_in['b1'], 'L0_ffn_g1': _L0_ffn_in['g1'], 'L0_ffn_be1': _L0_ffn_in['be1'], 'L0_ffn_m1': _L0_ffn_in['m1'], 'L0_ffn_v1': _L0_ffn_in['v1'], 'L0_ffn_W2': _L0_ffn_in['W2'], 'L0_ffn_b2': _L0_ffn_in['b2'], 'L0_ffn_g2': _L0_ffn_in['g2'], 'L0_ffn_be2': _L0_ffn_in['be2'], 'L0_ffn_m2': _L0_ffn_in['m2'], 'L0_ffn_v2': _L0_ffn_in['v2'], 'L0_ffn_Wo': _L0_ffn_in['Wo'], 'L0_ffn_bo': _L0_ffn_in['bo'], 'L1_gnn_W': _L1_gnn_in['W'], 'L1_gnn_att_src': _L1_gnn_in['att_src'], 'L1_gnn_att_dst': _L1_gnn_in['att_dst'], 'L1_gnn_bias': _L1_gnn_in['bias'], 'L1_mix_w_qkv': _L1_mix_in['w_qkv'], 'L1_mix_w_out': _L1_mix_in['w_out'], 'L1_mix_b_out': _L1_mix_in['b_out'], 'L1_ffn_W_gat': _L1_ffn_in['W_gat'], 'L1_ffn_att_src': _L1_ffn_in['att_src'], 'L1_ffn_att_dst': _L1_ffn_in['att_dst'], 'L1_ffn_b_gat': _L1_ffn_in['b_gat'], 'L1_ffn_ln_gamma': _L1_ffn_in['ln_gamma'], 'L1_ffn_ln_beta': _L1_ffn_in['ln_beta'], 'L1_ffn_W1': _L1_ffn_in['W1'], 'L1_ffn_b1': _L1_ffn_in['b1'], 'L1_ffn_W2': _L1_ffn_in['W2'], 'L1_ffn_b2': _L1_ffn_in['b2'], 'L1_ffn_edge_index': _L1_ffn_in['edge_index']}

def reference(x, src, dst, L0_gnn_W_gcn, L0_gnn_b_gcn, L0_gnn_W_out, L0_gnn_b_out, L0_mix_w_qkv, L0_mix_b_qkv, L0_mix_kln_g, L0_mix_kln_b, L0_mix_vln_g, L0_mix_vln_b, L0_mix_w1, L0_mix_b1, L0_mix_w2, L0_mix_b2, L0_ffn_Wr, L0_ffn_br, L0_ffn_W1, L0_ffn_b1, L0_ffn_g1, L0_ffn_be1, L0_ffn_m1, L0_ffn_v1, L0_ffn_W2, L0_ffn_b2, L0_ffn_g2, L0_ffn_be2, L0_ffn_m2, L0_ffn_v2, L0_ffn_Wo, L0_ffn_bo, L1_gnn_W, L1_gnn_att_src, L1_gnn_att_dst, L1_gnn_bias, L1_mix_w_qkv, L1_mix_w_out, L1_mix_b_out, L1_ffn_W_gat, L1_ffn_att_src, L1_ffn_att_dst, L1_ffn_b_gat, L1_ffn_ln_gamma, L1_ffn_ln_beta, L1_ffn_W1, L1_ffn_b1, L1_ffn_W2, L1_ffn_b2, L1_ffn_edge_index):
    import jax
    import jax.numpy as jnp

    def _L0_gnn_ref(features, src, dst, W_gcn, b_gcn, W_out, b_out):
        import jax, jax.numpy as jnp
        import numpy as np
        N_NODES = 12500
        n = features.shape[0]
        ones = jnp.ones(src.shape[0], dtype=features.dtype)
        out_deg = jax.ops.segment_sum(ones, src, num_segments=n)
        in_deg = jax.ops.segment_sum(ones, dst, num_segments=n)
        norm_src = jax.lax.rsqrt(jnp.maximum(out_deg, 1.0))[:, None]
        norm_dst = jax.lax.rsqrt(jnp.maximum(in_deg, 1.0))[:, None]
        x = features * norm_src @ W_gcn
        msg = x[src]
        agg = jax.ops.segment_sum(msg, dst, num_segments=n)
        h = agg * norm_dst + b_gcn
        h = jax.nn.relu(h)
        return h @ W_out + b_out

    def _L0_mix_ref(x, w_qkv, b_qkv, kln_g, kln_b, vln_g, vln_b, w1, b1, w2, b2):
        import jax, jax.numpy as jnp
        import numpy as np
        MIDC = 256
        HEADS = 8
        HEADC = MIDC // HEADS
        EPS = 1e-05

        def _ln(x, gamma, beta):
            mu = jnp.mean(x, axis=-1, keepdims=True)
            var = jnp.var(x, axis=-1, keepdims=True)
            return (x - mu) * jax.lax.rsqrt(var + EPS) * gamma + beta
        B, HW, C = x.shape
        bias = x
        qkv = (x @ w_qkv + b_qkv).reshape(B, HW, HEADS, 3 * HEADC)
        qkv = qkv.transpose(0, 2, 1, 3)
        q, k, v = jnp.split(qkv, 3, axis=-1)
        k = _ln(k, kln_g, kln_b)
        v = _ln(v, vln_g, vln_b)
        kv = jnp.einsum('bhnd,bhne->bhde', k, v) / HW
        out = jnp.einsum('bhnd,bhde->bhne', q, kv)
        out = out.transpose(0, 2, 1, 3).reshape(B, HW, C)
        ret = out + bias
        h = jax.nn.gelu(ret @ w1 + b1, approximate=False)
        return h @ w2 + b2 + bias

    def _L0_ffn_ref(x, Wr, br, W1, b1, g1, be1, m1, v1, W2, b2, g2, be2, m2, v2, Wo, bo):
        import jax, jax.numpy as jnp
        import numpy as np
        BN_EPS = 0.001

        def _bn(h, g, b, m, v):
            return g * (h - m) * jax.lax.rsqrt(v + BN_EPS) + b
        feat = jnp.mean(x, axis=0)
        w = jax.nn.softmax(feat @ Wr + br, axis=-1)
        h = jnp.einsum('bfd,edh->bfeh', x, W1) + b1
        h = jax.nn.relu(_bn(h, g1, be1, m1, v1))
        h = jnp.einsum('bfeh,ehk->bfek', h, W2) + b2
        h = jax.nn.relu(_bn(h, g2, be2, m2, v2))
        y = jnp.einsum('bfeh,ehd->bfed', h, Wo) + bo
        return jnp.einsum('bfed,fe->bfd', y, w)

    def _L1_gnn_ref(x, edge_index, W, att_src, att_dst, bias):
        import jax, jax.numpy as jnp
        import numpy as np
        N_NODES = 6250
        N_EDGES = 100000
        IN_CH = 256
        OUT_CH = 32
        HEADS = 8
        NEG_SLOPE = 0.2
        N = x.shape[0]
        H, C = att_src.shape
        loop = jnp.arange(N, dtype=edge_index.dtype)
        src = jnp.concatenate([edge_index[0], loop])
        dst = jnp.concatenate([edge_index[1], loop])
        h = (x @ W).reshape(N, H, C)
        a_src = jnp.einsum('nhc,hc->nh', h, att_src)
        a_dst = jnp.einsum('nhc,hc->nh', h, att_dst)
        e = a_src[src] + a_dst[dst]
        e = jnp.where(e > 0, e, NEG_SLOPE * e)
        m = jax.ops.segment_max(e, dst, num_segments=N)
        ex = jnp.exp(e - m[dst])
        denom = jax.ops.segment_sum(ex, dst, num_segments=N)
        alpha = ex / (denom[dst] + 1e-16)
        msg = h[src] * alpha[:, :, None]
        out = jax.ops.segment_sum(msg, dst, num_segments=N)
        return out.reshape(N, H * C) + bias

    def _L1_mix_ref(x, w_qkv, w_out, b_out):
        import jax, jax.numpy as jnp
        import numpy as np
        HEADS = 8
        DIM_HEAD = 64
        EPS = 1e-05

        def _inst_norm(t):
            mu = jnp.mean(t, axis=-1, keepdims=True)
            var = jnp.var(t, axis=-1, keepdims=True)
            return (t - mu) / jnp.sqrt(var + EPS)
        b, n, dim = x.shape
        qkv = x @ w_qkv
        q, k, v = jnp.split(qkv, 3, axis=-1)
        to_heads = lambda t: t.reshape(b, n, HEADS, DIM_HEAD).transpose(0, 2, 1, 3)
        q, k, v = (to_heads(q), to_heads(k), to_heads(v))
        k = _inst_norm(k)
        v = _inst_norm(v)
        dots = jnp.einsum('bhnd,bhne->bhde', k, v)
        out = jnp.einsum('bhnd,bhde->bhne', q, dots) * (1.0 / n)
        out = out.transpose(0, 2, 1, 3).reshape(b, n, HEADS * DIM_HEAD)
        return out @ w_out + b_out

    def _L1_ffn_ref(x, W_gat, att_src, att_dst, b_gat, ln_gamma, ln_beta, W1, b1, W2, b2, edge_index):
        import jax, jax.numpy as jnp
        import numpy as np
        B, N, D = (16, 512, 256)
        NUM_EXPERTS, TOP_K, HEADS = (4, 2, 4)
        N_EDGES = 131072
        LN_EPS = 1e-05

        def _layernorm(x, g, b):
            mu = x.mean(-1, keepdims=True)
            var = ((x - mu) ** 2).mean(-1, keepdims=True)
            return (x - mu) * jax.lax.rsqrt(var + LN_EPS) * g + b

        def _forward(x, edge_index, W_gat, att_src, att_dst, b_gat, ln_gamma, ln_beta, W1, b1, W2, b2):
            Bc, Nc, Dc = x.shape
            M = Bc * Nc
            x_flat = x.reshape(M, Dc)
            h = (x_flat @ W_gat).reshape(M, HEADS, NUM_EXPERTS)
            loops = jnp.arange(M, dtype=edge_index.dtype)
            src = jnp.concatenate([edge_index[0], loops])
            dst = jnp.concatenate([edge_index[1], loops])
            a_src = (h * att_src).sum(-1)
            a_dst = (h * att_dst).sum(-1)
            e = jax.nn.leaky_relu(a_src[src] + a_dst[dst], negative_slope=0.2)
            e_max = jax.ops.segment_max(e, dst, num_segments=M)
            ee = jnp.exp(e - e_max[dst])
            denom = jax.ops.segment_sum(ee, dst, num_segments=M)
            alpha = ee / (denom[dst] + 1e-16)
            msg = h[src] * alpha[:, :, None]
            agg = jax.ops.segment_sum(msg, dst, num_segments=M).reshape(M, HEADS * NUM_EXPERTS) + b_gat
            scores = _layernorm(agg, ln_gamma, ln_beta).reshape(M, HEADS, NUM_EXPERTS).mean(1)
            scores = scores.reshape(Bc, Nc, NUM_EXPERTS)
            topk_s, topk_i = jax.lax.top_k(scores, TOP_K)
            w = jax.nn.softmax(topk_s, axis=-1)
            out = jnp.zeros_like(x)
            for ei in range(NUM_EXPERTS):
                g = jnp.where(topk_i == ei, w, 0.0).sum(-1)
                hh = jax.nn.gelu(x @ W1[ei] + b1[ei], approximate=False)
                out = out + g[..., None] * (hh @ W2[ei] + b2[ei])
            return out
        return _forward(x, edge_index, W_gat, att_src, att_dst, b_gat, ln_gamma, ln_beta, W1, b1, W2, b2)
    edge_index = jnp.stack([src, dst])
    xn = _layernorm(x, axis=-1)
    x = x + _L0_gnn_ref(xn, src, dst, L0_gnn_W_gcn, L0_gnn_b_gcn, L0_gnn_W_out, L0_gnn_b_out) + _L0_mix_ref(xn[None], L0_mix_w_qkv, L0_mix_b_qkv, L0_mix_kln_g, L0_mix_kln_b, L0_mix_vln_g, L0_mix_vln_b, L0_mix_w1, L0_mix_b1, L0_mix_w2, L0_mix_b2)[0]
    x = x + _L0_ffn_ref(_layernorm(x, axis=-1)[None], L0_ffn_Wr, L0_ffn_br, L0_ffn_W1, L0_ffn_b1, L0_ffn_g1, L0_ffn_be1, L0_ffn_m1, L0_ffn_v1, L0_ffn_W2, L0_ffn_b2, L0_ffn_g2, L0_ffn_be2, L0_ffn_m2, L0_ffn_v2, L0_ffn_Wo, L0_ffn_bo)[0]
    xn = _layernorm(x, axis=-1)
    x = x + _L1_gnn_ref(xn, edge_index, L1_gnn_W, L1_gnn_att_src, L1_gnn_att_dst, L1_gnn_bias) + _L1_mix_ref(xn[None], L1_mix_w_qkv, L1_mix_w_out, L1_mix_b_out)[0]
    x = x + _L1_ffn_ref(_layernorm(x, axis=-1)[None], L1_ffn_W_gat, L1_ffn_att_src, L1_ffn_att_dst, L1_ffn_b_gat, L1_ffn_ln_gamma, L1_ffn_ln_beta, L1_ffn_W1, L1_ffn_b1, L1_ffn_W2, L1_ffn_b2, L1_ffn_edge_index)[0]
    return x

_drawn_inputs = setup_inputs


def setup_inputs(seed=0):
    import zlib

    import numpy as np

    out = dict(_drawn_inputs(seed))
    spreads = {'L0_gnn_b_gcn': (0.0, 0.1),
     'L0_gnn_b_out': (0.0, 0.1),
     'L0_mix_b_qkv': (0.0, 0.1),
     'L0_mix_kln_g': (1.0, 0.6),
     'L0_mix_kln_b': (0.0, 0.412),
     'L0_mix_vln_g': (1.0, 0.545),
     'L0_mix_vln_b': (0.0, 0.365),
     'L0_mix_b1': (0.0, 0.1),
     'L0_mix_b2': (0.0, 0.1),
     'L0_ffn_br': (0.0, 0.323),
     'L0_ffn_b1': (0.0, 0.518),
     'L0_ffn_g1': (1.0, 0.595),
     'L0_ffn_be1': (0.0, 0.559),
     'L0_ffn_m1': (0.0, 0.443),
     'L0_ffn_v1': (1.0, 0.6),
     'L0_ffn_b2': (0.0, 0.379),
     'L0_ffn_g2': (1.0, 0.2),
     'L0_ffn_be2': (0.0, 0.426),
     'L0_ffn_m2': (0.0, 0.398),
     'L0_ffn_v2': (1.0, 0.6),
     'L0_ffn_bo': (0.0, 0.274),
     'L1_ffn_b_gat': (0.0, 0.1),
     'L1_ffn_ln_gamma': (1.0, 0.565),
     'L1_ffn_ln_beta': (0.0, 0.323),
     'L1_ffn_b1': (0.0, 0.287),
     'L1_ffn_b2': (0.0, 0.1)}
    factors = {'L1_gnn_bias': 3.63,
     'L1_mix_b_out': 5.051,
     'L1_ffn_att_src': 3.651,
     'L1_ffn_att_dst': 21.677}
    for name, (base, spread) in spreads.items():
        noise = np.random.default_rng([zlib.crc32(name.encode()), seed]).standard_normal(out[name].shape)
        drawn = base * np.exp(spread * noise) if base else spread * noise
        out[name] = jnp.asarray(drawn.astype(out[name].dtype))
    for name, factor in factors.items():
        out[name] = (out[name] * factor).astype(out[name].dtype)
    return out
```

```python
from contextlib import ExitStack

import concourse.bass as bass
from concourse import mybir

F32 = mybir.dt.float32
BF16 = mybir.dt.bfloat16
I32 = mybir.dt.int32
U32 = mybir.dt.uint32
ALU = mybir.AluOpType
ACT = mybir.ActivationFunctionType
AXX = mybir.AxisListType.X
ENG = mybir.EngineType

P = 128
N = 6250
D = 256
C = D // P
W = -(-N // P)
NP = W * P
TPI = 7
ITER = W // TPI
TOK = TPI * P
HALF = TOK // 2
assert W % TPI == 0 and HALF <= 512

HEADS = 8
HC0 = 32
HC1 = 64
GCN = 64
GH, GC = 8, 32
GROW = GH * GC + GH
E0, E1 = 8, 4
HID1 = 512
FH, FC = 4, 4
FROW = FH * FC + FH
LN_EPS = 1e-5
BN_EPS = 1e-3

GE = 50000 * 2 + N
GB = 832
FE = 131072
FB = FE // P
PAD_NODE = 8192
GROUP = 4
NBUF = 4
TURN = NBUF * GROUP
GROUP8 = 8
GSLOTS = -(-(GB + W - 1) // TURN) * TURN
FSLOTS = -(-(FB + W - 1) // TURN) * TURN
assert GB * P >= GE


class Phase:

    def __init__(self, nc, tag):
        self.nc, self.tag, self.ctx, self.sems = nc, tag, ExitStack(), []

    def __enter__(self):
        return self

    def __exit__(self, *a):
        if self.sems:
            self.nc.clear_and_free_semaphores(self.sems)
            self.nc.all_engine_barrier()
        self.ctx.close()

    def sb(self, name, shape, dt=F32):
        return self.ctx.enter_context(self.nc.sbuf_tensor(f"{self.tag}_{name}", shape, dt))

    def ps(self, name, shape, dt=F32):
        return self.ctx.enter_context(self.nc.psum_tensor(f"{self.tag}_{name}", shape, dt))

    def sem(self, name):
        self.sems.append(self.nc.alloc_semaphore(f"{self.tag}_{name}"))
        return self.sems[-1]


class Steps:

    def __init__(self, eng, sem, start=0):
        self.eng, self.sem, self.n = eng, sem, start

    def then(self, ins):
        ins.then_inc(self.sem, 1)
        self.n += 1
        self.eng.wait_ge(self.sem, self.n)


def rows(ap):
    return ap.rearrange("(c p) n -> p c n", p=P)


def spread(ap, n=P):
    return ap.partition_broadcast(n)



def constants(nc, R):
    with Phase(nc, "cst") as f:
        made = f.sem("made")
        row_i = f.sb("row_i", [P, P], I32)
        with nc.Block() as block:
            @block.gpsimd
            def _(g):
                st = Steps(g, made)
                st.then(g.memset(R.ident[:, :], 0.0))
                st.then(g.affine_select(out=R.ident[:, :], in_=R.ident[:, :], compare_op=ALU.not_equal, fill=1.0,
                                        base=0, pattern=[[-1, P]], channel_multiplier=1))
                st.then(g.iota(row_i[:, :], pattern=[[1, P]], base=0, channel_multiplier=0))
                st.then(g.tensor_copy(R.iota[:, :], row_i[:, :]))
                st.then(g.memset(R.ones[:, :], 1.0))
                st.then(g.memset(R.mask[:, :], 1.0))
                st.then(g.affine_select(out=R.mask[:, W - 1:W], in_=R.mask[:, W - 1:W], compare_op=ALU.is_ge, fill=0.0,
                                        base=N - (W - 1) * P - 1, pattern=[[0, 1]], channel_multiplier=-1))



def place_edges(nc, R, A):
    with Phase(nc, "pos") as f:
        wdst = f.sb("wdst", [P, FB], I32)
        win = f.sb("win", [P, FB])
        hit = f.sb("hit", [P, FB])
        junk = f.sb("junk", [P, FB])
        rank = f.sb("rank", [P, FB])
        one = f.sb("one", [P, FB])
        pos = f.sb("pos", [P, FB])
        tot = f.sb("tot", [P, W + 1])
        tri = f.sb("tri", [P, P])
        start = f.sb("start", [P, W + 2])
        base = f.sb("base", [P, W + 1])
        scanin = f.sb("scanin", [P, W + 2])
        below = f.ps("below", [P, 512])
        total = f.ps("total", [P, 512])
        loaded, tri_made, step, counted, summed = (f.sem(n) for n in ("loaded", "tri", "step", "counted", "summed"))
        with nc.Block() as block:
            @block.sync
            def _(s):
                s.dma_start(R.frec[:, :, :], A.ffn_edges).then_inc(loaded, 16)

            @block.gpsimd
            def _(g):
                g.memset(tri[:, :], 1.0).then_inc(tri_made, 1)
                g.wait_ge(tri_made, 1)
                g.affine_select(out=tri[:, :], in_=tri[:, :], compare_op=ALU.is_gt, fill=0.0,
                                base=0, pattern=[[1, P]], channel_multiplier=-1).then_inc(tri_made, 1)

            @block.tensor
            def _(t):
                t.wait_ge(tri_made, 2)
                t.wait_ge(counted, 1)
                t.matmul(below[:, 0:W + 1], tri[:, :], tot[:, :], start=True, stop=True)
                t.matmul(total[:, 0:W + 1], R.ones[:, :], tot[:, :], start=True, stop=True).then_inc(summed, 1)

            @block.vector
            def _(v):
                st = Steps(v, step)
                v.wait_ge(loaded, 16)
                st.then(v.tensor_scalar(wdst[:, :], R.frec[:, :, 1], 7, None, ALU.arith_shift_right))
                st.then(v.tensor_scalar(win[:, :], wdst[:, :], float(W), None, ALU.min))
                st.then(v.memset(one[:, :], 1.0))
                for w in range(W + 1):
                    ins = v.tensor_scalar(junk[:, :], win[:, :], float(w), None, ALU.is_equal, ALU.add,
                                          accum_out=tot[:, w:w + 1])
                    st.then(ins)
                v.sem_inc(counted, 1)
                v.wait_ge(summed, 1)
                st.then(v.memset(scanin[:, :], 0.0))
                st.then(v.tensor_copy(scanin[:, 1:W + 2], total[:, 0:W + 1]))
                st.then(v.tensor_tensor_scan(start[:, :], one[:, 0:W + 2], scanin[:, :], 0.0, ALU.mult, ALU.add))
                st.then(v.tensor_copy(R.fstart[:, :], start[:, 0:W]))
                st.then(v.tensor_tensor(base[:, :], start[:, 0:W + 1], below[:, 0:W + 1], ALU.add))
                for w in range(W + 1):
                    st.then(v.tensor_scalar(hit[:, :], win[:, :], float(w), None, ALU.is_equal))
                    st.then(v.tensor_tensor_scan(rank[:, :], one[:, :], hit[:, :], base[:, w:w + 1], ALU.mult, ALU.add))
                    st.then(v.copy_predicated(pos[:, :], hit[:, :].bitcast(I32), rank[:, :]))
                st.then(v.tensor_scalar(R.fpos[:, :], pos[:, :], 1.0, None, ALU.subtract))



def degrees(nc, R, A):
    BAT = 16
    TURNS = GB // (2 * BAT)
    with Phase(nc, "deg") as f:
        si = f.sb("si", [P, GB], I32)
        di = f.sb("di", [P, GB], I32)
        part = f.sb("part", [P, GB], I32)
        lo = f.sb("lo", [P, GB])
        hi = f.sb("hi", [P, GB])
        dstf = f.sb("dstf", [P, GB])
        junk = f.sb("junk", [P, GB])
        cnt = f.sb("cnt", [P, W])
        ohlo = f.sb("ohlo", [P, 2, BAT, P], BF16)
        ohhi = f.sb("ohhi", [P, 2, BAT, W], BF16)
        deg = f.ps("deg", [P, 512])
        total = f.ps("total", [P, 512])
        zero = f.sb("zero", [P, P], BF16)
        loaded, step, hot, used, zeroed, counted, summed, rooted = (
            f.sem(n) for n in ("loaded", "step", "hot", "used", "zeroed", "counted", "summed", "rooted"))
        std = f.sb("std", [P, W])
        with nc.Block() as block:
            @block.sync
            def _(s):
                s.dma_start(si[:, :], A.gsrc_t).then_inc(loaded, 16)
                s.dma_start(di[:, :], A.gdst_t).then_inc(loaded, 16)

            @block.vector
            def _(v):
                st = Steps(v, step)
                v.memset(zero[:, :], 0.0).then_inc(zeroed, 1)
                v.wait_ge(loaded, 32)
                st.then(v.tensor_scalar(part[:, :], si[:, :], P - 1, None, ALU.bitwise_and))
                st.then(v.tensor_copy(lo[:, :], part[:, :]))
                st.then(v.tensor_scalar(part[:, :], si[:, :], 7, None, ALU.arith_shift_right))
                st.then(v.tensor_copy(hi[:, :], part[:, :]))
                st.then(v.tensor_copy(dstf[:, :], di[:, :]))
                with v.Fori(0, TURNS) as i:
                    for g in range(2):
                        v.wait_ge(used, 2 * i)
                        col = (2 * i + g) * BAT
                        v.tensor_tensor(ohlo[:, g], R.iota[:, :].unsqueeze(1).to_broadcast([P, BAT, P]),
                                        lo[:, bass.ds(col, BAT)].unsqueeze(2).to_broadcast([P, BAT, P]),
                                        ALU.is_equal).then_inc(hot, 1)
                        v.tensor_tensor(ohhi[:, g], R.iota[:, 0:W].unsqueeze(1).to_broadcast([P, BAT, W]),
                                        hi[:, bass.ds(col, BAT)].unsqueeze(2).to_broadcast([P, BAT, W]),
                                        ALU.is_equal).then_inc(hot, 1)
                for w in range(W):
                    st.then(v.tensor_scalar(junk[:, :], dstf[:, :], float(P * w), None, ALU.is_lt, ALU.add,
                                            accum_out=cnt[:, w:w + 1]))
                v.sem_inc(counted, 1)
                v.wait_ge(summed, 1)
                st.then(v.tensor_copy(R.gstart[:, :], total[:, 0:W]))
                st.then(v.tensor_scalar(std[:, :], deg[:, 0:W], 1.0, None, ALU.max))
                v.sem_inc(counted, 1)
                v.wait_ge(rooted, 1)
                v.reciprocal(R.nsrc[:, :], std[:, :])

            @block.scalar
            def _(a):
                a.wait_ge(counted, 2)
                a.activation(std[:, :], std[:, :], ACT.Sqrt).then_inc(rooted, 1)

            @block.tensor
            def _(t):
                t.wait_ge(zeroed, 1)
                t.matmul(deg[:, 0:W], zero[:, :], zero[:, 0:W], start=True, stop=False, skip_group_check=True)
                with t.Fori(0, TURNS) as i:
                    for g in range(2):
                        t.wait_ge(hot, 4 * i + 2 * g + 2)
                        for b in range(BAT):
                            mm = t.matmul(deg[:, 0:W], ohlo[:, g, b, :], ohhi[:, g, b, :], start=False, stop=False,
                                          skip_group_check=True)
                        mm.then_inc(used, 1)
                t.wait_ge(counted, 1)
                t.matmul(total[:, 0:W], R.ones[:, :], cnt[:, :], start=True, stop=True).then_inc(summed, 1)



def slot_tables(nc, R, tag, start, rec, nblocks, nslots, src_ix, dst_rel, wtab, wnext):
    J = -(-nslots // P)
    with Phase(nc, tag) as f:
        si = f.sb("si", [P, W], I32)
        sf = f.sb("sf", [P, W])
        iw = f.sb("iw", [P, W], I32)
        slot_i = f.sb("slot_i", [P, J], I32)
        slot = f.sb("slot", [P, J])
        cmp = f.sb("cmp", [P, J, W - 1])
        win = f.sb("win", [P, J])
        blk = f.sb("blk", [P, J])
        off = f.sb("off", [P, J])
        blk_i = f.sb("blk_i", [P, J], U32)
        win_i = f.sb("win_i", [P, J], I32)
        edge = f.sb("edge", [P, J, P, 2], I32)
        srcf = f.sb("srcf", [P, J, P])
        dstf = f.sb("dstf", [P, J, P])
        pt = f.ps("pt", [P, 4, 512])
        made, step, tabbed, gathered, split, turned, put, wout, win_done = (
            f.sem(n) for n in ("made", "step", "tabbed", "gathered", "split", "turned", "put", "wout", "win_done"))
        gath = [f.sem(f"gath{j}") for j in range(J)]
        with nc.Block() as block:
            @block.gpsimd
            def _(g):
                g.iota(slot_i[:, :], pattern=[[P, J]], base=0, channel_multiplier=1).then_inc(made, 1)
                g.iota(iw[:, :], pattern=[[1, W]], base=0, channel_multiplier=0).then_inc(made, 1)
                g.wait_ge(tabbed, 1)
                for j in range(J):
                    g.indirect_dma_start(edge[:, j].rearrange("p e k -> p (e k)"), None, rec,
                                         bass.IndirectOffsetOnAxis(blk_i[:, j:j + 1], 0)).then_inc(gath[j], 16)

            @block.vector
            def _(v):
                st = Steps(v, step)
                v.wait_ge(made, 2)
                st.then(v.tensor_copy(slot[:, :], slot_i[:, :]))
                st.then(v.tensor_copy(si[:, :], start[:, :]))
                st.then(v.tensor_scalar(si[:, :], si[:, :], 7, None, ALU.arith_shift_right))
                st.then(v.tensor_tensor(sf[:, :], si[:, :], iw[:, :], ALU.add))
                st.then(v.tensor_tensor(cmp[:, :, :], sf[:, 1:W].unsqueeze(1).to_broadcast([P, J, W - 1]),
                                        slot[:, :].unsqueeze(2).to_broadcast([P, J, W - 1]), ALU.is_le))
                st.then(v.tensor_reduce(win[:, :], cmp[:, :, :], AXX, ALU.add))
                st.then(v.tensor_tensor(blk[:, :], slot[:, :], win[:, :], ALU.subtract))
                st.then(v.tensor_scalar(blk_i[:, :], blk[:, :], float(nblocks - 1), None, ALU.min))
                st.then(v.tensor_copy(win_i[:, :], win[:, :]))
                st.then(v.tensor_scalar(off[:, :], blk[:, :], float(nblocks), -float(1 << 22), ALU.is_ge, ALU.mult))
                st.then(v.scalar_tensor_tensor(off[:, :], win[:, :], float(P), off[:, :], ALU.mult, ALU.add))
                v.sem_inc(tabbed, 1)
                for j in range(J):
                    v.wait_ge(gath[j], 16)
                    v.tensor_scalar(srcf[:, j], edge[:, j, :, 0], float(N - 1), None, ALU.min).then_inc(split, 1)
                    v.tensor_scalar(dstf[:, j], edge[:, j, :, 1], off[:, j:j + 1], None,
                                    ALU.subtract).then_inc(split, 1)
                for j in range(J):
                    v.wait_ge(turned, j + 1)
                    v.tensor_copy(src_ix[:, j * P:(j + 1) * P], pt[:, 2 * (j % 2), 0:P]).then_inc(put, 1)
                    v.tensor_copy(dst_rel[:, j * P:(j + 1) * P], pt[:, 2 * (j % 2) + 1, 0:P]).then_inc(put, 1)

            @block.tensor
            def _(t):
                for j in range(J):
                    t.wait_ge(split, 2 * (j + 1))
                    if j >= 2:
                        t.wait_ge(put, 2 * (j - 1))
                    t.transpose(pt[:, 2 * (j % 2), 0:P], srcf[:, j], R.ident[:, :])
                    t.transpose(pt[:, 2 * (j % 2) + 1, 0:P], dstf[:, j], R.ident[:, :]).then_inc(turned, 1)

            @block.sync
            def _(s):
                s.wait_ge(tabbed, 1)
                with nc.allow_non_contiguous_dma(reason="one number per slot, once"):
                    s.dma_start(R.wdram[0:J * P].rearrange("(j p) -> p j", p=P), win_i[:, :]).then_inc(wout, 16)
                s.wait_ge(wout, 16)
                s.dma_start(wtab[0:1, :], R.wdram[0:J * P].unsqueeze(0)).then_inc(wout, 16)
                s.dma_start(wnext[0:1, 0:J * P - 2 * GROUP], R.wdram[2 * GROUP:J * P].unsqueeze(0)).then_inc(wout, 16)
                s.wait_ge(wout, 48)



class Norm:

    def __init__(self, f, R):
        self.R = R
        self.stats = f.sb("stats", [P, TPI, 6])
        self.mv = f.sb("mv", [P, TPI, 2])
        self.var = f.sb("var", [P, TPI])
        self.std = f.sb("std", [P, TPI])
        self.rstd = f.sb("rstd", [P, TPI])
        self.xn = f.sb("xn", [P, TPI, D])
        self.xt = f.sb("xt", [P, TPI, C, P])
        self.pt = f.ps("pt", [P, 2, 512])
        self.s_stat, self.s_mv, self.s_var, self.s_std, self.s_rstd = (
            f.sem(n) for n in ("stat", "mv", "var", "std", "rstd"))
        self.s_seen = f.sem("seen")
        self.s_xn, self.s_tp, self.s_xt, self.s_xr = (f.sem(n) for n in ("xn", "tp", "xt", "xr"))

    def vector(self, v, i):
        R = self.R
        for j in range(TPI):
            v.bn_stats(self.stats[:, j], R.X[:, bass.ds(TPI * i + j, 1), :].rearrange("p a d -> p (a d)")).then_inc(self.s_stat, 1)
        v.wait_ge(self.s_stat, TPI * i + TPI)
        v.sem_inc(self.s_seen, 1)
        for j in range(TPI):
            v.bn_aggr(self.mv[:, j], self.stats[:, j]).then_inc(self.s_mv, 1)
        v.wait_ge(self.s_mv, TPI * i + TPI)
        v.tensor_scalar(self.var[:, :], self.mv[:, :, 1], LN_EPS, None, ALU.add).then_inc(self.s_var, 1)
        v.wait_ge(self.s_std, i + 1)
        v.reciprocal(self.rstd[:, :], self.std[:, :]).then_inc(self.s_rstd, 1)
        v.wait_ge(self.s_rstd, i + 1)
        v.wait_ge(self.s_tp, TPI * i)
        for j in range(TPI):
            v.tensor_scalar(self.xn[:, j], R.X[:, bass.ds(TPI * i + j, 1), :].rearrange("p a d -> p (a d)"),
                            self.mv[:, j, 0:1], self.rstd[:, j:j + 1], ALU.subtract, ALU.mult).then_inc(self.s_xn, 1)

    def scalar_root(self, a, i):
        a.wait_ge(self.s_var, i + 1)
        a.activation(self.std[:, :], self.var[:, :], ACT.Sqrt).then_inc(self.s_std, 1)

    def scalar_copy(self, a, i, j):
        a.wait_ge(self.s_tp, TPI * i + j + 1)
        src = self.pt[:, j % 2, 0:C * P].rearrange("p (c t) -> p c t", c=C)
        a.activation(self.xt[:, j], src, ACT.Copy).then_inc(self.s_xt, 1)
        a.activation(self.R.XT[:, :, bass.ds((TPI * i + j) * P, P)], src, ACT.Copy).then_inc(self.s_xr, 1)

    def tensor(self, t, i, j):
        t.wait_ge(self.s_xn, TPI * i + j + 1)
        t.wait_ge(self.s_xr, TPI * i + (j - 1 if j >= 2 else 0))
        for c in range(C):
            mm = t.transpose(self.pt[:, j % 2, c * P:(c + 1) * P], self.xn[:, j, c * P:(c + 1) * P], self.R.ident[:, :])
        mm.then_inc(self.s_tp, 1)


def kv_phase(nc, R, A, L):
    first = L == 0
    hd = HC0 if first else HC1
    G = 2 * HEADS
    KV = G * hd
    NB_KV = KV // 512
    EXT = GCN if first else GH * GC + 2 * GH
    TAB = GCN if first else GROW
    PAIRS = KV // 2 // P
    wkv_d, ext_d, tab_d = (A.m0_kv, A.gcn_w, R.tab0) if first else (A.m1_kv, A.gat_w, R.tab1)
    with Phase(nc, f"kv{L}") as f:
        nm = Norm(f, R)
        wkv = f.sb("wkv", [P, C, KV])
        wext = f.sb("wext", [P, C, EXT])
        gsum = f.sb("gsum", [P, C, G])
        kc = f.sb("kc", [P, TPI, KV])
        sq = f.sb("sq", [P, KV])
        ssum = f.sb("ssum", [P, TPI, G])
        sstd = f.sb("sstd", [P, TPI, G])
        srs = f.sb("srs", [P, TPI, G])
        ext = f.sb("ext", [P, TPI, EXT])
        tabt = f.sb("tabt", [P, TPI, TAB])
        zero = f.sb("zero", [P, 512], BF16)
        if first:
            bias = f.sb("bias", [P, KV])
            bsum = f.sb("bsum", [P, G])
            gam = f.sb("gam", [P, KV])
            bet = f.sb("bet", [P, KV])
        else:
            att = f.sb("att", [P, 2, GH * GC])
            wa = f.sb("wa", [P, GH * GC])
        pkv = f.ps("pkv", [P, 4 // NB_KV if NB_KV > 1 else 2, NB_KV, 512])
        pext = f.ps("pext", [P, 512])
        pacc = f.ps("pacc", [P, 512])
        s_w, s_st, s_z, s_ready, s_x = (f.sem(n) for n in ("w", "st", "z", "ready", "x"))
        s_kvp, s_kc, s_sq, s_red, s_ve, s_sd, s_r2, s_rm = (
            f.sem(n) for n in ("kvp", "kc", "sq", "red", "ve", "sd", "r2", "rm"))
        s_k1, s_k2, s_k3, s_kv, s_ep, s_ec, s_tab, s_tab_d, s_out, s_acc, s_gm = (
            f.sem(n) for n in ("k1", "k2", "k3", "kv", "ep", "ec", "tab", "tabd", "out", "acc", "gm"))
        s_xa = f.sem("xa")
        s_kdone = s_k3 if first else s_k1
        loads = 6 if first else 4
        with nc.Block() as block:
            @block.sync
            def _(s):
                s.dma_start(wkv[:, :, :], rows(wkv_d)).then_inc(s_w, 16)
                s.dma_start(wext[:, :, 0:ext_d.shape[1]], rows(ext_d)).then_inc(s_w, 16)
                if first:
                    s.dma_start(bias[:, :], spread(A.m0_bkv)).then_inc(s_w, 16)
                    for tile, row in ((gam, A.m0_gam), (bet, A.m0_bet)):
                        for k in range(2):
                            s.dma_start(tile[:, k * KV // 2:k * KV // 2 + hd], spread(row[k])).then_inc(s_w, 16)
                    s.wait_ge(s_z, 2)
                    full = W - 1
                    s.dma_start(R.X[:, 0:full, :], A.x[0:full * P, :].rearrange("(t p) d -> p t d", p=P))\
                        .then_inc(s_x, 16)
                    s.dma_start(R.X[0:N - full * P, full, :], A.x[full * P:N, :]).then_inc(s_x, 16)
                else:
                    for k, row in enumerate((A.gat_src, A.gat_dst)):
                        s.dma_start(att[:, k, :], spread(row)).then_inc(s_w, 16)
                with s.Fori(0, ITER) as i:
                    s.wait_ge(s_tab, i + 1)
                    s.dma_start(tab_d[bass.ds(i * TOK, TOK), :].rearrange("(t p) d -> p t d", p=P), tabt[:, :, :])\
                        .then_inc(s_out, 16)
                s.wait_ge(s_out, 16 * ITER)

            if first:
                @block.gpsimd
                def _(g):
                    with g.Fori(0, ITER) as i:
                        for j in range(TPI):
                            g.wait_ge(nm.s_xn, TPI * i + j + 1)
                            xj = R.X[:, bass.ds(TPI * i + j, 1), :].rearrange("p a d -> p (a d)")
                            g.tensor_tensor(xj, xj, nm.xn[:, j], ALU.add).then_inc(s_xa, 1)

            @block.vector
            def _(v):
                st = Steps(v, s_st)
                v.memset(zero[:, :], 0.0).then_inc(s_z, 1)
                if first:
                    v.memset(R.X[:, W - 1, :], 0.0).then_inc(s_z, 1)
                v.wait_ge(s_w, 16 * (7 if first else 4))
                if first:
                    for tile in (gam, bet):
                        for k in range(2):
                            o = k * KV // 2
                            for m in (1, 2, 4):
                                st.then(v.tensor_copy(tile[:, o + m * hd:o + 2 * m * hd], tile[:, o:o + m * hd]))
                for c in range(C):
                    v3 = wkv[:, c, :].rearrange("p (g e) -> p g e", g=G)
                    st.then(v.tensor_reduce(gsum[:, c, :], v3, AXX, ALU.add))
                    st.then(v.tensor_scalar(gsum[:, c, :], gsum[:, c, :], 1.0 / hd, None, ALU.mult))
                    st.then(v.tensor_tensor(v3, v3, gsum[:, c, :].unsqueeze(2).to_broadcast([P, G, hd]), ALU.subtract))
                if first:
                    b3 = bias[:, :].rearrange("p (g e) -> p g e", g=G)
                    st.then(v.tensor_reduce(bsum[:, :], b3, AXX, ALU.add))
                    st.then(v.tensor_scalar(bsum[:, :], bsum[:, :], 1.0 / hd, None, ALU.mult))
                    st.then(v.tensor_tensor(b3, b3, bsum[:, :].unsqueeze(2).to_broadcast([P, G, hd]), ALU.subtract))
                    v.wait_ge(s_x, 32)
                else:
                    for c in range(C):
                        for k in range(2):
                            st.then(v.tensor_tensor(wa[:, :], wext[:, c, 0:GH * GC], att[:, k, :], ALU.mult))
                            o = GH * GC + k * GH
                            st.then(v.tensor_reduce(wext[:, c, o:o + GH],
                                                    wa[:, :].rearrange("p (h c) -> p h c", h=GH), AXX, ALU.add))
                    st.then(v.memset(R.gmax[:, :], -3.0e38))
                v.sem_inc(s_ready, 1)
                with v.Fori(0, ITER) as i:
                    if first:
                        v.wait_ge(s_xa, TPI * i)
                    nm.vector(v, i)
                    v.wait_ge(s_kv, i)
                    for j in range(TPI):
                        v.wait_ge(s_kvp, TPI * i + j + 1)
                        src = pkv[:, j % 2].rearrange("p b n -> p (b n)")
                        if first:
                            v.tensor_tensor(kc[:, j], src, bias[:, :], ALU.add).then_inc(s_kc, 1)
                        else:
                            v.tensor_copy(kc[:, j], src).then_inc(s_kc, 1)
                        v.wait_ge(s_sq, TPI * i + j + 1)
                        v.tensor_reduce(ssum[:, j], sq[:, :].rearrange("p (g e) -> p g e", g=G), AXX,
                                        ALU.add).then_inc(s_red, 1)
                    v.wait_ge(s_red, TPI * i + TPI)
                    v.tensor_scalar(ssum[:, :, :], ssum[:, :, :], 1.0 / hd, LN_EPS, ALU.mult,
                                    ALU.add).then_inc(s_ve, 1)
                    v.wait_ge(s_sd, i + 1)
                    v.reciprocal(srs[:, :, :], sstd[:, :, :]).then_inc(s_r2, 1)
                    v.wait_ge(s_r2, i + 1)
                    v.tensor_tensor(srs[:, :, :], srs[:, :, :],
                                    R.mask[:, bass.ds(TPI * i, TPI)].unsqueeze(2).to_broadcast([P, TPI, G]),
                                    ALU.mult).then_inc(s_rm, 1)
                    v.wait_ge(s_rm, i + 1)
                    for j in range(TPI):
                        k3 = kc[:, j].rearrange("p (g e) -> p g e", g=G)
                        v.tensor_tensor(k3, k3, srs[:, j].unsqueeze(2).to_broadcast([P, G, hd]),
                                        ALU.mult).then_inc(s_k1, 1)
                        if first:
                            v.wait_ge(s_k1, TPI * i + j + 1)
                            v.tensor_tensor(kc[:, j], kc[:, j], gam[:, :], ALU.mult).then_inc(s_k2, 1)
                            v.wait_ge(s_k2, TPI * i + j + 1)
                            v.scalar_tensor_tensor(kc[:, j], bet[:, :], R.mask[:, bass.ds(TPI * i + j, 1)],
                                                   kc[:, j], ALU.mult, ALU.add).then_inc(s_k3, 1)
                    v.wait_ge(s_ec, TPI * i + TPI)
                    v.wait_ge(s_out, 16 * i)
                    if first:
                        v.tensor_tensor(tabt[:, :, :], ext[:, :, :],
                                        R.nsrc[:, bass.ds(TPI * i, TPI)].unsqueeze(2).to_broadcast([P, TPI, GCN]),
                                        ALU.mult).then_inc(s_tab, 1)
                    else:
                        v.tensor_copy(tabt[:, :, :], ext[:, :, 0:TAB]).then_inc(s_tab, 1)
                        v.tensor_copy(R.adst[:, bass.ds(TPI * i, TPI), :], ext[:, :, TAB:EXT]).then_inc(s_tab_d, 1)
                        for j in range(TPI):
                            v.tensor_tensor(R.gmax[:, :], R.gmax[:, :], ext[:, j, GH * GC:TAB],
                                            ALU.max).then_inc(s_gm, 1)
                            v.wait_ge(s_gm, TPI * i + j + 1)
                v.wait_ge(s_acc, 1)
                v.tensor_copy(R.kvsum[:, 0:PAIRS * P], pacc[:, 0:PAIRS * P])

            def evac(a, i, j):
                a.wait_ge(s_ep, TPI * i + j + 1)
                a.activation(ext[:, j], pext[:, 0:EXT], ACT.Copy).then_inc(s_ec, 1)
                a.wait_ge(s_kc, TPI * i + j + 1)
                a.wait_ge(s_red, TPI * i + j)
                a.activation(sq[:, :], kc[:, j], ACT.Square).then_inc(s_sq, 1)

            @block.scalar
            def _(a):
                with a.Fori(0, ITER) as i:
                    nm.scalar_root(a, i)
                    for j in range(TPI):
                        if j == 0:
                            a.wait_ge(s_ep, TPI * i)
                            a.wait_ge(s_tab, i)
                            if not first:
                                a.wait_ge(s_gm, TPI * i)
                                a.wait_ge(s_tab_d, i)
                        nm.scalar_copy(a, i, j)
                        if j >= 1:
                            evac(a, i, j - 1)
                    evac(a, i, TPI - 1)
                    a.wait_ge(s_ve, i + 1)
                    a.activation(sstd[:, :, :], ssum[:, :, :], ACT.Sqrt).then_inc(s_sd, 1)

            @block.tensor
            def _(t):
                t.wait_ge(s_z, 1)
                t.matmul(pacc[:, 0:PAIRS * P], zero[:, 0:P], zero[:, 0:PAIRS * P], start=True, stop=False, skip_group_check=True)
                t.wait_ge(s_ready, 1)
                with t.Fori(0, ITER) as i:
                    nm.tensor(t, i, 0)
                    for j in range(TPI):
                        if j + 1 < TPI:
                            nm.tensor(t, i, j + 1)
                        t.wait_ge(nm.s_xt, TPI * i + j + 1)
                        t.wait_ge(s_kc, TPI * i + (j - 1 if j >= 2 else 0))
                        for b in range(NB_KV):
                            for c in range(C):
                                mm = t.matmul(pkv[:, j % 2, b], nm.xt[:, j, c], wkv[:, c, b * 512:(b + 1) * 512],
                                              start=(c == 0), stop=(c == C - 1))
                        mm.then_inc(s_kvp, 1)
                        t.wait_ge(s_ec, TPI * i + j)
                        for c in range(C):
                            mm = t.matmul(pext[:, 0:EXT], nm.xt[:, j, c], wext[:, c, :], start=(c == 0),
                                          stop=(c == C - 1))
                        mm.then_inc(s_ep, 1)
                    for j in range(TPI):
                        t.wait_ge(s_kdone, TPI * i + j + 1)
                        for b in range(PAIRS):
                            k = kc[:, j, b * P:(b + 1) * P]
                            u = kc[:, j, KV // 2 + b * P:KV // 2 + (b + 1) * P]
                            if not first:
                                k, u = u, k
                            mm = t.matmul(pacc[:, b * P:(b + 1) * P], k, u, start=False, stop=False,
                                          skip_group_check=True)
                    mm.then_inc(s_kv, 1)
                t.wait_ge(s_kv, ITER)
                t.sem_inc(s_acc, 1)



def block_mask(g, st, tile, width):
    st.then(g.memset(tile[:, :], 1.0))
    v = tile[:, :].rearrange("p (g e) -> p g e", e=width)
    n = P // width
    st.then(g.affine_select(out=v, in_=v, compare_op=ALU.is_ge, fill=0.0, base=0,
                            pattern=[[-width, n], [0, width]], channel_multiplier=1))
    st.then(g.affine_select(out=v, in_=v, compare_op=ALU.is_ge, fill=0.0, base=width - 1,
                            pattern=[[width, n], [0, width]], channel_multiplier=-1))


def fold0(nc, R, A):
    with Phase(nc, "fold0") as f:
        diag = f.sb("diag", [P, P])
        bd = f.sb("bd", [P, C, P])
        wqt = f.sb("wqt", [P, C, D])
        w1 = f.sb("w1", [P, C, D])
        bq = f.sb("bq", [P, C])
        b1 = f.sb("b1", [P, C])
        rwt = f.sb("rwt", [P, C, D])
        bk = f.sb("bk", [P, C])
        pr = f.ps("pr", [P, C, 512])
        pb = f.ps("pb", [P, 512])
        pw = f.ps("pw", [P, C, 512])
        loaded, made, step, masked, mixed, copied, folded = (
            f.sem(n) for n in ("loaded", "made", "step", "masked", "mixed", "copied", "folded"))
        with nc.Block() as block:
            @block.sync
            def _(s):
                s.dma_start(wqt[:, :, :], rows(A.m0_wqt)).then_inc(loaded, 16)
                s.dma_start(w1[:, :, :], rows(A.m0_w1)).then_inc(loaded, 16)
                s.dma_start(bq[:, :], A.m0_bq_t).then_inc(loaded, 16)
                s.dma_start(b1[:, :], A.m0_b1_t).then_inc(loaded, 16)

            @block.gpsimd
            def _(g):
                block_mask(g, Steps(g, made), diag, HC0)

            @block.vector
            def _(v):
                st = Steps(v, step)
                v.wait_ge(made, 3)
                for k in range(C):
                    v.scalar_tensor_tensor(bd[:, k, :], R.kvsum[:, k * P:(k + 1) * P], 1.0 / N, diag[:, :], ALU.mult,
                                           ALU.mult).then_inc(masked, 1)
                v.wait_ge(mixed, 1)
                for k in range(C):
                    st.then(v.tensor_copy(rwt[:, k, :], pr[:, k, 0:D]))
                    st.then(v.tensor_tensor(rwt[:, k, k * P:(k + 1) * P], rwt[:, k, k * P:(k + 1) * P], R.ident[:, :],
                                            ALU.add))
                st.then(v.tensor_copy(bk[:, :], pb[:, 0:C]))
                v.sem_inc(copied, 1)
                v.wait_ge(folded, 1)
                v.tensor_copy(R.weff[:, :, :], pw[:, :, 0:D])
                v.wait_ge(loaded, 64)
                v.tensor_tensor(R.beff[:, :], pb[:, 64:64 + C], b1[:, :], ALU.add)

            @block.tensor
            def _(t):
                t.wait_ge(loaded, 64)
                t.wait_ge(masked, C)
                for k in range(C):
                    t.matmul(pr[:, k, 0:D], bd[:, k, :], wqt[:, k, :], start=True, stop=True)
                for k in range(C):
                    mm = t.matmul(pb[:, k:k + 1], bd[:, k, :], bq[:, k:k + 1], start=True, stop=True)
                mm.then_inc(mixed, 1)
                t.wait_ge(copied, 1)
                for m in range(C):
                    for k in range(C):
                        t.matmul(pw[:, m, 0:D], rwt[:, k, m * P:(m + 1) * P], w1[:, k, :], start=(k == 0),
                                 stop=(k == C - 1))
                for m in range(C):
                    for k in range(C):
                        mm = t.matmul(pb[:, 64 + m:65 + m], w1[:, k, m * P:(m + 1) * P], bk[:, k:k + 1],
                                      start=(k == 0), stop=(k == C - 1))
                mm.then_inc(folded, 1)


def fold1(nc, R, A):
    K = HEADS * HC1 // P
    with Phase(nc, "fold1") as f:
        diag = f.sb("diag", [P, P])
        bd = f.sb("bd", [P, K, P])
        wqt = f.sb("wqt", [P, K, D])
        wout = f.sb("wout", [P, K, D])
        m1 = f.sb("m1", [P, K, D])
        pm = f.ps("pm", [P, K, 512])
        pw = f.ps("pw", [P, C, 512])
        loaded, made, masked, mixed, copied, folded, red = (
            f.sem(n) for n in ("loaded", "made", "masked", "mixed", "copied", "folded", "red"))
        with nc.Block() as block:
            @block.sync
            def _(s):
                s.dma_start(wqt[:, :, :], rows(A.m1_wqt)).then_inc(loaded, 16)
                s.dma_start(wout[:, :, :], rows(A.m1_wout)).then_inc(loaded, 16)

            @block.gpsimd
            def _(g):
                block_mask(g, Steps(g, made), diag, HC1)
                g.partition_all_reduce(R.gmaxa[:, :], R.gmax[:, :], P, bass.bass_isa.ReduceOp.max).then_inc(red, 1)

            @block.vector
            def _(v):
                v.wait_ge(made, 3)
                for k in range(K):
                    v.scalar_tensor_tensor(bd[:, k, :], R.kvsum[:, k * P:(k + 1) * P], 1.0 / N, diag[:, :], ALU.mult,
                                           ALU.mult).then_inc(masked, 1)
                v.wait_ge(mixed, 1)
                v.tensor_copy(m1[:, :, :], pm[:, :, 0:D]).then_inc(copied, 1)
                v.wait_ge(folded, 1)
                v.tensor_copy(R.weff[:, :, :], pw[:, :, 0:D])

            @block.tensor
            def _(t):
                t.wait_ge(loaded, 32)
                t.wait_ge(masked, K)
                for k in range(K):
                    mm = t.matmul(pm[:, k, 0:D], bd[:, k, :], wout[:, k, :], start=True, stop=True)
                mm.then_inc(mixed, 1)
                t.wait_ge(copied, 1)
                for m in range(C):
                    for k in range(K):
                        mm = t.matmul(pw[:, m, 0:D], wqt[:, k, m * P:(m + 1) * P], m1[:, k, :], start=(k == 0),
                                      stop=(k == K - 1))
                mm.then_inc(folded, 1)



def xtile(R, n):
    return R.X[:, bass.ds(n, 1), :].rearrange("p a d -> p (a d)")


def mixer0(nc, R, A):
    with Phase(nc, "mix0") as f:
        w2 = f.sb("w2", [P, C, D])
        b2 = f.sb("b2", [1, D])
        hid = f.sb("hid", [P, C, TOK])
        ph = f.ps("ph", [P, 4, 512])
        po = f.ps("po", [P, 2, 512])
        s_w, s_h, s_g, s_o, s_a, s_free = (f.sem(n) for n in ("w", "h", "g", "o", "a", "free"))
        with nc.Block() as block:
            @block.sync
            def _(s):
                s.dma_start(w2[:, :, :], rows(A.m0_w2)).then_inc(s_w, 16)
                s.dma_start(b2[:, :], A.m0_b2).then_inc(s_w, 16)

            @block.tensor
            def _(t):
                t.wait_ge(s_w, 32)
                with t.Fori(0, ITER) as i:
                    t.wait_ge(s_g, 4 * i)
                    for fb in range(C):
                        for h in range(2):
                            for c in range(C):
                                mm = t.matmul(ph[:, 2 * fb + h, 0:HALF], R.weff[:, c, fb * P:(fb + 1) * P],
                                              R.XT[:, c, bass.ds(i * TOK + h * HALF, HALF)], start=(c == 0),
                                              stop=(c == C - 1))
                            mm.then_inc(s_h, 1)
                    t.wait_ge(s_g, 4 * i + 4)
                    for j in range(TPI):
                        t.wait_ge(s_a, TPI * i + (j - 1 if j >= 2 else 0))
                        t.matmul(po[:, j % 2, 0:D], R.ones[0:1, :], b2[0:1, :], start=True, stop=False)
                        for c in range(C):
                            mm = t.matmul(po[:, j % 2, 0:D], hid[:, c, j * P:(j + 1) * P], w2[:, c, :], start=False,
                                          stop=(c == C - 1))
                        mm.then_inc(s_o, 1)

            @block.scalar
            def _(a):
                with a.Fori(0, ITER) as i:
                    a.wait_ge(s_o, TPI * i)
                    for fb in range(C):
                        for h in range(2):
                            a.wait_ge(s_h, 4 * i + 2 * fb + h + 1)
                            a.activation(hid[:, fb, h * HALF:(h + 1) * HALF], ph[:, 2 * fb + h, 0:HALF], ACT.Gelu,
                                         bias=R.beff[:, fb:fb + 1]).then_inc(s_g, 1)

            @block.vector
            def _(v):
                with v.Fori(0, ITER) as i:
                    for j in range(TPI):
                        v.wait_ge(s_o, TPI * i + j + 1)
                        xj = xtile(R, TPI * i + j)
                        v.tensor_tensor(xj, xj, po[:, j % 2, 0:D], ALU.add).then_inc(s_a, 1)



def edges(nc, R, tag, table, nslots, src_ix, dst_rel, wtab, wnext, acc, heads=0, width=0, adst=None, gmax=None):
    F = acc.shape[2]
    FEAT = heads * width
    ROW = table.shape[1]
    Q = nslots // TURN
    with Phase(nc, tag) as f:
        rowsb = f.sb("rows", [P, NBUF, GROUP, F])
        ix = f.sb("ix", [P, NBUF, GROUP], U32)
        hot = f.sb("hot", [P, NBUF, GROUP, P])
        po = f.ps("po", [P, GROUP, 512])
        s_rows = [f.sem(f"rows{b}") for b in range(NBUF)]
        s_ix, s_hot, s_sum, s_acc, s_one, s_seen = (f.sem(n) for n in ("ix", "hot", "sum", "acc", "one", "seen"))
        if heads:
            hott = f.sb("hott", [P, 2, GROUP, P])
            adw = f.sb("adw", [P, 2, GROUP, heads])
            z = f.sb("z", [P, GROUP, heads])
            lz = f.sb("lz", [P, GROUP, heads])
            zm = f.sb("zm", [P, GROUP, heads])
            lm = f.sb("lm", [P, GROUP, heads])
            ptt = f.ps("ptt", [P, GROUP * P])
            pad = f.ps("pad", [P, 2, 512])
            s_tp, s_tt, s_adw, s_ad, s_z, s_zm, s_lz, s_lm, s_d, s_ex, s_msg = (
                f.sem(n) for n in ("tp", "tt", "adw", "ad", "z", "zm", "lz", "lm", "d", "ex", "msg"))

        def windows(engine, at, n):
            _, ws = nc.values_load_multi_w_load_instructions(
                at, engines=(engine,), min_val=0, max_val=W - 1,
                skip_runtime_bounds_check_because="a count of at most W - 1 windows")
            assert len(ws) == n
            return ws

        with nc.Block() as block:
            @block.gpsimd
            def _(g):
                def gather(b, copied):
                    g.wait_ge(s_ix, copied)
                    g.sem_inc(s_seen, 1)
                    for u in range(GROUP):
                        g.indirect_dma_start(rowsb[:, b, u, 0:ROW], None, table,
                                             bass.IndirectOffsetOnAxis(ix[:, b, u:u + 1], 0)).then_inc(s_rows[b], 16)

                with g.Fori(0, Q) as i:
                    for b in range(NBUF):
                        gather(b, NBUF * i + b + 1)
                if heads:
                    gather(0, NBUF * Q + 1)

            @block.scalar
            def _(a):
                def indices(q, b):
                    a.activation(ix[:, b], src_ix[:, bass.ds(GROUP * q, GROUP)], ACT.Copy).then_inc(s_ix, 1)

                def window_scores(par, ws):
                    for u in range(GROUP):
                        ins = a.activation(adw[:, par, u], adst[:, bass.ds(ws[u], 1), :].rearrange("p a h -> p (a h)"),
                                           ACT.Copy)
                    ins.then_inc(s_adw, 1)

                def turned(q, par):
                    a.wait_ge(s_tp, q + 1)
                    a.activation(hott[:, par], ptt[:, :].rearrange("p (u e) -> p u e", u=GROUP), ACT.Copy)\
                        .then_inc(s_tt, 1)

                def weight(q, b):
                    a.wait_ge(s_d, q + 1)
                    a.activation(rowsb[:, b, :, FEAT:FEAT + heads], z[:, :, :], ACT.Exp).then_inc(s_ex, 1)

                for b in range(NBUF):
                    indices(b, b)
                if heads:
                    ws = windows(ENG.Activation, wtab[0:1, 0:2 * GROUP], 2 * GROUP)
                    for q in range(2):
                        window_scores(q, ws[q * GROUP:(q + 1) * GROUP])
                        turned(q, q)
                    weight(0, 0)
                with a.Fori(0, Q) as i:
                    if heads:
                        ws = windows(ENG.Activation, wnext[0:1, bass.ds(TURN * i, TURN)], TURN)
                    for b in range(NBUF):
                        q = NBUF * i + b
                        if heads:
                            weight(q + 1, (b + 1) % NBUF)
                            a.wait_ge(s_ad, q + 1)
                            window_scores(b % 2, ws[b * GROUP:(b + 1) * GROUP])
                        a.wait_ge(s_sum, GROUP * q + GROUP)
                        indices(q + NBUF, b)
                        if heads:
                            turned(q + 2, b % 2)

            @block.vector
            def _(v):
                def one_hot(q, b):
                    v.tensor_tensor(hot[:, b], R.iota[:, :].unsqueeze(1).to_broadcast([P, GROUP, P]),
                                    dst_rel[:, bass.ds(GROUP * q, GROUP)].unsqueeze(2).to_broadcast([P, GROUP, P]),
                                    ALU.is_equal).then_inc(s_hot, 1)

                def exponents(q, b, gathered):
                    v.wait_ge(s_ad, q + 1)
                    ad = pad[:, b % 2, 0:GROUP * heads].rearrange("p (u h) -> p u h", h=heads)
                    v.tensor_tensor(zm[:, :, :], ad, gmax[:, :].unsqueeze(1).to_broadcast([P, GROUP, heads]),
                                    ALU.add).then_inc(s_zm, 1)
                    v.wait_ge(s_rows[b], gathered)
                    v.tensor_tensor(z[:, :, :], ad, rowsb[:, b, :, FEAT:FEAT + heads], ALU.add).then_inc(s_z, 1)
                    v.wait_ge(s_zm, q + 1)
                    v.scalar_tensor_tensor(lm[:, :, :], zm[:, :, :], 0.2, zm[:, :, :], ALU.mult, ALU.max)\
                        .then_inc(s_lm, 1)
                    v.wait_ge(s_z, q + 1)
                    v.scalar_tensor_tensor(lz[:, :, :], z[:, :, :], 0.2, z[:, :, :], ALU.mult, ALU.max)\
                        .then_inc(s_lz, 1)
                    v.wait_ge(s_lm, q + 1)
                    v.wait_ge(s_lz, q + 1)
                    v.tensor_tensor(z[:, :, :], lz[:, :, :], lm[:, :, :], ALU.subtract).then_inc(s_d, 1)

                if F > ROW:
                    v.memset(rowsb[:, :, :, ROW:F], 1.0).then_inc(s_one, 1)
                one_hot(0, 0)
                one_hot(1, 1)
                if heads:
                    exponents(0, 0, 16 * GROUP)
                with v.Fori(0, Q) as i:
                    wt = windows(ENG.DVE, wtab[0:1, bass.ds(TURN * i, TURN)], TURN)
                    for b in range(NBUF):
                        q = NBUF * i + b
                        if heads:
                            v.wait_ge(s_ex, q + 1)
                            m = rowsb[:, b, :, 0:FEAT].rearrange("p u (h c) -> p u h c", h=heads)
                            v.tensor_tensor(m, m, rowsb[:, b, :, FEAT:FEAT + heads].unsqueeze(3)
                                            .to_broadcast([P, GROUP, heads, width]), ALU.mult).then_inc(s_msg, 1)
                            nb = (b + 1) % NBUF
                            exponents(q + 1, nb, 16 * GROUP * (i + 1 + (b + 1) // NBUF))
                        one_hot(q + 2, (b + 2) % NBUF)
                        for u in range(GROUP):
                            v.wait_ge(s_sum, GROUP * q + u + 1)
                            v.wait_ge(s_acc, GROUP * q + u + GROUP)
                            aw = acc[:, bass.ds(wt[b * GROUP + u], 1), :].rearrange("p a d -> p (a d)")
                            v.tensor_tensor(aw, aw, po[:, u, 0:F], ALU.add).then_inc(s_acc, 1)

            @block.tensor
            def _(t):
                def scores(q, b):
                    t.wait_ge(s_hot, q + 1)
                    for u in range(GROUP):
                        mm = t.transpose(ptt[:, u * P:(u + 1) * P], hot[:, b, u], R.ident[:, :])
                    mm.then_inc(s_tp, 1)
                    t.wait_ge(s_tt, q + 1)
                    t.wait_ge(s_adw, q + 1)
                    for u in range(GROUP):
                        o = u * heads
                        mm = t.matmul(pad[:, b % 2, o:o + heads], hott[:, b % 2, u], adw[:, b % 2, u], start=True, stop=True)
                    mm.then_inc(s_ad, 1)

                t.sem_inc(s_acc, GROUP)
                if F > ROW:
                    t.wait_ge(s_one, 1)
                if heads:
                    scores(0, 0)
                    scores(1, 1)
                with t.Fori(0, Q) as i:
                    for b in range(NBUF):
                        q = NBUF * i + b
                        if heads:
                            t.wait_ge(s_msg, q + 1)
                        else:
                            t.wait_ge(s_hot, q + 1)
                            t.wait_ge(s_rows[b], 16 * GROUP * i + 16 * GROUP)
                        for u in range(GROUP):
                            t.wait_ge(s_acc, GROUP * q + u + 1)
                            t.matmul(po[:, u, 0:F], hot[:, b, u], rowsb[:, b, u, :], start=True, stop=True)\
                                .then_inc(s_sum, 1)
                        if heads:
                            scores(q + 2, (b + 2) % NBUF)


def loops(nc, R, tag, table, acc, heads, width, adst, gmax):
    FEAT = heads * width
    with Phase(nc, tag) as f:
        z = f.sb("z", [P, W, heads])
        zm = f.sb("zm", [P, W, heads])
        s_in, s_st, s_go, s_ex = (f.sem(n) for n in ("in", "st", "go", "ex"))
        with nc.Block() as block:
            @block.sync
            def _(s):
                s.dma_start(acc[:, :, :], table.rearrange("(t p) d -> p t d", p=P)).then_inc(s_in, 16)

            @block.vector
            def _(v):
                st = Steps(v, s_st)
                st.then(v.tensor_tensor(zm[:, :, :], adst[:, :, :], gmax[:, :].unsqueeze(1).to_broadcast([P, W, heads]),
                                        ALU.add))
                st.then(v.scalar_tensor_tensor(zm[:, :, :], zm[:, :, :], 0.2, zm[:, :, :], ALU.mult, ALU.max))
                v.wait_ge(s_in, 16)
                st.then(v.tensor_tensor(z[:, :, :], acc[:, :, FEAT:FEAT + heads], adst[:, :, :], ALU.add))
                st.then(v.scalar_tensor_tensor(z[:, :, :], z[:, :, :], 0.2, z[:, :, :], ALU.mult, ALU.max))
                st.then(v.tensor_tensor(z[:, :, :], z[:, :, :], zm[:, :, :], ALU.subtract))
                v.sem_inc(s_go, 1)
                v.wait_ge(s_ex, 1)
                a4 = acc[:, :, 0:FEAT].rearrange("p t (h c) -> p t h c", h=heads)
                v.tensor_tensor(a4, a4, acc[:, :, FEAT:FEAT + heads].unsqueeze(3).to_broadcast([P, W, heads, width]),
                                ALU.mult)

            @block.scalar
            def _(a):
                a.wait_ge(s_go, 1)
                a.activation(acc[:, :, FEAT:FEAT + heads], z[:, :, :], ACT.Exp).then_inc(s_ex, 1)


def clear(nc, tile):
    with nc.Block() as block:
        @block.vector
        def _(v):
            v.memset(tile, 0.0)



def gcn_finish(nc, R, A):
    with Phase(nc, "gcnf") as f:
        wout = f.sb("wout", [GCN + 1, D])
        bg = f.sb("bg", [P, GCN])
        nd = f.sb("nd", [P, W])
        h = f.sb("h", [P, TPI, GCN + 1])
        ht = f.sb("ht", [GCN + 1, TPI, P])
        pt = f.ps("pt", [P, 2, 512])
        po = f.ps("po", [P, 2, 512])
        s_w, s_st, s_sq, s_rt, s_ready, s_h, s_t, s_c, s_o, s_a, s_m = (
            f.sem(n) for n in ("w", "st", "sq", "rt", "ready", "h", "t", "c", "o", "a", "m"))
        with nc.Block() as block:
            @block.sync
            def _(s):
                s.dma_start(wout[0:GCN, :], A.gcn_wout).then_inc(s_w, 16)
                s.dma_start(wout[GCN:GCN + 1, :], A.gcn_bout).then_inc(s_w, 16)
                s.dma_start(bg[:, :], spread(A.gcn_b)).then_inc(s_w, 16)

            @block.vector
            def _(v):
                st = Steps(v, s_st)
                st.then(v.tensor_scalar(nd[:, :], R.gcn[:, :, GCN], 1.0, None, ALU.max))
                v.sem_inc(s_sq, 1)
                v.memset(h[:, :, GCN:GCN + 1], 1.0).then_inc(s_m, 1)
                v.wait_ge(s_rt, 1)
                st.then(v.reciprocal(nd[:, :], nd[:, :]))
                g3 = R.gcn[:, :, 0:GCN]
                v.wait_ge(s_w, 48)
                st.then(v.tensor_tensor(g3, g3, nd[:, :].unsqueeze(2).to_broadcast([P, W, GCN]), ALU.mult))
                st.then(v.tensor_tensor(g3, g3, bg[:, :].unsqueeze(1).to_broadcast([P, W, GCN]), ALU.add))
                with v.Fori(0, ITER) as i:
                    v.wait_ge(s_t, TPI * i)
                    v.tensor_scalar(h[:, :, 0:GCN], R.gcn[:, bass.ds(TPI * i, TPI), 0:GCN], 0.0, None, ALU.max)\
                        .then_inc(s_h, 1)
                    for j in range(TPI):
                        v.wait_ge(s_o, TPI * i + j + 1)
                        xj = xtile(R, TPI * i + j)
                        v.tensor_tensor(xj, xj, po[:, j % 2, 0:D], ALU.add).then_inc(s_a, 1)

            @block.scalar
            def _(a):
                a.wait_ge(s_sq, 1)
                a.activation(nd[:, :], nd[:, :], ACT.Sqrt).then_inc(s_rt, 1)
                with a.Fori(0, ITER) as i:
                    a.wait_ge(s_o, TPI * i)
                    for j in range(TPI):
                        a.wait_ge(s_t, TPI * i + j + 1)
                        a.activation(ht[:, j], pt[0:GCN + 1, j % 2, 0:P], ACT.Copy).then_inc(s_c, 1)

            @block.tensor
            def _(t):
                t.wait_ge(s_w, 48)
                t.wait_ge(s_m, 1)
                with t.Fori(0, ITER) as i:
                    t.wait_ge(s_h, i + 1)
                    for j in range(TPI):
                        t.wait_ge(s_c, TPI * i + (j - 1 if j >= 2 else 0))
                        t.transpose(pt[0:GCN + 1, j % 2, 0:P], h[:, j], R.ident[:, :]).then_inc(s_t, 1)
                        t.wait_ge(s_c, TPI * i + j + 1)
                        t.wait_ge(s_a, TPI * i + (j - 1 if j >= 2 else 0))
                        t.matmul(po[:, j % 2, 0:D], ht[:, j], wout[:, :], start=True, stop=True).then_inc(s_o, 1)



def gates0(nc, R, A):
    with Phase(nc, "gate0") as f:
        nm = Norm(f, R)
        wr = f.sb("wr", [P, C, E0])
        br = f.sb("br", [P, E0])
        bo = f.sb("bo", [E0, D])
        lg = f.sb("lg", [P, TPI, E0])
        mx = f.sb("mx", [P, TPI])
        gt = f.sb("gt", [E0, TPI, P])
        pl = f.ps("pl", [P, 512])
        pg = f.ps("pg", [P, 512])
        po = f.ps("po", [P, 2, 512])
        s_w, s_l, s_m, s_e, s_gt, s_gc, s_o, s_a, s_xr, s_c = (
            f.sem(n) for n in ("w", "l", "m", "e", "gt", "gc", "o", "a", "xr2", "c"))
        s_g = [f.sem(f"g{k}") for k in range(5)]
        with nc.Block() as block:
            @block.sync
            def _(s):
                s.dma_start(wr[:, :, :], rows(A.f0_wr)).then_inc(s_w, 16)
                s.dma_start(br[:, :], spread(A.f0_br)).then_inc(s_w, 16)
                s.dma_start(bo[:, :], A.f0_bo).then_inc(s_w, 16)

            @block.vector
            def _(v):
                v.wait_ge(s_w, 48)
                with v.Fori(0, ITER) as i:
                    nm.vector(v, i)
                    v.wait_ge(s_l, TPI * i + TPI)
                    v.tensor_tensor(lg[:, :, :], pl[:, 0:TPI * E0].rearrange("p (t e) -> p t e", e=E0),
                                    br[:, :].unsqueeze(1).to_broadcast([P, TPI, E0]), ALU.add).then_inc(s_g[0], 1)
                    v.wait_ge(s_g[0], i + 1)
                    v.tensor_reduce(mx[:, :], lg[:, :, :], AXX, ALU.max).then_inc(s_g[1], 1)
                    v.wait_ge(s_g[1], i + 1)
                    v.tensor_tensor(lg[:, :, :], lg[:, :, :], mx[:, :].unsqueeze(2).to_broadcast([P, TPI, E0]),
                                    ALU.subtract).then_inc(s_m, 1)
                    v.wait_ge(s_e, i + 1)
                    v.tensor_reduce(mx[:, :], lg[:, :, :], AXX, ALU.add).then_inc(s_g[2], 1)
                    v.wait_ge(s_g[2], i + 1)
                    v.reciprocal(mx[:, :], mx[:, :]).then_inc(s_g[3], 1)
                    v.wait_ge(s_g[3], i + 1)
                    v.tensor_tensor(R.gate[:, bass.ds(TPI * i, TPI), 0:E0], lg[:, :, :],
                                    mx[:, :].unsqueeze(2).to_broadcast([P, TPI, E0]), ALU.mult).then_inc(s_c, 1)
                    v.tensor_tensor(lg[:, :, :], lg[:, :, :], mx[:, :].unsqueeze(2).to_broadcast([P, TPI, E0]),
                                    ALU.mult).then_inc(s_g[4], 1)
                    for j in range(TPI):
                        v.wait_ge(s_o, TPI * i + j + 1)
                        xj = xtile(R, TPI * i + j)
                        v.tensor_tensor(xj, xj, po[:, j % 2, 0:D], ALU.add).then_inc(s_a, 1)

            @block.scalar
            def _(a):
                with a.Fori(0, ITER) as i:
                    nm.scalar_root(a, i)
                    a.wait_ge(s_l, TPI * i)
                    for j in range(TPI):
                        nm.scalar_copy(a, i, j)
                    a.wait_ge(s_m, i + 1)
                    a.activation(lg[:, :, :], lg[:, :, :], ACT.Exp).then_inc(s_e, 1)
                    for j in range(TPI):
                        a.wait_ge(s_gt, TPI * i + j + 1)
                        a.activation(gt[:, j], pg[0:E0, (j % 4) * P:(j % 4 + 1) * P], ACT.Copy).then_inc(s_gc, 1)

            @block.tensor
            def _(t):
                t.wait_ge(s_w, 48)
                with t.Fori(0, ITER) as i:
                    nm.tensor(t, i, 0)
                    t.wait_ge(s_g[0], i)
                    for j in range(TPI):
                        if j + 1 < TPI:
                            nm.tensor(t, i, j + 1)
                        t.wait_ge(nm.s_xt, TPI * i + j + 1)
                        for c in range(C):
                            mm = t.matmul(pl[:, j * E0:(j + 1) * E0], nm.xt[:, j, c], wr[:, c, :], start=(c == 0),
                                          stop=(c == C - 1))
                        mm.then_inc(s_l, 1)
                    t.wait_ge(s_g[4], i + 1)
                    for j in range(TPI):
                        t.wait_ge(s_gc, TPI * i + (j - 3 if j >= 4 else 0))
                        t.transpose(pg[0:E0, (j % 4) * P:(j % 4 + 1) * P], lg[:, j], R.ident[:, :]).then_inc(s_gt, 1)
                        t.wait_ge(s_gc, TPI * i + j + 1)
                        t.wait_ge(s_a, TPI * i + (j - 1 if j >= 2 else 0))
                        t.matmul(po[:, j % 2, 0:D], gt[:, j], bo[:, :], start=True, stop=True).then_inc(s_o, 1)


def experts0(nc, R, A):
    with Phase(nc, "exp0") as f:
        w1 = f.sb("w1", [P, E0, C, D])
        w2 = f.sb("w2", [P, E0, C, D])
        wo = f.sb("wo", [P, E0, C, D])
        bn = f.sb("bn", [P, 2, 5, E0 * C])
        scale = f.sb("scale", [P, 2, E0 * C])
        shift = f.sb("shift", [P, 2, E0 * C])
        h1 = f.sb("h1", [P, C, TOK])
        h2 = f.sb("h2", [P, C, TOK])
        ph = f.ps("ph", [P, 4, 512])
        po = f.ps("po", [P, 4, 512])
        s_w, s_b, s_st, s_v, s_rt, s_ready, s_h, s_g, s_o, s_a, s_l2 = (
            f.sem(n) for n in ("w", "b", "st", "v", "rt", "ready", "h", "g", "o", "a", "l2"))
        ix = f.sb("ix", [P, 2, GROUP8], U32)
        rec = f.sb("rec", [P, 2, GROUP8, 2], I32)
        s_seen = f.sem("seen")
        s_ix, s_sc = f.sem("ix"), [f.sem(f"sc{k}") for k in range(2)]
        with nc.Block() as block:
            @block.gpsimd
            def _(g):
                with g.Fori(0, FB // (2 * GROUP8)) as i:
                    for b in range(2):
                        g.wait_ge(s_sc[b], 16 * GROUP8 * i)
                        q = 2 * i + b
                        g.tensor_copy(ix[:, b], R.fpos[:, bass.ds(GROUP8 * q, GROUP8)]).then_inc(s_ix, 1)
                        g.tensor_copy(rec[:, b].rearrange("p t k -> p (t k)"),
                                      R.frec[:, bass.ds(GROUP8 * q, GROUP8), :].rearrange("p t k -> p (t k)"))\
                            .then_inc(s_ix, 1)
                        g.wait_ge(s_ix, 4 * i + 2 * b + 2)
                        g.sem_inc(s_seen, 1)
                        for u in range(GROUP8):
                            g.indirect_dma_start(R.fsorted, bass.IndirectOffsetOnAxis(ix[:, b, u:u + 1], 0),
                                                 rec[:, b, u], None).then_inc(s_sc[b], 16)
                for b in range(2):
                    g.wait_ge(s_sc[b], 16 * FB // 2)

            @block.sync
            def _(s):
                s.dma_start(bn[:, :, :, :], A.f0_bn).then_inc(s_b, 16)
                for wt, wd in ((w1, A.f0_w1), (w2, A.f0_w2), (wo, A.f0_wo)):
                    for e in range(E0):
                        s.dma_start(wt[:, e], rows(wd[e])).then_inc(s_w, 16)

            @block.tensor
            def _(t):
                t.wait_ge(s_w, 16 * 3 * E0)
                with t.Fori(0, ITER) as i:
                    base = 8 * E0 * i

                    def layer(e, l):
                        k = 2 * e + l
                        for fb in range(C):
                            for h in range(2):
                                n = 2 * fb + h
                                t.wait_ge(s_g, base + (4 * (k - 1) + n + 1 if k else 0))
                                for c in range(C):
                                    x = R.XT[:, c, bass.ds(i * TOK + h * HALF, HALF)] if l == 0 else \
                                        h1[:, c, h * HALF:(h + 1) * HALF]
                                    w = (w1, w2)[l][:, e, c, fb * P:(fb + 1) * P]
                                    mm = t.matmul(ph[:, n, 0:HALF], w, x, start=(c == 0), stop=(c == C - 1))
                                mm.then_inc(s_h, 1)

                    layer(0, 0)
                    for e in range(E0):
                        t.wait_ge(s_g, base + 8 * e + 4)
                        layer(e, 1)
                        if e + 1 < E0:
                            layer(e + 1, 0)
                        t.wait_ge(s_g, base + 8 * e + 8)
                        for j in range(TPI):
                            n = TPI * e + j
                            t.wait_ge(s_a, TPI * E0 * i + max(n - 3, 0))
                            for c in range(C):
                                mm = t.matmul(po[:, n % 4, 0:D], h2[:, c, j * P:(j + 1) * P], wo[:, e, c, :],
                                              start=(c == 0), stop=(c == C - 1))
                            mm.then_inc(s_o, 1)

            @block.vector
            def _(v):
                st = Steps(v, s_st)
                v.wait_ge(s_b, 16)
                st.then(v.tensor_scalar(scale[:, :, :], bn[:, :, 4, :], BN_EPS, None, ALU.add))
                v.sem_inc(s_v, 1)
                v.wait_ge(s_rt, 1)
                st.then(v.reciprocal(scale[:, :, :], scale[:, :, :]))
                st.then(v.tensor_tensor(scale[:, :, :], scale[:, :, :], bn[:, :, 1, :], ALU.mult))
                st.then(v.tensor_tensor(shift[:, :, :], bn[:, :, 0, :], bn[:, :, 3, :], ALU.subtract))
                st.then(v.tensor_tensor(shift[:, :, :], shift[:, :, :], scale[:, :, :], ALU.mult))
                st.then(v.tensor_tensor(shift[:, :, :], shift[:, :, :], bn[:, :, 2, :], ALU.add))
                v.sem_inc(s_ready, 1)
                with v.Fori(0, ITER) as i:
                    for e in range(E0):
                        for j in range(TPI):
                            n = TPI * e + j
                            v.wait_ge(s_o, TPI * E0 * i + n + 1)
                            v.wait_ge(s_a, TPI * E0 * i + max(n - 6, 0))
                            xj = xtile(R, TPI * i + j)
                            g = R.gate[:, bass.ds(TPI * i + j, 1), e:e + 1].rearrange("p a b -> p (a b)")
                            v.scalar_tensor_tensor(xj, po[:, n % 4, 0:D], g, xj, ALU.mult, ALU.add).then_inc(s_a, 1)

            @block.scalar
            def _(a):
                a.wait_ge(s_v, 1)
                a.activation(scale[:, :, :], scale[:, :, :], ACT.Sqrt).then_inc(s_rt, 1)
                a.wait_ge(s_ready, 1)
                with a.Fori(0, ITER) as i:
                    for e in range(E0):
                        for l in range(2):
                            k = 2 * e + l
                            if l:
                                a.wait_ge(s_o, TPI * E0 * i + TPI * e)
                            for fb in range(C):
                                for h in range(2):
                                    n = 2 * fb + h
                                    a.wait_ge(s_h, 8 * E0 * i + 4 * k + n + 1)
                                    a.activation((h1, h2)[l][:, fb, h * HALF:(h + 1) * HALF], ph[:, n, 0:HALF],
                                                 ACT.Relu, bias=shift[:, l, C * e + fb:C * e + fb + 1],
                                                 scale=scale[:, l, C * e + fb:C * e + fb + 1]).then_inc(s_g, 1)



def finish1(nc, R, A):
    with Phase(nc, "fin1") as f:
        bias = f.sb("bias", [1, 2, D])
        den = f.sb("den", [P, W, GH])
        xt = f.sb("xt", [P, TPI, C, P])
        po = f.ps("po", [P, 2, 512])
        s_w, s_st, s_x, s_o, s_m, s_b, s_a = (f.sem(n) for n in ("w", "st", "x", "o", "m", "b", "a"))
        with nc.Block() as block:
            @block.sync
            def _(s):
                s.dma_start(bias[:, 0, :], A.gat_bias).then_inc(s_w, 16)
                s.dma_start(bias[:, 1, :], A.m1_bout).then_inc(s_w, 16)

            @block.scalar
            def _(a):
                with a.Fori(0, ITER) as i:
                    a.wait_ge(s_o, TPI * i)
                    for j in range(TPI):
                        a.activation(xt[:, j], R.XT[:, :, bass.ds((TPI * i + j) * P, P)], ACT.Copy).then_inc(s_x, 1)

            @block.tensor
            def _(t):
                t.wait_ge(s_w, 32)
                with t.Fori(0, ITER) as i:
                    for j in range(TPI):
                        t.wait_ge(s_x, TPI * i + j + 1)
                        t.wait_ge(s_b, TPI * i + (j - 1 if j >= 2 else 0))
                        for k in range(2):
                            t.matmul(po[:, j % 2, 0:D], R.ones[0:1, :], bias[0:1, k, :], start=(k == 0), stop=False)
                        for c in range(C):
                            mm = t.matmul(po[:, j % 2, 0:D], xt[:, j, c], R.weff[:, c, :], start=False,
                                          stop=(c == C - 1))
                        mm.then_inc(s_o, 1)

            @block.vector
            def _(v):
                st = Steps(v, s_st)
                st.then(v.tensor_scalar(den[:, :, :], R.gat[:, :, GH * GC:GROW], 1e-30, None, ALU.max))
                st.then(v.reciprocal(den[:, :, :], den[:, :, :]))
                with v.Fori(0, ITER) as i:
                    for j in range(TPI):
                        n = TPI * i + j
                        a3 = R.gat[:, bass.ds(n, 1), 0:GH * GC].rearrange("p a (h c) -> p (a h) c", c=GC)
                        a2 = R.gat[:, bass.ds(n, 1), 0:GH * GC].rearrange("p a d -> p (a d)")
                        d3 = den[:, bass.ds(n, 1), :].rearrange("p a h -> p (a h)").unsqueeze(2).to_broadcast([P, GH, GC])
                        v.tensor_tensor(a3, a3, d3, ALU.mult).then_inc(s_m, 1)
                        xj = xtile(R, n)
                        v.wait_ge(s_o, n + 1)
                        v.tensor_tensor(xj, xj, po[:, j % 2, 0:D], ALU.add).then_inc(s_b, 1)
                        v.wait_ge(s_m, n + 1)
                        v.wait_ge(s_b, n + 1)
                        v.tensor_tensor(xj, xj, a2, ALU.add).then_inc(s_a, 1)



def router_table(nc, R, A):
    FX = FH * FC
    EXT = FX + 2 * FH
    with Phase(nc, "rtab") as f:
        nm = Norm(f, R)
        w = f.sb("w", [P, C, EXT])
        att = f.sb("att", [P, 2, FX])
        wa = f.sb("wa", [P, FX])
        tabt = f.sb("tabt", [P, W, FROW])
        gm = f.sb("gm", [P, FH])
        pl = f.ps("pl", [P, 512])
        s_w, s_st, s_l, s_e, s_t, s_ready, s_o, s_red = (
            f.sem(n) for n in ("w_", "st", "l", "e", "t", "ready", "o", "red"))
        with nc.Block() as block:
            @block.sync
            def _(s):
                s.dma_start(w[:, :, 0:FX], rows(A.r_w)).then_inc(s_w, 16)
                for k, row in enumerate((A.r_src, A.r_dst)):
                    s.dma_start(att[:, k, :], spread(row)).then_inc(s_w, 16)
                s.wait_ge(s_t, 1)
                s.dma_start(R.tabr.rearrange("(t p) d -> p t d", p=P), tabt[:, :, :]).then_inc(s_o, 16)
                s.wait_ge(s_o, 16)

            @block.vector
            def _(v):
                st = Steps(v, s_st)
                v.wait_ge(s_w, 48)
                for c in range(C):
                    for k in range(2):
                        st.then(v.tensor_tensor(wa[:, :], w[:, c, 0:FX], att[:, k, :], ALU.mult))
                        o = FX + k * FH
                        st.then(v.tensor_reduce(w[:, c, o:o + FH], wa[:, :].rearrange("p (h c) -> p h c", h=FH), AXX,
                                                ALU.add))
                v.sem_inc(s_ready, 1)
                with v.Fori(0, ITER) as i:
                    nm.vector(v, i)
                    v.wait_ge(s_l, TPI * i + TPI)
                    v.tensor_copy(R.rext[:, bass.ds(TPI * i, TPI), :],
                                  pl[:, 0:TPI * EXT].rearrange("p (t e) -> p t e", e=EXT)).then_inc(s_e, 1)
                v.wait_ge(s_e, ITER)
                st.then(v.tensor_copy(tabt[:, :, :], R.rext[:, :, 0:FROW]))
                v.sem_inc(s_t, 1)
                st.then(v.tensor_copy(R.rdst[:, :, :], R.rext[:, :, FROW:EXT]))
                st.then(v.tensor_reduce(gm[:, :], R.rext[:, :, FX:FROW].rearrange("p t h -> p h t"), AXX, ALU.max))
                v.sem_inc(s_red, 1)

            @block.gpsimd
            def _(g):
                g.wait_ge(s_red, 1)
                g.partition_all_reduce(R.rmax[:, :], gm[:, :], P, bass.bass_isa.ReduceOp.max)

            @block.scalar
            def _(a):
                with a.Fori(0, ITER) as i:
                    nm.scalar_root(a, i)
                    a.wait_ge(s_l, TPI * i)
                    for j in range(TPI):
                        nm.scalar_copy(a, i, j)

            @block.tensor
            def _(t):
                t.wait_ge(s_ready, 1)
                with t.Fori(0, ITER) as i:
                    nm.tensor(t, i, 0)
                    t.wait_ge(s_e, i)
                    for j in range(TPI):
                        if j + 1 < TPI:
                            nm.tensor(t, i, j + 1)
                        t.wait_ge(nm.s_xt, TPI * i + j + 1)
                        for c in range(C):
                            mm = t.matmul(pl[:, j * EXT:(j + 1) * EXT], nm.xt[:, j, c], w[:, c, :], start=(c == 0),
                                          stop=(c == C - 1))
                        mm.then_inc(s_l, 1)


def router_gates(nc, R, A):
    FX = FH * FC
    K = E1
    with Phase(nc, "rgate") as f:
        z = f.sb("z", [P, W, FH])
        t16 = f.sb("t16", [P, W, FX])
        a = f.sb("a", [P, W, FX])
        m = f.sb("m", [P, W])
        r = f.sb("r", [P, W])
        bg = f.sb("bg", [P, 3, FX])
        sc = f.sb("sc", [P, W, K])
        rank = f.sb("rank", [P, W, K])
        gt = f.sb("gt", [P, W])
        b2 = f.sb("b2", [K, D])
        gs = f.sb("gs", [P, TPI, K])
        gT = f.sb("gT", [K, TPI, P])
        pg = f.ps("pg", [P, 4, 512])
        po = f.ps("po", [P, 2, 512])
        s_w, s_st, s_go, s_back, s_gs, s_gt, s_gc, s_o, s_a = (
            f.sem(n) for n in ("w", "st", "go", "back", "gs", "gt", "gc", "o", "a"))
        with nc.Block() as block:
            @block.sync
            def _(s):
                for k, row in enumerate((A.r_b, A.r_gam, A.r_bet)):
                    s.dma_start(bg[:, k, :], spread(row)).then_inc(s_w, 16)
                s.dma_start(b2[:, :], A.f1_b2).then_inc(s_w, 16)

            @block.scalar
            def _(s):
                s.wait_ge(s_go, 1)
                s.activation(r[:, :], r[:, :], ACT.Sqrt).then_inc(s_back, 1)
                s.wait_ge(s_go, 2)
                s.activation(sc[:, :, :], sc[:, :, :], ACT.Exp).then_inc(s_back, 1)
                with s.Fori(0, ITER) as i:
                    for j in range(TPI):
                        s.wait_ge(s_gt, TPI * i + j + 1)
                        s.activation(gT[:, j], pg[0:K, j % 4, 0:P], ACT.Copy).then_inc(s_gc, 1)

            @block.vector
            def _(v):
                st = Steps(v, s_st)

                def wide(t, n):
                    return t.unsqueeze(2).to_broadcast([P, W, n])

                st.then(v.tensor_scalar(z[:, :, :], R.racc[:, :, FX:FROW], 1e-30, None, ALU.max))
                st.then(v.reciprocal(z[:, :, :], z[:, :, :]))
                for h in range(FH):
                    c = slice(h * FC, (h + 1) * FC)
                    st.then(v.tensor_tensor(a[:, :, c], R.racc[:, :, c], wide(z[:, :, h], FC), ALU.mult))
                v.wait_ge(s_w, 64)

                def row(k):
                    return bg[:, k, :].unsqueeze(1).to_broadcast([P, W, FX])

                st.then(v.tensor_tensor(a[:, :, :], a[:, :, :], row(0), ALU.add))
                st.then(v.tensor_reduce(m[:, :], a[:, :, :], AXX, ALU.add))
                st.then(v.tensor_scalar(m[:, :], m[:, :], 1.0 / FX, None, ALU.mult))
                st.then(v.tensor_tensor(a[:, :, :], a[:, :, :], wide(m[:, :], FX), ALU.subtract))
                st.then(v.tensor_tensor(t16[:, :, :], a[:, :, :], a[:, :, :], ALU.mult))
                st.then(v.tensor_reduce(r[:, :], t16[:, :, :], AXX, ALU.add))
                st.then(v.tensor_scalar(r[:, :], r[:, :], 1.0 / FX, LN_EPS, ALU.mult, ALU.add))
                v.sem_inc(s_go, 1)
                v.wait_ge(s_back, 1)
                st.then(v.reciprocal(r[:, :], r[:, :]))
                st.then(v.tensor_tensor(a[:, :, :], a[:, :, :], wide(r[:, :], FX), ALU.mult))
                st.then(v.tensor_tensor(a[:, :, :], a[:, :, :], row(1), ALU.mult))
                st.then(v.tensor_tensor(a[:, :, :], a[:, :, :], row(2), ALU.add))
                st.then(v.tensor_reduce(sc[:, :, :], a[:, :, :].rearrange("p t (h c) -> p t c h", c=FC), AXX, ALU.add))
                st.then(v.tensor_scalar(sc[:, :, :], sc[:, :, :], 1.0 / FH, None, ALU.mult))
                st.then(v.memset(rank[:, :, :], 0.0))
                for k in range(K):
                    for o in range(K):
                        if o != k:
                            st.then(v.tensor_tensor(gt[:, :], sc[:, :, o], sc[:, :, k],
                                                    ALU.is_ge if o < k else ALU.is_gt))
                            st.then(v.tensor_tensor(rank[:, :, k], rank[:, :, k], gt[:, :], ALU.add))
                st.then(v.tensor_scalar(rank[:, :, :], rank[:, :, :], 1.5, None, ALU.is_lt))
                st.then(v.tensor_reduce(m[:, :], sc[:, :, :], AXX, ALU.max))
                st.then(v.tensor_tensor(sc[:, :, :], sc[:, :, :], wide(m[:, :], K), ALU.subtract))
                v.sem_inc(s_go, 1)
                v.wait_ge(s_back, 2)
                st.then(v.tensor_tensor(sc[:, :, :], sc[:, :, :], rank[:, :, :], ALU.mult))
                st.then(v.tensor_reduce(m[:, :], sc[:, :, :], AXX, ALU.add))
                st.then(v.reciprocal(m[:, :], m[:, :]))
                st.then(v.tensor_tensor(R.gate[:, :, 0:K], sc[:, :, :], wide(m[:, :], K), ALU.mult))
                with v.Fori(0, ITER) as i:
                    v.wait_ge(s_gt, TPI * i)
                    v.tensor_copy(gs[:, :, :], R.gate[:, bass.ds(TPI * i, TPI), 0:K]).then_inc(s_gs, 1)
                    for j in range(TPI):
                        v.wait_ge(s_o, TPI * i + j + 1)
                        xj = xtile(R, TPI * i + j)
                        v.tensor_tensor(xj, xj, po[:, j % 2, 0:D], ALU.add).then_inc(s_a, 1)

            @block.tensor
            def _(t):
                t.wait_ge(s_w, 64)
                with t.Fori(0, ITER) as i:
                    t.wait_ge(s_gs, i + 1)
                    for j in range(TPI):
                        t.wait_ge(s_gc, TPI * i + (j - 3 if j >= 4 else 0))
                        t.transpose(pg[0:K, j % 4, 0:P], gs[:, j], R.ident[:, :]).then_inc(s_gt, 1)
                        t.wait_ge(s_gc, TPI * i + j + 1)
                        t.wait_ge(s_a, TPI * i + (j - 1 if j >= 2 else 0))
                        t.matmul(po[:, j % 2, 0:D], gT[:, j], b2[:, :], start=True, stop=True).then_inc(s_o, 1)



def experts1(nc, R, A, out):
    HB = HID1 // P
    STEPS = 2 * HB
    with Phase(nc, "exp1") as f:
        w1 = f.sb("w1", [P, E1, C, HID1])
        w2 = f.sb("w2", [P, E1, HB, D])
        b1 = f.sb("b1", [P, E1, HB])
        hid = f.sb("hid", [P, 2, HB, TOK])
        ph = f.ps("ph", [P, 4, 512])
        po = f.ps("po", [P, 4, 512])
        s_w, s_h, s_g, s_o, s_a, s_out = (f.sem(n) for n in ("w", "h", "g", "o", "a", "out"))
        with nc.Block() as block:
            @block.sync
            def _(s):
                s.dma_start(b1[:, :, :], A.f1_b1).then_inc(s_w, 16)
                for e in range(E1):
                    s.dma_start(w1[:, e], rows(A.f1_w1[e])).then_inc(s_w, 16)
                    s.dma_start(w2[:, e], rows(A.f1_w2[e])).then_inc(s_w, 16)
                with s.Fori(0, ITER - 1) as i:
                    s.wait_ge(s_a, TPI * E1 * i + TPI * E1)
                    s.dma_start(out[bass.ds(i * TOK, TOK), :].rearrange("(t p) d -> p t d", p=P),
                                R.X[:, bass.ds(TPI * i, TPI), :]).then_inc(s_out, 16)
                s.wait_ge(s_a, TPI * E1 * ITER)
                s.dma_start(out[(ITER - 1) * TOK:(W - 1) * P, :].rearrange("(t p) d -> p t d", p=P),
                            R.X[:, W - TPI:W - 1, :]).then_inc(s_out, 16)
                s.dma_start(out[(W - 1) * P:N, :], R.X[0:N - (W - 1) * P, W - 1, :]).then_inc(s_out, 16)
                s.wait_ge(s_out, 16 * (ITER + 1))

            @block.tensor
            def _(t):
                t.wait_ge(s_w, 16 * (1 + 2 * E1))
                with t.Fori(0, ITER) as i:
                    def hidden(e):
                        for fb in range(HB):
                            for h in range(2):
                                n = 2 * fb + h
                                t.wait_ge(s_g, STEPS * E1 * i + max(STEPS * e + n - 3, 0))
                                for c in range(C):
                                    mm = t.matmul(ph[:, n % 4, 0:HALF], w1[:, e, c, fb * P:(fb + 1) * P],
                                                  R.XT[:, c, bass.ds(i * TOK + h * HALF, HALF)], start=(c == 0),
                                                  stop=(c == C - 1))
                                mm.then_inc(s_h, 1)

                    hidden(0)
                    for e in range(E1):
                        if e + 1 < E1:
                            hidden(e + 1)
                        t.wait_ge(s_g, STEPS * E1 * i + STEPS * (e + 1))
                        for j in range(TPI):
                            n = TPI * e + j
                            t.wait_ge(s_a, TPI * E1 * i + max(n - 3, 0))
                            for c in range(HB):
                                mm = t.matmul(po[:, n % 4, 0:D], hid[:, e % 2, c, j * P:(j + 1) * P], w2[:, e, c, :],
                                              start=(c == 0), stop=(c == HB - 1))
                            mm.then_inc(s_o, 1)

            @block.scalar
            def _(a):
                with a.Fori(0, ITER) as i:
                    for e in range(E1):
                        a.wait_ge(s_o, TPI * E1 * i + TPI * max(e - 1, 0))
                        for fb in range(HB):
                            for h in range(2):
                                n = 2 * fb + h
                                a.wait_ge(s_h, STEPS * (E1 * i + e) + n + 1)
                                a.activation(hid[:, e % 2, fb, h * HALF:(h + 1) * HALF], ph[:, n % 4, 0:HALF],
                                             ACT.Gelu, bias=b1[:, e, fb:fb + 1]).then_inc(s_g, 1)

            @block.vector
            def _(v):
                with v.Fori(0, ITER) as i:
                    for e in range(E1):
                        for j in range(TPI):
                            n = TPI * e + j
                            v.wait_ge(s_o, TPI * E1 * i + n + 1)
                            v.wait_ge(s_a, TPI * E1 * i + max(n - 6, 0))
                            xj = xtile(R, TPI * i + j)
                            g = R.gate[:, bass.ds(TPI * i + j, 1), e:e + 1].rearrange("p a b -> p (a b)")
                            v.scalar_tensor_tensor(xj, po[:, n % 4, 0:D], g, xj, ALU.mult, ALU.add).then_inc(s_a, 1)



class Shared:
    pass


def build(nc, A, out):
    R = Shared()
    R.tab0 = nc.dram_tensor("tab0", [NP, GCN], F32).ap()
    R.tab1 = nc.dram_tensor("tab1", [NP, GROW], F32).ap()
    R.tabr = nc.dram_tensor("tabr", [NP, FROW], F32).ap()
    R.fsorted = nc.dram_tensor("fsorted", [FE, 2], I32).ap()
    R.wdram = nc.dram_tensor("wdram", [16 * P], I32).ap()
    GT, FT = -(-(GSLOTS + TURN) // P) * P, -(-(FSLOTS + TURN) // P) * P
    with Phase(nc, "all") as f:
        R.ident = f.sb("ident", [P, P])
        R.iota = f.sb("iota", [P, P])
        R.ones = f.sb("ones", [P, P])
        R.mask = f.sb("mask", [P, W])
        R.X = f.sb("X", [P, W, D])
        R.XT = f.sb("XT", [P, C, NP])
        R.weff = f.sb("weff", [P, C, D])
        R.beff = f.sb("beff", [P, C])
        R.kvsum = f.sb("kvsum", [P, 512])
        R.fstart = f.sb("fstart", [P, W])
        R.gmax = f.sb("gmax", [P, GH])
        R.gmaxa = f.sb("gmaxa", [P, GH])
        R.gate = f.sb("gate", [P, W, E0])
        constants(nc, R)
        with Phase(nc, "graph") as g:
            R.gstart = g.sb("gstart", [P, W])
            R.nsrc = g.sb("nsrc", [P, W])
            R.adst = g.sb("adst", [P, W, GH])
            R.gsrc = g.sb("gsrc", [P, GT])
            R.gdst = g.sb("gdst", [P, GT])
            R.gwin = g.sb("gwin", [1, GT], I32)
            R.gwinn = g.sb("gwinn", [1, GT], I32)
            with Phase(nc, "fedge") as fe:
                R.frec = fe.sb("frec", [P, FB, 2], I32)
                R.fpos = fe.sb("fpos", [P, FB])
                place_edges(nc, R, A)
                degrees(nc, R, A)
                slot_tables(nc, R, "gslot", R.gstart, A.grec, GB, GT, R.gsrc, R.gdst, R.gwin, R.gwinn)
                kv_phase(nc, R, A, 0)
                fold0(nc, R, A)
                mixer0(nc, R, A)
                with Phase(nc, "gcn") as h:
                    R.gcn = h.sb("sum", [P, W, GCN + 1])
                    clear(nc, R.gcn[:, :, :])
                    edges(nc, R, "gcne", R.tab0, GSLOTS, R.gsrc, R.gdst, R.gwin, R.gwinn, R.gcn)
                    gcn_finish(nc, R, A)
                gates0(nc, R, A)
                experts0(nc, R, A)
            kv_phase(nc, R, A, 1)
            fold1(nc, R, A)
            with Phase(nc, "gat") as h:
                R.gat = h.sb("sum", [P, W, GROW])
                loops(nc, R, "gloop", R.tab1, R.gat, GH, GC, R.adst, R.gmaxa)
                edges(nc, R, "gate", R.tab1, GSLOTS, R.gsrc, R.gdst, R.gwin, R.gwinn, R.gat, GH, GC, R.adst, R.gmaxa)
                finish1(nc, R, A)
        with Phase(nc, "router") as g:
            R.rsrc = g.sb("rsrc", [P, FT])
            R.rdrel = g.sb("rdrel", [P, FT])
            R.rwin = g.sb("rwin", [1, FT], I32)
            R.rwinn = g.sb("rwinn", [1, FT], I32)
            R.rext = g.sb("rext", [P, W, FROW + FH])
            R.rdst = g.sb("rdst", [P, W, FH])
            R.rmax = g.sb("rmax", [P, FH])
            R.racc = g.sb("racc", [P, W, FROW])
            router_table(nc, R, A)
            slot_tables(nc, R, "fslot", R.fstart, R.fsorted.rearrange("(b e) k -> b (e k)", e=P), FB, FT, R.rsrc,
                        R.rdrel, R.rwin, R.rwinn)
            loops(nc, R, "rloop", R.tabr, R.racc, FH, FC, R.rdst, R.rmax)
            edges(nc, R, "rtr", R.tabr, FSLOTS, R.rsrc, R.rdrel, R.rwin, R.rwinn, R.racc, FH, FC, R.rdst, R.rmax)
            router_gates(nc, R, A)
            experts1(nc, R, A, out)


def kernel(**inputs):
    import numpy as np
    import concourse.bacc as bacc
    from concourse.bass_utils import run_bass_kernel_spmd as run

    g = {k: np.asarray(v) for k, v in inputs.items()}
    pad = np.full(GB * P - GE, PAD_NODE, np.int32)
    src, dst = np.concatenate([g["src"], pad]), np.concatenate([g["dst"], pad])
    qkv0 = g["L0_mix_w_qkv"].reshape(D, HEADS, 3, HC0)
    bqkv0 = g["L0_mix_b_qkv"].reshape(HEADS, 3, HC0)
    qkv1 = g["L1_mix_w_qkv"]
    inner = HEADS * HC1

    def cols(b):
        return b.reshape(-1, P).T

    bn = [[g[f"L0_ffn_{n}{k}"].reshape(E0 * C, P).T for n in ("b", "g", "be", "m", "v")] for k in (1, 2)]
    given = dict(
        x=g["x"],
        gsrc_t=src.reshape(GB, P).T, gdst_t=dst.reshape(GB, P).T,
        grec=np.stack([src, dst], -1).reshape(GB, 2 * P),
        ffn_edges=g["L1_ffn_edge_index"].T.reshape(P, FB, 2),
        gcn_w=g["L0_gnn_W_gcn"], gcn_b=g["L0_gnn_b_gcn"], gcn_wout=g["L0_gnn_W_out"], gcn_bout=g["L0_gnn_b_out"][None],
        m0_kv=np.concatenate([qkv0[:, :, 1].reshape(D, D), qkv0[:, :, 2].reshape(D, D)], 1),
        m0_wqt=qkv0[:, :, 0].reshape(D, D).T,
        m0_bkv=np.concatenate([bqkv0[:, 1].reshape(D), bqkv0[:, 2].reshape(D)]),
        m0_bq_t=cols(bqkv0[:, 0].reshape(D)),
        m0_gam=np.stack([g["L0_mix_kln_g"], g["L0_mix_vln_g"]]), m0_bet=np.stack([g["L0_mix_kln_b"], g["L0_mix_vln_b"]]),
        m0_w1=g["L0_mix_w1"], m0_b1_t=cols(g["L0_mix_b1"]), m0_w2=g["L0_mix_w2"], m0_b2=g["L0_mix_b2"][None],
        f0_wr=g["L0_ffn_Wr"], f0_br=g["L0_ffn_br"], f0_w1=g["L0_ffn_W1"], f0_w2=g["L0_ffn_W2"], f0_wo=g["L0_ffn_Wo"],
        f0_bo=g["L0_ffn_bo"], f0_bn=np.stack([np.stack(k, 1) for k in bn], 1),
        gat_w=g["L1_gnn_W"], gat_src=g["L1_gnn_att_src"].reshape(-1), gat_dst=g["L1_gnn_att_dst"].reshape(-1),
        gat_bias=g["L1_gnn_bias"][None],
        m1_kv=qkv1[:, inner:], m1_wqt=qkv1[:, :inner].T, m1_wout=g["L1_mix_w_out"], m1_bout=g["L1_mix_b_out"][None],
        r_w=g["L1_ffn_W_gat"], r_src=g["L1_ffn_att_src"].reshape(-1), r_dst=g["L1_ffn_att_dst"].reshape(-1),
        r_b=g["L1_ffn_b_gat"], r_gam=g["L1_ffn_ln_gamma"], r_bet=g["L1_ffn_ln_beta"],
        f1_w1=g["L1_ffn_W1"], f1_b1=g["L1_ffn_b1"].reshape(E1, -1, P).transpose(2, 0, 1), f1_w2=g["L1_ffn_W2"],
        f1_b2=g["L1_ffn_b2"],
    )
    nc = bacc.Bacc("TRN2", target_bir_lowering=False, num_devices=1)
    arrays, A = {}, Shared()
    for name, a in given.items():
        a = np.ascontiguousarray(a)
        arrays[f"in_{name}"] = a
        A.__dict__[name] = nc.dram_tensor(f"in_{name}", a.shape, mybir.dt.from_np(a.dtype), kind="ExternalInput").ap()
    out = nc.dram_tensor("out", [N, D], F32, kind="ExternalOutput").ap()
    build(nc, A, out)
    r = run(nc, [arrays], core_ids=[0])
    return r.results[0]["out"]
```

```python
from contextlib import ExitStack

import concourse.bass as bass
from concourse import mybir

F32 = mybir.dt.float32
BF16 = mybir.dt.bfloat16
I32 = mybir.dt.int32
U32 = mybir.dt.uint32
ALU = mybir.AluOpType
ACT = mybir.ActivationFunctionType
AXX = mybir.AxisListType.X
ENG = mybir.EngineType

P = 128
N = 6250
D = 256
C = D // P
W = -(-N // P)
NP = W * P
TPI = 7
ITER = W // TPI
TOK = TPI * P
HALF = TOK // 2
assert W % TPI == 0 and HALF <= 512

HEADS = 8
HC0 = 32
HC1 = 64
GCN = 64
GH, GC = 8, 32
GROW = GH * GC + GH
E0, E1 = 8, 4
HID1 = 512
FH, FC = 4, 4
FROW = FH * FC + FH
LN_EPS = 1e-5
BN_EPS = 1e-3

GE = 50000 * 2 + N
GB = 832
FE = 131072
FB = FE // P
PAD_NODE = 8192
GROUP = 4
NBUF = 4
TURN = NBUF * GROUP
GROUP8 = 8
GSLOTS = -(-(GB + W - 1) // TURN) * TURN
FSLOTS = -(-(FB + W - 1) // TURN) * TURN
assert GB * P >= GE


class Phase:

    def __init__(self, nc, tag):
        self.nc, self.tag, self.ctx, self.sems = nc, tag, ExitStack(), []

    def __enter__(self):
        return self

    def __exit__(self, *a):
        if self.sems:
            self.nc.clear_and_free_semaphores(self.sems)
            self.nc.all_engine_barrier()
        self.ctx.close()

    def sb(self, name, shape, dt=F32):
        return self.ctx.enter_context(self.nc.sbuf_tensor(f"{self.tag}_{name}", shape, dt))

    def ps(self, name, shape, dt=F32):
        return self.ctx.enter_context(self.nc.psum_tensor(f"{self.tag}_{name}", shape, dt))

    def sem(self, name):
        self.sems.append(self.nc.alloc_semaphore(f"{self.tag}_{name}"))
        return self.sems[-1]


class Steps:

    def __init__(self, eng, sem, start=0):
        self.eng, self.sem, self.n = eng, sem, start

    def then(self, ins):
        ins.then_inc(self.sem, 1)
        self.n += 1
        self.eng.wait_ge(self.sem, self.n)


def rows(ap):
    return ap.rearrange("(c p) n -> p c n", p=P)


def spread(ap, n=P):
    return ap.partition_broadcast(n)



def constants(nc, R):
    with Phase(nc, "cst") as f:
        made = f.sem("made")
        row_i = f.sb("row_i", [P, P], I32)
        with nc.Block() as block:
            @block.gpsimd
            def _(g):
                st = Steps(g, made)
                st.then(g.memset(R.ident[:, :], 0.0))
                st.then(g.affine_select(out=R.ident[:, :], in_=R.ident[:, :], compare_op=ALU.not_equal, fill=1.0,
                                        base=0, pattern=[[-1, P]], channel_multiplier=1))
                st.then(g.tensor_copy(R.identb[:, :], R.ident[:, :]))
                st.then(g.iota(row_i[:, :], pattern=[[1, P]], base=0, channel_multiplier=0))
                st.then(g.tensor_copy(R.iota[:, :], row_i[:, :]))
                st.then(g.memset(R.ones[:, :], 1.0))
                st.then(g.memset(R.mask[:, :], 1.0))
                st.then(g.affine_select(out=R.mask[:, W - 1:W], in_=R.mask[:, W - 1:W], compare_op=ALU.is_ge, fill=0.0,
                                        base=N - (W - 1) * P - 1, pattern=[[0, 1]], channel_multiplier=-1))



def degrees(nc, R, A):
    BAT = 16
    TURNS = GB // (2 * BAT)
    with Phase(nc, "deg") as f:
        si = f.sb("si", [P, GB], I32)
        di = f.sb("di", [P, GB], I32)
        part = f.sb("part", [P, GB], I32)
        lo = f.sb("lo", [P, GB])
        hi = f.sb("hi", [P, GB])
        dstf = f.sb("dstf", [P, GB])
        junk = f.sb("junk", [P, GB])
        cnt = f.sb("cnt", [P, W])
        ohlo = f.sb("ohlo", [P, 2, BAT, P], BF16)
        ohhi = f.sb("ohhi", [P, 2, BAT, W], BF16)
        deg = f.ps("deg", [P, 512])
        total = f.ps("total", [P, 512])
        zero = f.sb("zero", [P, P], BF16)
        loaded, step, hot, used, zeroed, counted, summed, rooted = (
            f.sem(n) for n in ("loaded", "step", "hot", "used", "zeroed", "counted", "summed", "rooted"))
        std = f.sb("std", [P, W])
        with nc.Block() as block:
            @block.sync
            def _(s):
                s.dma_start(si[:, :], A.gsrc_t).then_inc(loaded, 16)
                s.dma_start(di[:, :], A.gdst_t).then_inc(loaded, 16)

            @block.vector
            def _(v):
                st = Steps(v, step)
                v.memset(zero[:, :], 0.0).then_inc(zeroed, 1)
                v.wait_ge(loaded, 32)
                st.then(v.tensor_scalar(part[:, :], si[:, :], P - 1, None, ALU.bitwise_and))
                st.then(v.tensor_copy(lo[:, :], part[:, :]))
                st.then(v.tensor_scalar(part[:, :], si[:, :], 7, None, ALU.arith_shift_right))
                st.then(v.tensor_copy(hi[:, :], part[:, :]))
                st.then(v.tensor_copy(dstf[:, :], di[:, :]))
                with v.Fori(0, TURNS) as i:
                    for g in range(2):
                        v.wait_ge(used, 2 * i)
                        col = (2 * i + g) * BAT
                        v.tensor_tensor(ohlo[:, g], R.iota[:, :].unsqueeze(1).to_broadcast([P, BAT, P]),
                                        lo[:, bass.ds(col, BAT)].unsqueeze(2).to_broadcast([P, BAT, P]),
                                        ALU.is_equal).then_inc(hot, 1)
                        v.tensor_tensor(ohhi[:, g], R.iota[:, 0:W].unsqueeze(1).to_broadcast([P, BAT, W]),
                                        hi[:, bass.ds(col, BAT)].unsqueeze(2).to_broadcast([P, BAT, W]),
                                        ALU.is_equal).then_inc(hot, 1)
                for w in range(W):
                    st.then(v.tensor_scalar(junk[:, :], dstf[:, :], float(P * w), None, ALU.is_lt, ALU.add,
                                            accum_out=cnt[:, w:w + 1]))
                v.sem_inc(counted, 1)
                v.wait_ge(summed, 1)
                st.then(v.tensor_copy(R.gstart[:, :], total[:, 0:W]))
                st.then(v.tensor_scalar(std[:, :], deg[:, 0:W], 1.0, None, ALU.max))
                v.sem_inc(counted, 1)
                v.wait_ge(rooted, 1)
                v.reciprocal(R.nsrc[:, :], std[:, :])

            @block.scalar
            def _(a):
                a.wait_ge(counted, 2)
                a.activation(std[:, :], std[:, :], ACT.Sqrt).then_inc(rooted, 1)

            @block.tensor
            def _(t):
                t.wait_ge(zeroed, 1)
                t.matmul(deg[:, 0:W], zero[:, :], zero[:, 0:W], start=True, stop=False, skip_group_check=True)
                with t.Fori(0, TURNS) as i:
                    for g in range(2):
                        t.wait_ge(hot, 4 * i + 2 * g + 2)
                        for b in range(BAT):
                            mm = t.matmul(deg[:, 0:W], ohlo[:, g, b, :], ohhi[:, g, b, :], start=False, stop=False,
                                          skip_group_check=True)
                        mm.then_inc(used, 1)
                t.wait_ge(counted, 1)
                t.matmul(total[:, 0:W], R.ones[:, :], cnt[:, :], start=True, stop=True).then_inc(summed, 1)



def slot_tables(nc, R, tag, start, rec, nblocks, nslots, src_ix, dst_rel, wtab, wnext):
    J = -(-nslots // P)
    with Phase(nc, tag) as f:
        si = f.sb("si", [P, W], I32)
        sf = f.sb("sf", [P, W])
        iw = f.sb("iw", [P, W], I32)
        slot_i = f.sb("slot_i", [P, J], I32)
        slot = f.sb("slot", [P, J])
        cmp = f.sb("cmp", [P, J, W - 1])
        win = f.sb("win", [P, J])
        blk = f.sb("blk", [P, J])
        off = f.sb("off", [P, J])
        blk_i = f.sb("blk_i", [P, J], U32)
        win_i = f.sb("win_i", [P, J], I32)
        edge = f.sb("edge", [P, J, P, 2], I32)
        srcf = f.sb("srcf", [P, J, P])
        dstf = f.sb("dstf", [P, J, P])
        pt = f.ps("pt", [P, 4, 512])
        made, step, tabbed, gathered, split, turned, put, wout, win_done = (
            f.sem(n) for n in ("made", "step", "tabbed", "gathered", "split", "turned", "put", "wout", "win_done"))
        gath = [f.sem(f"gath{j}") for j in range(J)]
        with nc.Block() as block:
            @block.gpsimd
            def _(g):
                g.iota(slot_i[:, :], pattern=[[P, J]], base=0, channel_multiplier=1).then_inc(made, 1)
                g.iota(iw[:, :], pattern=[[1, W]], base=0, channel_multiplier=0).then_inc(made, 1)
                g.wait_ge(tabbed, 1)
                for j in range(J):
                    g.indirect_dma_start(edge[:, j].rearrange("p e k -> p (e k)"), None, rec,
                                         bass.IndirectOffsetOnAxis(blk_i[:, j:j + 1], 0)).then_inc(gath[j], 16)

            @block.vector
            def _(v):
                st = Steps(v, step)
                v.wait_ge(made, 2)
                st.then(v.tensor_copy(slot[:, :], slot_i[:, :]))
                st.then(v.tensor_copy(si[:, :], start[:, :]))
                st.then(v.tensor_scalar(si[:, :], si[:, :], 7, None, ALU.arith_shift_right))
                st.then(v.tensor_tensor(sf[:, :], si[:, :], iw[:, :], ALU.add))
                st.then(v.tensor_tensor(cmp[:, :, :], sf[:, 1:W].unsqueeze(1).to_broadcast([P, J, W - 1]),
                                        slot[:, :].unsqueeze(2).to_broadcast([P, J, W - 1]), ALU.is_le))
                st.then(v.tensor_reduce(win[:, :], cmp[:, :, :], AXX, ALU.add))
                st.then(v.tensor_tensor(blk[:, :], slot[:, :], win[:, :], ALU.subtract))
                st.then(v.tensor_scalar(blk_i[:, :], blk[:, :], float(nblocks - 1), None, ALU.min))
                st.then(v.tensor_copy(win_i[:, :], win[:, :]))
                st.then(v.tensor_scalar(off[:, :], blk[:, :], float(nblocks), -float(1 << 22), ALU.is_ge, ALU.mult))
                st.then(v.scalar_tensor_tensor(off[:, :], win[:, :], float(P), off[:, :], ALU.mult, ALU.add))
                v.sem_inc(tabbed, 1)
                for j in range(J):
                    v.wait_ge(gath[j], 16)
                    v.tensor_scalar(srcf[:, j], edge[:, j, :, 0], float(N - 1), None, ALU.min).then_inc(split, 1)
                    v.tensor_scalar(dstf[:, j], edge[:, j, :, 1], off[:, j:j + 1], None,
                                    ALU.subtract).then_inc(split, 1)
                for j in range(J):
                    v.wait_ge(turned, j + 1)
                    v.tensor_copy(src_ix[:, j * P:(j + 1) * P], pt[:, 2 * (j % 2), 0:P]).then_inc(put, 1)
                    v.tensor_copy(dst_rel[:, j * P:(j + 1) * P], pt[:, 2 * (j % 2) + 1, 0:P]).then_inc(put, 1)

            @block.tensor
            def _(t):
                for j in range(J):
                    t.wait_ge(split, 2 * (j + 1))
                    if j >= 2:
                        t.wait_ge(put, 2 * (j - 1))
                    t.transpose(pt[:, 2 * (j % 2), 0:P], srcf[:, j], R.ident[:, :])
                    t.transpose(pt[:, 2 * (j % 2) + 1, 0:P], dstf[:, j], R.ident[:, :]).then_inc(turned, 1)

            @block.sync
            def _(s):
                s.wait_ge(tabbed, 1)
                with nc.allow_non_contiguous_dma(reason="one number per slot, once"):
                    s.dma_start(R.wdram[0:J * P].rearrange("(j p) -> p j", p=P), win_i[:, :]).then_inc(wout, 16)
                s.wait_ge(wout, 16)
                s.dma_start(wtab[0:1, :], R.wdram[0:J * P].unsqueeze(0)).then_inc(wout, 16)
                s.dma_start(wnext[0:1, 0:J * P - 2 * GROUP], R.wdram[2 * GROUP:J * P].unsqueeze(0)).then_inc(wout, 16)
                s.wait_ge(wout, 48)



class Norm:

    def __init__(self, f, R):
        self.R = R
        self.stats = f.sb("stats", [P, TPI, 6])
        self.mv = f.sb("mv", [P, TPI, 2])
        self.var = f.sb("var", [P, TPI])
        self.std = f.sb("std", [P, TPI])
        self.rstd = f.sb("rstd", [P, TPI])
        self.xn = f.sb("xn", [P, TPI, D])
        self.xt = f.sb("xt", [P, TPI, C, P])
        self.pt = f.ps("pt", [P, 2, 512])
        self.s_stat, self.s_mv, self.s_var, self.s_std, self.s_rstd = (
            f.sem(n) for n in ("stat", "mv", "var", "std", "rstd"))
        self.s_seen = f.sem("seen")
        self.s_xn, self.s_tp, self.s_xt, self.s_xr = (f.sem(n) for n in ("xn", "tp", "xt", "xr"))

    def vector(self, v, i):
        R = self.R
        for j in range(TPI):
            v.bn_stats(self.stats[:, j], R.X[:, bass.ds(TPI * i + j, 1), :].rearrange("p a d -> p (a d)")).then_inc(self.s_stat, 1)
        v.wait_ge(self.s_stat, TPI * i + TPI)
        v.sem_inc(self.s_seen, 1)
        for j in range(TPI):
            v.bn_aggr(self.mv[:, j], self.stats[:, j]).then_inc(self.s_mv, 1)
        v.wait_ge(self.s_mv, TPI * i + TPI)
        v.tensor_scalar(self.var[:, :], self.mv[:, :, 1], LN_EPS, None, ALU.add).then_inc(self.s_var, 1)
        v.wait_ge(self.s_std, i + 1)
        v.reciprocal(self.rstd[:, :], self.std[:, :]).then_inc(self.s_rstd, 1)
        v.wait_ge(self.s_rstd, i + 1)
        v.wait_ge(self.s_tp, TPI * i)
        for j in range(TPI):
            v.tensor_scalar(self.xn[:, j], R.X[:, bass.ds(TPI * i + j, 1), :].rearrange("p a d -> p (a d)"),
                            self.mv[:, j, 0:1], self.rstd[:, j:j + 1], ALU.subtract, ALU.mult).then_inc(self.s_xn, 1)

    def scalar_root(self, a, i):
        a.wait_ge(self.s_var, i + 1)
        a.activation(self.std[:, :], self.var[:, :], ACT.Sqrt).then_inc(self.s_std, 1)

    def scalar_copy(self, a, i, j):
        a.wait_ge(self.s_tp, TPI * i + j + 1)
        src = self.pt[:, j % 2, 0:C * P].rearrange("p (c t) -> p c t", c=C)
        a.activation(self.xt[:, j], src, ACT.Copy).then_inc(self.s_xt, 1)
        a.activation(self.R.XT[:, :, bass.ds((TPI * i + j) * P, P)], src, ACT.Copy).then_inc(self.s_xr, 1)

    def tensor(self, t, i, j):
        t.wait_ge(self.s_xn, TPI * i + j + 1)
        t.wait_ge(self.s_xr, TPI * i + (j - 1 if j >= 2 else 0))
        for c in range(C):
            mm = t.transpose(self.pt[:, j % 2, c * P:(c + 1) * P], self.xn[:, j, c * P:(c + 1) * P], self.R.ident[:, :])
        mm.then_inc(self.s_tp, 1)


def kv_phase(nc, R, A, L):
    first = L == 0
    hd = HC0 if first else HC1
    G = 2 * HEADS
    KV = G * hd
    NB_KV = KV // 512
    EXT = GCN if first else GH * GC + 2 * GH
    TAB = GCN if first else GROW
    PAIRS = KV // 2 // P
    wkv_d, ext_d, tab_d = (A.m0_kv, A.gcn_w, R.tab0) if first else (A.m1_kv, A.gat_w, R.tab1)
    with Phase(nc, f"kv{L}") as f:
        nm = Norm(f, R)
        wkv = f.sb("wkv", [P, C, KV])
        wext = f.sb("wext", [P, C, EXT])
        gsum = f.sb("gsum", [P, C, G])
        kc = f.sb("kc", [P, TPI, KV])
        sq = f.sb("sq", [P, KV])
        ssum = f.sb("ssum", [P, TPI, G])
        sstd = f.sb("sstd", [P, TPI, G])
        srs = f.sb("srs", [P, TPI, G])
        ext = f.sb("ext", [P, TPI, EXT])
        tabt = f.sb("tabt", [P, TPI, TAB])
        zero = f.sb("zero", [P, 512], BF16)
        if first:
            bias = f.sb("bias", [P, KV])
            bsum = f.sb("bsum", [P, G])
            gam = f.sb("gam", [P, KV])
            bet = f.sb("bet", [P, KV])
        else:
            att = f.sb("att", [P, 2, GH * GC])
            wa = f.sb("wa", [P, GH * GC])
        pkv = f.ps("pkv", [P, 4 // NB_KV if NB_KV > 1 else 2, NB_KV, 512])
        pext = f.ps("pext", [P, 512])
        pacc = f.ps("pacc", [P, 512])
        s_w, s_st, s_z, s_ready, s_x = (f.sem(n) for n in ("w", "st", "z", "ready", "x"))
        s_kvp, s_kc, s_sq, s_red, s_ve, s_sd, s_r2, s_rm = (
            f.sem(n) for n in ("kvp", "kc", "sq", "red", "ve", "sd", "r2", "rm"))
        s_k1, s_k2, s_k3, s_kv, s_ep, s_ec, s_tab, s_tab_d, s_out, s_acc, s_gm = (
            f.sem(n) for n in ("k1", "k2", "k3", "kv", "ep", "ec", "tab", "tabd", "out", "acc", "gm"))
        s_xa = f.sem("xa")
        s_kdone = s_k3 if first else s_k1
        loads = 6 if first else 4
        with nc.Block() as block:
            @block.sync
            def _(s):
                s.dma_start(wkv[:, :, :], rows(wkv_d)).then_inc(s_w, 16)
                s.dma_start(wext[:, :, 0:ext_d.shape[1]], rows(ext_d)).then_inc(s_w, 16)
                if first:
                    s.dma_start(bias[:, :], spread(A.m0_bkv)).then_inc(s_w, 16)
                    for tile, row in ((gam, A.m0_gam), (bet, A.m0_bet)):
                        for k in range(2):
                            s.dma_start(tile[:, k * KV // 2:k * KV // 2 + hd], spread(row[k])).then_inc(s_w, 16)
                    s.wait_ge(s_z, 2)
                    full = W - 1
                    s.dma_start(R.X[:, 0:full, :], A.x[0:full * P, :].rearrange("(t p) d -> p t d", p=P))\
                        .then_inc(s_x, 16)
                    s.dma_start(R.X[0:N - full * P, full, :], A.x[full * P:N, :]).then_inc(s_x, 16)
                else:
                    for k, row in enumerate((A.gat_src, A.gat_dst)):
                        s.dma_start(att[:, k, :], spread(row)).then_inc(s_w, 16)
                with s.Fori(0, ITER) as i:
                    s.wait_ge(s_tab, i + 1)
                    s.dma_start(tab_d[bass.ds(i * TOK, TOK), :].rearrange("(t p) d -> p t d", p=P), tabt[:, :, :])\
                        .then_inc(s_out, 16)
                s.wait_ge(s_out, 16 * ITER)

            if first:
                @block.gpsimd
                def _(g):
                    with g.Fori(0, ITER) as i:
                        for j in range(TPI):
                            g.wait_ge(nm.s_xn, TPI * i + j + 1)
                            xj = R.X[:, bass.ds(TPI * i + j, 1), :].rearrange("p a d -> p (a d)")
                            g.tensor_tensor(xj, xj, nm.xn[:, j], ALU.add).then_inc(s_xa, 1)

            @block.vector
            def _(v):
                st = Steps(v, s_st)
                v.memset(zero[:, :], 0.0).then_inc(s_z, 1)
                if first:
                    v.memset(R.X[:, W - 1, :], 0.0).then_inc(s_z, 1)
                v.wait_ge(s_w, 16 * (7 if first else 4))
                if first:
                    for tile in (gam, bet):
                        for k in range(2):
                            o = k * KV // 2
                            for m in (1, 2, 4):
                                st.then(v.tensor_copy(tile[:, o + m * hd:o + 2 * m * hd], tile[:, o:o + m * hd]))
                for c in range(C):
                    v3 = wkv[:, c, :].rearrange("p (g e) -> p g e", g=G)
                    st.then(v.tensor_reduce(gsum[:, c, :], v3, AXX, ALU.add))
                    st.then(v.tensor_scalar(gsum[:, c, :], gsum[:, c, :], 1.0 / hd, None, ALU.mult))
                    st.then(v.tensor_tensor(v3, v3, gsum[:, c, :].unsqueeze(2).to_broadcast([P, G, hd]), ALU.subtract))
                if first:
                    b3 = bias[:, :].rearrange("p (g e) -> p g e", g=G)
                    st.then(v.tensor_reduce(bsum[:, :], b3, AXX, ALU.add))
                    st.then(v.tensor_scalar(bsum[:, :], bsum[:, :], 1.0 / hd, None, ALU.mult))
                    st.then(v.tensor_tensor(b3, b3, bsum[:, :].unsqueeze(2).to_broadcast([P, G, hd]), ALU.subtract))
                    v.wait_ge(s_x, 32)
                else:
                    for c in range(C):
                        for k in range(2):
                            st.then(v.tensor_tensor(wa[:, :], wext[:, c, 0:GH * GC], att[:, k, :], ALU.mult))
                            o = GH * GC + k * GH
                            st.then(v.tensor_reduce(wext[:, c, o:o + GH],
                                                    wa[:, :].rearrange("p (h c) -> p h c", h=GH), AXX, ALU.add))
                    st.then(v.memset(R.gmax[:, :], -3.0e38))
                v.sem_inc(s_ready, 1)
                with v.Fori(0, ITER) as i:
                    if first:
                        v.wait_ge(s_xa, TPI * i)
                    nm.vector(v, i)
                    v.wait_ge(s_kv, i)
                    for j in range(TPI):
                        v.wait_ge(s_kvp, TPI * i + j + 1)
                        src = pkv[:, j % 2].rearrange("p b n -> p (b n)")
                        if first:
                            v.tensor_tensor(kc[:, j], src, bias[:, :], ALU.add).then_inc(s_kc, 1)
                        else:
                            v.tensor_copy(kc[:, j], src).then_inc(s_kc, 1)
                        v.wait_ge(s_sq, TPI * i + j + 1)
                        v.tensor_reduce(ssum[:, j], sq[:, :].rearrange("p (g e) -> p g e", g=G), AXX,
                                        ALU.add).then_inc(s_red, 1)
                    v.wait_ge(s_red, TPI * i + TPI)
                    v.tensor_scalar(ssum[:, :, :], ssum[:, :, :], 1.0 / hd, LN_EPS, ALU.mult,
                                    ALU.add).then_inc(s_ve, 1)
                    v.wait_ge(s_sd, i + 1)
                    v.reciprocal(srs[:, :, :], sstd[:, :, :]).then_inc(s_r2, 1)
                    v.wait_ge(s_r2, i + 1)
                    v.tensor_tensor(srs[:, :, :], srs[:, :, :],
                                    R.mask[:, bass.ds(TPI * i, TPI)].unsqueeze(2).to_broadcast([P, TPI, G]),
                                    ALU.mult).then_inc(s_rm, 1)
                    v.wait_ge(s_rm, i + 1)
                    for j in range(TPI):
                        k3 = kc[:, j].rearrange("p (g e) -> p g e", g=G)
                        v.tensor_tensor(k3, k3, srs[:, j].unsqueeze(2).to_broadcast([P, G, hd]),
                                        ALU.mult).then_inc(s_k1, 1)
                        if first:
                            v.wait_ge(s_k1, TPI * i + j + 1)
                            v.tensor_tensor(kc[:, j], kc[:, j], gam[:, :], ALU.mult).then_inc(s_k2, 1)
                            v.wait_ge(s_k2, TPI * i + j + 1)
                            v.scalar_tensor_tensor(kc[:, j], bet[:, :], R.mask[:, bass.ds(TPI * i + j, 1)],
                                                   kc[:, j], ALU.mult, ALU.add).then_inc(s_k3, 1)
                    v.wait_ge(s_ec, TPI * i + TPI)
                    v.wait_ge(s_out, 16 * i)
                    if first:
                        v.tensor_tensor(tabt[:, :, :], ext[:, :, :],
                                        R.nsrc[:, bass.ds(TPI * i, TPI)].unsqueeze(2).to_broadcast([P, TPI, GCN]),
                                        ALU.mult).then_inc(s_tab, 1)
                    else:
                        v.tensor_copy(tabt[:, :, :], ext[:, :, 0:TAB]).then_inc(s_tab, 1)
                        v.tensor_copy(R.adst[:, bass.ds(TPI * i, TPI), :], ext[:, :, TAB:EXT]).then_inc(s_tab_d, 1)
                        for j in range(TPI):
                            v.tensor_tensor(R.gmax[:, :], R.gmax[:, :], ext[:, j, GH * GC:TAB],
                                            ALU.max).then_inc(s_gm, 1)
                            v.wait_ge(s_gm, TPI * i + j + 1)
                v.wait_ge(s_acc, 1)
                v.tensor_copy(R.kvsum[:, 0:PAIRS * P], pacc[:, 0:PAIRS * P])

            def evac(a, i, j):
                a.wait_ge(s_ep, TPI * i + j + 1)
                a.activation(ext[:, j], pext[:, 0:EXT], ACT.Copy).then_inc(s_ec, 1)
                a.wait_ge(s_kc, TPI * i + j + 1)
                a.wait_ge(s_red, TPI * i + j)
                a.activation(sq[:, :], kc[:, j], ACT.Square).then_inc(s_sq, 1)

            @block.scalar
            def _(a):
                with a.Fori(0, ITER) as i:
                    nm.scalar_root(a, i)
                    for j in range(TPI):
                        if j == 0:
                            a.wait_ge(s_ep, TPI * i)
                            a.wait_ge(s_tab, i)
                            if not first:
                                a.wait_ge(s_gm, TPI * i)
                                a.wait_ge(s_tab_d, i)
                        nm.scalar_copy(a, i, j)
                        if j >= 1:
                            evac(a, i, j - 1)
                    evac(a, i, TPI - 1)
                    a.wait_ge(s_ve, i + 1)
                    a.activation(sstd[:, :, :], ssum[:, :, :], ACT.Sqrt).then_inc(s_sd, 1)

            @block.tensor
            def _(t):
                t.wait_ge(s_z, 1)
                t.matmul(pacc[:, 0:PAIRS * P], zero[:, 0:P], zero[:, 0:PAIRS * P], start=True, stop=False, skip_group_check=True)
                t.wait_ge(s_ready, 1)
                with t.Fori(0, ITER) as i:
                    nm.tensor(t, i, 0)
                    for j in range(TPI):
                        if j + 1 < TPI:
                            nm.tensor(t, i, j + 1)
                        t.wait_ge(nm.s_xt, TPI * i + j + 1)
                        t.wait_ge(s_kc, TPI * i + (j - 1 if j >= 2 else 0))
                        for b in range(NB_KV):
                            for c in range(C):
                                mm = t.matmul(pkv[:, j % 2, b], nm.xt[:, j, c], wkv[:, c, b * 512:(b + 1) * 512],
                                              start=(c == 0), stop=(c == C - 1))
                        mm.then_inc(s_kvp, 1)
                        t.wait_ge(s_ec, TPI * i + j)
                        for c in range(C):
                            mm = t.matmul(pext[:, 0:EXT], nm.xt[:, j, c], wext[:, c, :], start=(c == 0),
                                          stop=(c == C - 1))
                        mm.then_inc(s_ep, 1)
                    for j in range(TPI):
                        t.wait_ge(s_kdone, TPI * i + j + 1)
                        for b in range(PAIRS):
                            k = kc[:, j, b * P:(b + 1) * P]
                            u = kc[:, j, KV // 2 + b * P:KV // 2 + (b + 1) * P]
                            if not first:
                                k, u = u, k
                            mm = t.matmul(pacc[:, b * P:(b + 1) * P], k, u, start=False, stop=False,
                                          skip_group_check=True)
                    mm.then_inc(s_kv, 1)
                t.wait_ge(s_kv, ITER)
                t.sem_inc(s_acc, 1)



def block_mask(g, st, tile, width):
    st.then(g.memset(tile[:, :], 1.0))
    v = tile[:, :].rearrange("p (g e) -> p g e", e=width)
    n = P // width
    st.then(g.affine_select(out=v, in_=v, compare_op=ALU.is_ge, fill=0.0, base=0,
                            pattern=[[-width, n], [0, width]], channel_multiplier=1))
    st.then(g.affine_select(out=v, in_=v, compare_op=ALU.is_ge, fill=0.0, base=width - 1,
                            pattern=[[width, n], [0, width]], channel_multiplier=-1))


def fold0(nc, R, A):
    with Phase(nc, "fold0") as f:
        diag = f.sb("diag", [P, P])
        bd = f.sb("bd", [P, C, P])
        wqt = f.sb("wqt", [P, C, D])
        w1 = f.sb("w1", [P, C, D])
        bq = f.sb("bq", [P, C])
        b1 = f.sb("b1", [P, C])
        rwt = f.sb("rwt", [P, C, D])
        bk = f.sb("bk", [P, C])
        pr = f.ps("pr", [P, C, 512])
        pb = f.ps("pb", [P, 512])
        pw = f.ps("pw", [P, C, 512])
        loaded, made, step, masked, mixed, copied, folded = (
            f.sem(n) for n in ("loaded", "made", "step", "masked", "mixed", "copied", "folded"))
        with nc.Block() as block:
            @block.sync
            def _(s):
                s.dma_start(wqt[:, :, :], rows(A.m0_wqt)).then_inc(loaded, 16)
                s.dma_start(w1[:, :, :], rows(A.m0_w1)).then_inc(loaded, 16)
                s.dma_start(bq[:, :], A.m0_bq_t).then_inc(loaded, 16)
                s.dma_start(b1[:, :], A.m0_b1_t).then_inc(loaded, 16)

            @block.gpsimd
            def _(g):
                block_mask(g, Steps(g, made), diag, HC0)

            @block.vector
            def _(v):
                st = Steps(v, step)
                v.wait_ge(made, 3)
                for k in range(C):
                    v.scalar_tensor_tensor(bd[:, k, :], R.kvsum[:, k * P:(k + 1) * P], 1.0 / N, diag[:, :], ALU.mult,
                                           ALU.mult).then_inc(masked, 1)
                v.wait_ge(mixed, 1)
                for k in range(C):
                    st.then(v.tensor_copy(rwt[:, k, :], pr[:, k, 0:D]))
                    st.then(v.tensor_tensor(rwt[:, k, k * P:(k + 1) * P], rwt[:, k, k * P:(k + 1) * P], R.ident[:, :],
                                            ALU.add))
                st.then(v.tensor_copy(bk[:, :], pb[:, 0:C]))
                v.sem_inc(copied, 1)
                v.wait_ge(folded, 1)
                v.tensor_copy(R.weff[:, :, :], pw[:, :, 0:D])
                v.wait_ge(loaded, 64)
                v.tensor_tensor(R.beff[:, :], pb[:, 64:64 + C], b1[:, :], ALU.add)

            @block.tensor
            def _(t):
                t.wait_ge(loaded, 64)
                t.wait_ge(masked, C)
                for k in range(C):
                    t.matmul(pr[:, k, 0:D], bd[:, k, :], wqt[:, k, :], start=True, stop=True)
                for k in range(C):
                    mm = t.matmul(pb[:, k:k + 1], bd[:, k, :], bq[:, k:k + 1], start=True, stop=True)
                mm.then_inc(mixed, 1)
                t.wait_ge(copied, 1)
                for m in range(C):
                    for k in range(C):
                        t.matmul(pw[:, m, 0:D], rwt[:, k, m * P:(m + 1) * P], w1[:, k, :], start=(k == 0),
                                 stop=(k == C - 1))
                for m in range(C):
                    for k in range(C):
                        mm = t.matmul(pb[:, 64 + m:65 + m], w1[:, k, m * P:(m + 1) * P], bk[:, k:k + 1],
                                      start=(k == 0), stop=(k == C - 1))
                mm.then_inc(folded, 1)


def fold1(nc, R, A):
    K = HEADS * HC1 // P
    with Phase(nc, "fold1") as f:
        diag = f.sb("diag", [P, P])
        bd = f.sb("bd", [P, K, P])
        wqt = f.sb("wqt", [P, K, D])
        wout = f.sb("wout", [P, K, D])
        m1 = f.sb("m1", [P, K, D])
        pm = f.ps("pm", [P, K, 512])
        pw = f.ps("pw", [P, C, 512])
        loaded, made, masked, mixed, copied, folded, red = (
            f.sem(n) for n in ("loaded", "made", "masked", "mixed", "copied", "folded", "red"))
        with nc.Block() as block:
            @block.sync
            def _(s):
                s.dma_start(wqt[:, :, :], rows(A.m1_wqt)).then_inc(loaded, 16)
                s.dma_start(wout[:, :, :], rows(A.m1_wout)).then_inc(loaded, 16)

            @block.gpsimd
            def _(g):
                block_mask(g, Steps(g, made), diag, HC1)
                g.partition_all_reduce(R.gmaxa[:, :], R.gmax[:, :], P, bass.bass_isa.ReduceOp.max).then_inc(red, 1)

            @block.vector
            def _(v):
                v.wait_ge(made, 3)
                for k in range(K):
                    v.scalar_tensor_tensor(bd[:, k, :], R.kvsum[:, k * P:(k + 1) * P], 1.0 / N, diag[:, :], ALU.mult,
                                           ALU.mult).then_inc(masked, 1)
                v.wait_ge(mixed, 1)
                v.tensor_copy(m1[:, :, :], pm[:, :, 0:D]).then_inc(copied, 1)
                v.wait_ge(folded, 1)
                v.tensor_copy(R.weff[:, :, :], pw[:, :, 0:D])

            @block.tensor
            def _(t):
                t.wait_ge(loaded, 32)
                t.wait_ge(masked, K)
                for k in range(K):
                    mm = t.matmul(pm[:, k, 0:D], bd[:, k, :], wout[:, k, :], start=True, stop=True)
                mm.then_inc(mixed, 1)
                t.wait_ge(copied, 1)
                for m in range(C):
                    for k in range(K):
                        mm = t.matmul(pw[:, m, 0:D], wqt[:, k, m * P:(m + 1) * P], m1[:, k, :], start=(k == 0),
                                      stop=(k == K - 1))
                mm.then_inc(folded, 1)



def xtile(R, n):
    return R.X[:, bass.ds(n, 1), :].rearrange("p a d -> p (a d)")



class Layer0Work:
    WINS = W + 1
    HALFW = WINS // 2

    def __init__(self, nc, R, A):
        self.nc, self.R, self.A = nc, R, A

    def stages(self, Q):
        H = self.HALFW
        assert 2 * H == self.WINS and H + 1 < W < 2 * H + 1 < Q
        return [(0, H, "count mix"), (H, H + 1, "sum mix"), (H + 1, W, "rank mix"), (W, 2 * H + 1, "rank"),
                (2 * H + 1, 2 * H + 2, "end"), (2 * H + 2, Q, None)]

    def place(self, f):
        self.w2 = f.sb("w2", [P, C, D])
        self.b2 = f.sb("b2", [1, D])
        self.hid = f.sb("hid", [P, C, P])
        self.ph = f.ps("ph", [P, 512])
        self.py = f.ps("py", [P, 512])
        self.s_w, self.s_h, self.s_g, self.s_o, self.s_a = (f.sem(n) for n in ("mw", "mh", "mg", "mo", "ma"))
        self.wdst = f.sb("wdst", [P, FB], I32)
        self.win = f.sb("win", [P, FB])
        self.hit = f.sb("hit", [P, FB])
        self.rank = f.sb("rank", [P, FB])
        self.one = f.sb("one", [P, FB])
        self.pos = f.sb("pos", [P, FB])
        self.tot = f.sb("tot", [P, self.WINS])
        self.tri = f.sb("tri", [P, P])
        self.start = f.sb("start", [P, self.WINS + 1])
        self.base = f.sb("base", [P, self.WINS])
        self.scanin = f.sb("scanin", [P, self.WINS + 1])
        self.wcol = f.sb("wcol", [P, 1])
        self.bcol = f.sb("bcol", [P, 1])
        self.psum = f.ps("psum", [P, 2, 64])
        self.s_load, self.s_tri, self.s_step, self.s_cnt, self.s_rank, self.s_counted, self.s_summed, self.s_seen = (
            f.sem(n) for n in ("pload", "ptri", "pstep", "pcnt", "prank", "pcounted", "psummed", "pseen"))

    def sync(self, s):
        s.dma_start(self.R.frec[:, :, :], self.A.ffn_edges).then_inc(self.s_load, 16)
        s.dma_start(self.w2[:, :, :], rows(self.A.m0_w2)).then_inc(self.s_w, 16)
        s.dma_start(self.b2[:, :], self.A.m0_b2).then_inc(self.s_w, 16)

    def pool_start(self, g):
        g.memset(self.tri[:, :], 1.0).then_inc(self.s_tri, 1)
        g.wait_ge(self.s_tri, 1)
        g.affine_select(out=self.tri[:, :], in_=self.tri[:, :], compare_op=ALU.is_gt, fill=0.0,
                        base=0, pattern=[[1, P]], channel_multiplier=-1).then_inc(self.s_tri, 1)

    def tensor_start(self, t):
        t.sem_inc(self.s_g, 1)
        t.sem_inc(self.s_a, 1)
        t.wait_ge(self.s_w, 32)
        t.wait_ge(self.s_tri, 2)

    def vector_start(self, v):
        st = self.st = Steps(v, self.s_step)
        v.wait_ge(self.s_load, 16)
        st.then(v.tensor_scalar(self.wdst[:, :], self.R.frec[:, :, 1], 7, None, ALU.arith_shift_right))
        st.then(v.tensor_scalar(self.win[:, :], self.wdst[:, :], float(W), None, ALU.min))
        st.then(v.memset(self.one[:, :], 1.0))
        st.then(v.memset(self.pos[:, :], 0.0))

    def tensor(self, t, i, b, work):
        if "mix" in work and b == 0:
            t.wait_ge(self.s_g, i + 1)
            for fb in range(C):
                for c in range(C):
                    mm = t.matmul(self.ph[:, fb * P:(fb + 1) * P], self.R.weff[:, c, fb * P:(fb + 1) * P],
                                  self.R.XT[:, c, bass.ds(i * P, P)], start=(c == 0), stop=(c == C - 1))
            mm.then_inc(self.s_h, 1)
        if "mix" in work and b == 2:
            t.wait_ge(self.s_g, i + 2)
            t.wait_ge(self.s_a, i + 1)
            t.matmul(self.py[:, 0:D], self.R.ones[0:1, :], self.b2[0:1, :], start=True, stop=False)
            for c in range(C):
                mm = t.matmul(self.py[:, 0:D], self.hid[:, c], self.w2[:, c, :], start=False, stop=(c == C - 1))
            mm.then_inc(self.s_o, 1)
        if "sum" in work and b == 1:
            t.wait_ge(self.s_counted, 1)
            t.matmul(self.psum[:, 0, 0:self.WINS], self.tri[:, :], self.tot[:, :], start=True, stop=True)
            t.matmul(self.psum[:, 1, 0:self.WINS], self.R.ones[:, :], self.tot[:, :], start=True, stop=True)\
                .then_inc(self.s_summed, 1)

    def scalar(self, a, i, b, work):
        if "mix" in work and b == 1:
            a.wait_ge(self.s_h, i + 1)
            for fb in range(C):
                ins = a.activation(self.hid[:, fb], self.ph[:, fb * P:(fb + 1) * P], ACT.Gelu,
                                   bias=self.R.beff[:, fb:fb + 1])
            ins.then_inc(self.s_g, 1)

    def vector(self, v, i, step, work):
        if "mix" in work and step == 3:
            v.wait_ge(self.s_o, i + 1)
            xi = xtile(self.R, i)
            v.tensor_tensor(xi, xi, self.py[:, 0:D], ALU.add).then_inc(self.s_a, 1)
        h = step // 2
        if "count" in work and step in (0, 2):
            n = 4 * i + 2 * h
            w = 2 * i + h
            v.tensor_copy(self.wcol[:, :], self.R.iota[:, bass.ds(w, 1)]).then_inc(self.s_cnt, 1)
            v.wait_ge(self.s_cnt, n + 1)
            v.tensor_scalar(self.hit[:, :], self.win[:, :], self.wcol[:, 0:1], None, ALU.is_equal, ALU.add,
                            accum_out=self.tot[:, bass.ds(w, 1)]).then_inc(self.s_cnt, 1)
            v.wait_ge(self.s_cnt, n + 2)
        if "sum" in work and step == 0:
            v.sem_inc(self.s_counted, 1)
        if "sum" in work and step == 2:
            st = self.st
            v.wait_ge(self.s_summed, 1)
            st.then(v.memset(self.scanin[:, :], 0.0))
            st.then(v.tensor_copy(self.scanin[:, 1:], self.psum[:, 1, 0:self.WINS]))
            st.then(v.tensor_tensor_scan(self.start[:, :], self.one[:, 0:self.WINS + 1], self.scanin[:, :], 0.0,
                                         ALU.mult, ALU.add))
            st.then(v.tensor_copy(self.R.fstart[:, :], self.start[:, 0:W]))
            st.then(v.tensor_tensor(self.base[:, :], self.start[:, 0:self.WINS], self.psum[:, 0, 0:self.WINS],
                                    ALU.add))
        if "rank" in work and step in (0, 2):
            n = 10 * (i - self.HALFW - 1) + 5 * h
            w = 2 * (i - self.HALFW - 1) + h
            v.tensor_copy(self.wcol[:, :], self.R.iota[:, bass.ds(w, 1)]).then_inc(self.s_rank, 1)
            v.tensor_copy(self.bcol[:, :], self.base[:, bass.ds(w, 1)]).then_inc(self.s_rank, 1)
            v.wait_ge(self.s_rank, n + 2)
            v.tensor_scalar(self.hit[:, :], self.win[:, :], self.wcol[:, 0:1], None, ALU.is_equal)\
                .then_inc(self.s_rank, 1)
            v.wait_ge(self.s_rank, n + 3)
            v.tensor_tensor_scan(self.rank[:, :], self.one[:, :], self.hit[:, :], self.bcol[:, 0:1], ALU.mult,
                                 ALU.add).then_inc(self.s_rank, 1)
            v.wait_ge(self.s_rank, n + 4)
            v.sem_inc(self.s_seen, 1)
            v.copy_predicated(self.pos[:, :], self.hit[:, :].bitcast(I32), self.rank[:, :]).then_inc(self.s_rank, 1)
            v.wait_ge(self.s_rank, n + 5)
        if "end" in work and step == 0:
            self.st.then(v.tensor_scalar(self.R.fpos[:, :], self.pos[:, :], 1.0, None, ALU.subtract))



def edges(nc, R, tag, table, nslots, src_ix, dst_rel, wtab, wnext, acc, heads=0, width=0, adst3=None, gmax=None,
          split=False, beside=None):
    FEAT = heads * width
    ROW = table.shape[1]
    F = ROW if split else acc.shape[2]
    SUM = acc.shape[2]
    Q = nslots // TURN
    with Phase(nc, tag) as f:
        rowsb = f.sb("rows", [P, NBUF, GROUP, F])
        ix = f.sb("ix", [P, NBUF, GROUP], U32)
        hot = f.sb("hot", [P, NBUF, GROUP, P], BF16 if split else F32)
        po = f.ps("po", [P, 2 if split else GROUP, 512])
        s_rows = [f.sem(f"rows{b}") for b in range(NBUF)]
        s_ix, s_hot, s_sum, s_acc, s_one, s_seen = (f.sem(n) for n in ("ix", "hot", "sum", "acc", "one", "seen"))
        ACREDIT = 2 * GROUP if split else GROUP
        if heads:
            hott = f.sb("hott", [P, 2, GROUP, P], BF16)
            adw = f.sb("adw", [P, 2, GROUP, 3 * heads], BF16)
            ad = f.sb("ad", [P, GROUP, heads])
            s_adsum, s_hb = f.sem("adsum"), f.sem("hb")
            hotb = None if split else f.sb("hotb", [P, 2, GROUP, P], BF16)
            z = f.sb("z", [P, GROUP, heads])
            lz = f.sb("lz", [P, GROUP, heads])
            zm = f.sb("zm", [P, GROUP, heads])
            lm = f.sb("lm", [P, GROUP, heads])
            ptt = f.ps("ptt", [P, GROUP * P], BF16)
            pad = f.ps("pad", [P, 2, 512])
            s_tp, s_tt, s_adw, s_ad, s_z, s_zm, s_lz, s_lm, s_d, s_ex, s_msg = (
                f.sem(n) for n in ("tp", "tt", "adw", "ad", "z", "zm", "lz", "lm", "d", "ex", "msg"))

        if split:
            parts = f.sb("parts", [P, 2, GROUP, 3, F], BF16)
            s_part = f.sem("part")

        def bank(b, u):
            return po[:, b % 2, u * SUM:(u + 1) * SUM] if split else po[:, u, 0:SUM]

        stages = beside.stages(Q) if beside else [(0, Q, None)]
        if beside:
            beside.place(f)

        def turns(engine, turn):
            for lo, hi, work in stages:
                if hi - lo == 1:
                    turn(lo, work)
                else:
                    with engine.Fori(lo, hi) as i:
                        turn(i, work)

        def windows(engine, at, n):
            _, ws = nc.values_load_multi_w_load_instructions(
                at, engines=(engine,), min_val=0, max_val=W - 1,
                skip_runtime_bounds_check_because="a count of at most W - 1 windows")
            assert len(ws) == n
            return ws

        with nc.Block() as block:
            @block.gpsimd
            def _(g):
                def gather(b, copied):
                    g.wait_ge(s_ix, copied)
                    g.sem_inc(s_seen, 1)
                    for u in range(GROUP):
                        g.indirect_dma_start(rowsb[:, b, u, 0:ROW], None, table,
                                             bass.IndirectOffsetOnAxis(ix[:, b, u:u + 1], 0)).then_inc(s_rows[b], 16)

                if beside:
                    beside.pool_start(g)
                with g.Fori(0, Q) as i:
                    for b in range(NBUF):
                        gather(b, NBUF * i + b + 1)
                if heads:
                    gather(0, NBUF * Q + 1)

            @block.scalar
            def _(a):
                def indices(q, b):
                    a.activation(ix[:, b], src_ix[:, bass.ds(GROUP * q, GROUP)], ACT.Copy).then_inc(s_ix, 1)

                def window_scores(par, ws):
                    for u in range(GROUP):
                        ins = a.activation(adw[:, par, u], adst3[:, bass.ds(ws[u], 1), :].rearrange("p a h -> p (a h)"),
                                           ACT.Copy)
                    ins.then_inc(s_adw, 1)

                def half_hot(q, b, ahead=True):
                    if not split:
                        a.wait_ge(s_hot, q + 1)
                        if ahead:
                            a.wait_ge(s_tp, q - 1)
                        a.activation(hotb[:, b % 2], hot[:, b], ACT.Copy).then_inc(s_hb, 1)

                def turned(q, par):
                    a.wait_ge(s_tp, q + 1)
                    a.activation(hott[:, par], ptt[:, :].rearrange("p (u e) -> p u e", u=GROUP), ACT.Copy)\
                        .then_inc(s_tt, 1)

                def weight(q, b):
                    a.wait_ge(s_d, q + 1)
                    a.activation(rowsb[:, b, :, FEAT:FEAT + heads], z[:, :, :], ACT.Exp).then_inc(s_ex, 1)

                for b in range(NBUF):
                    indices(b, b)
                if heads:
                    ws = windows(ENG.Activation, wtab[0:1, 0:2 * GROUP], 2 * GROUP)
                    for q in range(3):
                        if q < 2:
                            window_scores(q, ws[q * GROUP:(q + 1) * GROUP])
                        half_hot(q, q, q == 2)
                        turned(q, q % 2)
                    weight(0, 0)
                def turn(i, work):
                    if heads:
                        ws = windows(ENG.Activation, wnext[0:1, bass.ds(TURN * i, TURN)], TURN)
                    for b in range(NBUF):
                        q = NBUF * i + b
                        if heads:
                            a.wait_ge(s_ad, q + 1)
                            window_scores(b % 2, ws[b * GROUP:(b + 1) * GROUP])
                            weight(q + 1, (b + 1) % NBUF)
                            half_hot(q + 3, (b + 3) % NBUF)
                        if work:
                            beside.scalar(a, i, b, work)
                        if heads:
                            turned(q + 3, (b + 1) % 2)
                        a.wait_ge(s_sum, GROUP * q + GROUP)
                        indices(q + NBUF, b)

                turns(a, turn)

            @block.vector
            def _(v):
                def one_hot(q, b):
                    v.tensor_tensor(hot[:, b], R.iota[:, :].unsqueeze(1).to_broadcast([P, GROUP, P]),
                                    dst_rel[:, bass.ds(GROUP * q, GROUP)].unsqueeze(2).to_broadcast([P, GROUP, P]),
                                    ALU.is_equal).then_inc(s_hot, 1)

                def exponents(q, b, gathered):
                    v.wait_ge(s_ad, q + 1)
                    v.tensor_reduce(ad[:, :, :], pad[:, b % 2, 0:GROUP * 3 * heads]
                                    .rearrange("p (u k h) -> p u h k", k=3, h=heads), AXX, ALU.add).then_inc(s_adsum, 1)
                    v.wait_ge(s_adsum, q + 1)
                    v.tensor_tensor(zm[:, :, :], ad[:, :, :], gmax[:, :].unsqueeze(1).to_broadcast([P, GROUP, heads]),
                                    ALU.add).then_inc(s_zm, 1)
                    v.wait_ge(s_rows[b], gathered)
                    v.tensor_tensor(z[:, :, :], ad[:, :, :], rowsb[:, b, :, FEAT:FEAT + heads], ALU.add).then_inc(s_z, 1)
                    v.wait_ge(s_zm, q + 1)
                    v.scalar_tensor_tensor(lm[:, :, :], zm[:, :, :], 0.2, zm[:, :, :], ALU.mult, ALU.max)\
                        .then_inc(s_lm, 1)
                    v.wait_ge(s_z, q + 1)
                    v.scalar_tensor_tensor(lz[:, :, :], z[:, :, :], 0.2, z[:, :, :], ALU.mult, ALU.max)\
                        .then_inc(s_lz, 1)
                    v.wait_ge(s_lm, q + 1)
                    v.wait_ge(s_lz, q + 1)
                    v.tensor_tensor(z[:, :, :], lz[:, :, :], lm[:, :, :], ALU.subtract).then_inc(s_d, 1)

                def cut(q, b):
                    m, part = rowsb[:, b], parts[:, b % 2]
                    v.wait_ge(s_part, 4 * q + 1)
                    v.tensor_copy(part[:, :, 0], m).then_inc(s_part, 1)
                    v.wait_ge(s_part, 4 * q + 2)
                    v.tensor_tensor(m, m, part[:, :, 0], ALU.subtract).then_inc(s_part, 1)
                    v.wait_ge(s_part, 4 * q + 3)
                    v.tensor_copy(part[:, :, 1], m).then_inc(s_part, 1)
                    v.wait_ge(s_part, 4 * q + 4)
                    v.tensor_tensor(part[:, :, 2], m, part[:, :, 1], ALU.subtract).then_inc(s_msg, 1)

                def message(q, b):
                    v.wait_ge(s_ex, q + 1)
                    m = rowsb[:, b, :, 0:FEAT].rearrange("p u (h c) -> p u h c", h=heads)
                    v.tensor_tensor(m, m, rowsb[:, b, :, FEAT:FEAT + heads].unsqueeze(3)
                                    .to_broadcast([P, GROUP, heads, width]), ALU.mult)\
                        .then_inc(s_part if split else s_msg, 1)
                    if split:
                        cut(q, b)

                if F > ROW:
                    v.memset(rowsb[:, :, :, ROW:F], 1.0).then_inc(s_one, 1)
                one_hot(0, 0)
                one_hot(1, 1)
                one_hot(2, 2)
                if heads:
                    exponents(0, 0, 16 * GROUP)
                    message(0, 0)
                if beside:
                    beside.vector_start(v)

                def turn(i, work):
                    wt = windows(ENG.DVE, wtab[0:1, bass.ds(TURN * i, TURN)], TURN)
                    for b in range(NBUF):
                        q = NBUF * i + b
                        if heads:
                            exponents(q + 1, (b + 1) % NBUF, 16 * GROUP * (i + 1 + (b + 1) // NBUF))
                        one_hot(q + 3, (b + 3) % NBUF)
                        if work:
                            beside.vector(v, i, b, work)
                        for u in range(GROUP):
                            if heads and u == GROUP // 2:
                                message(q + 1, (b + 1) % NBUF)
                            v.wait_ge(s_sum, GROUP * q + (GROUP if split else u + 1))
                            v.wait_ge(s_acc, GROUP * q + u + ACREDIT)
                            aw = acc[:, bass.ds(wt[b * GROUP + u], 1), :].rearrange("p a d -> p (a d)")
                            v.tensor_tensor(aw, aw, bank(b, u), ALU.add).then_inc(s_acc, 1)
                    if work:
                        beside.vector(v, i, NBUF, work)

                turns(v, turn)

            @block.tensor
            def _(t):
                def turn_hot(q, b):
                    t.wait_ge(s_hot if split else s_hb, q + 1)
                    for u in range(GROUP):
                        one = hot[:, b, u] if split else hotb[:, b % 2, u]
                        mm = t.transpose(ptt[:, u * P:(u + 1) * P], one, R.identb[:, :])
                    mm.then_inc(s_tp, 1)

                def scores(q, b):
                    t.wait_ge(s_tt, q + 1)
                    t.wait_ge(s_adw, q + 1)
                    for u in range(GROUP):
                        o = u * 3 * heads
                        mm = t.matmul(pad[:, b % 2, o:o + 3 * heads], hott[:, b % 2, u], adw[:, b % 2, u], start=True,
                                      stop=True)
                    mm.then_inc(s_ad, 1)

                t.sem_inc(s_acc, ACREDIT)
                if F > ROW:
                    t.wait_ge(s_one, 1)
                if heads:
                    turn_hot(0, 0)
                    scores(0, 0)
                    turn_hot(1, 1)
                    scores(1, 1)
                    turn_hot(2, 2)
                if beside:
                    beside.tensor_start(t)

                def turn(i, work):
                    for b in range(NBUF):
                        q = NBUF * i + b
                        if heads:
                            t.wait_ge(s_msg, q + 1)
                        else:
                            t.wait_ge(s_hot, q + 1)
                            t.wait_ge(s_rows[b], 16 * GROUP * i + 16 * GROUP)
                        for u in range(GROUP):
                            if heads and u == GROUP // 2:
                                scores(q + 2, (b + 2) % NBUF)
                            t.wait_ge(s_acc, GROUP * q + (GROUP if split else u + 1))
                            w = parts[:, b % 2, u].rearrange("p k f -> p (k f)") if split else rowsb[:, b, u, :]
                            t.matmul(bank(b, u), hot[:, b, u], w, start=True, stop=True).then_inc(s_sum, 1)
                        if heads:
                            turn_hot(q + 3, (b + 3) % NBUF)
                        if work:
                            beside.tensor(t, i, b, work)

                turns(t, turn)

            @block.sync
            def _(s):
                if beside:
                    beside.sync(s)


def loops(nc, R, tag, table, acc, heads, width, adst, adst3, gmax):
    ROW = table.shape[1]
    FEAT = heads * width
    with Phase(nc, tag) as f:
        z = f.sb("z", [P, W, heads])
        zm = f.sb("zm", [P, W, heads])
        s_in, s_st, s_go, s_ex = (f.sem(n) for n in ("in", "st", "go", "ex"))
        with nc.Block() as block:
            @block.sync
            def _(s):
                s.dma_start(acc[:, :, 0:ROW], table.rearrange("(t p) d -> p t d", p=P)).then_inc(s_in, 16)

            @block.vector
            def _(v):
                st = Steps(v, s_st)
                if acc.shape[2] > ROW:
                    v.memset(acc[:, :, ROW:], 0.0)
                st.then(v.tensor_copy(z[:, :, :], adst[:, :, :]))
                for k in range(3):
                    part = adst3[:, :, k * heads:(k + 1) * heads]
                    st.then(v.tensor_copy(part, z[:, :, :]))
                    if k < 2:
                        st.then(v.tensor_tensor(z[:, :, :], z[:, :, :], part, ALU.subtract))
                st.then(v.tensor_tensor(zm[:, :, :], adst[:, :, :], gmax[:, :].unsqueeze(1).to_broadcast([P, W, heads]),
                                        ALU.add))
                st.then(v.scalar_tensor_tensor(zm[:, :, :], zm[:, :, :], 0.2, zm[:, :, :], ALU.mult, ALU.max))
                v.wait_ge(s_in, 16)
                st.then(v.tensor_tensor(z[:, :, :], acc[:, :, FEAT:FEAT + heads], adst[:, :, :], ALU.add))
                st.then(v.scalar_tensor_tensor(z[:, :, :], z[:, :, :], 0.2, z[:, :, :], ALU.mult, ALU.max))
                st.then(v.tensor_tensor(z[:, :, :], z[:, :, :], zm[:, :, :], ALU.subtract))
                v.sem_inc(s_go, 1)
                v.wait_ge(s_ex, 1)
                a4 = acc[:, :, 0:FEAT].rearrange("p t (h c) -> p t h c", h=heads)
                v.tensor_tensor(a4, a4, acc[:, :, FEAT:FEAT + heads].unsqueeze(3).to_broadcast([P, W, heads, width]),
                                ALU.mult)

            @block.scalar
            def _(a):
                a.wait_ge(s_go, 1)
                a.activation(acc[:, :, FEAT:FEAT + heads], z[:, :, :], ACT.Exp).then_inc(s_ex, 1)


def clear(nc, tile):
    with nc.Block() as block:
        @block.vector
        def _(v):
            v.memset(tile, 0.0)



def gcn_finish(nc, R, A):
    with Phase(nc, "gcnf") as f:
        wout = f.sb("wout", [GCN + 1, D])
        bg = f.sb("bg", [P, GCN])
        nd = f.sb("nd", [P, W])
        h = f.sb("h", [P, TPI, GCN + 1])
        ht = f.sb("ht", [GCN + 1, TPI, P])
        pt = f.ps("pt", [P, 2, 512])
        po = f.ps("po", [P, 2, 512])
        s_w, s_st, s_sq, s_rt, s_ready, s_h, s_t, s_c, s_o, s_a, s_m = (
            f.sem(n) for n in ("w", "st", "sq", "rt", "ready", "h", "t", "c", "o", "a", "m"))
        with nc.Block() as block:
            @block.sync
            def _(s):
                s.dma_start(wout[0:GCN, :], A.gcn_wout).then_inc(s_w, 16)
                s.dma_start(wout[GCN:GCN + 1, :], A.gcn_bout).then_inc(s_w, 16)
                s.dma_start(bg[:, :], spread(A.gcn_b)).then_inc(s_w, 16)

            @block.vector
            def _(v):
                st = Steps(v, s_st)
                st.then(v.tensor_scalar(nd[:, :], R.gcn[:, :, GCN], 1.0, None, ALU.max))
                v.sem_inc(s_sq, 1)
                v.memset(h[:, :, GCN:GCN + 1], 1.0).then_inc(s_m, 1)
                v.wait_ge(s_rt, 1)
                st.then(v.reciprocal(nd[:, :], nd[:, :]))
                g3 = R.gcn[:, :, 0:GCN]
                v.wait_ge(s_w, 48)
                st.then(v.tensor_tensor(g3, g3, nd[:, :].unsqueeze(2).to_broadcast([P, W, GCN]), ALU.mult))
                st.then(v.tensor_tensor(g3, g3, bg[:, :].unsqueeze(1).to_broadcast([P, W, GCN]), ALU.add))
                with v.Fori(0, ITER) as i:
                    v.wait_ge(s_t, TPI * i)
                    v.tensor_scalar(h[:, :, 0:GCN], R.gcn[:, bass.ds(TPI * i, TPI), 0:GCN], 0.0, None, ALU.max)\
                        .then_inc(s_h, 1)
                    for j in range(TPI):
                        v.wait_ge(s_o, TPI * i + j + 1)
                        xj = xtile(R, TPI * i + j)
                        v.tensor_tensor(xj, xj, po[:, j % 2, 0:D], ALU.add).then_inc(s_a, 1)

            @block.scalar
            def _(a):
                a.wait_ge(s_sq, 1)
                a.activation(nd[:, :], nd[:, :], ACT.Sqrt).then_inc(s_rt, 1)
                with a.Fori(0, ITER) as i:
                    a.wait_ge(s_o, TPI * i)
                    for j in range(TPI):
                        a.wait_ge(s_t, TPI * i + j + 1)
                        a.activation(ht[:, j], pt[0:GCN + 1, j % 2, 0:P], ACT.Copy).then_inc(s_c, 1)

            @block.tensor
            def _(t):
                t.wait_ge(s_w, 48)
                t.wait_ge(s_m, 1)
                with t.Fori(0, ITER) as i:
                    t.wait_ge(s_h, i + 1)
                    for j in range(TPI):
                        t.wait_ge(s_c, TPI * i + (j - 1 if j >= 2 else 0))
                        t.transpose(pt[0:GCN + 1, j % 2, 0:P], h[:, j], R.ident[:, :]).then_inc(s_t, 1)
                        t.wait_ge(s_c, TPI * i + j + 1)
                        t.wait_ge(s_a, TPI * i + (j - 1 if j >= 2 else 0))
                        t.matmul(po[:, j % 2, 0:D], ht[:, j], wout[:, :], start=True, stop=True).then_inc(s_o, 1)



def gates0(nc, R, A):
    with Phase(nc, "gate0") as f:
        nm = Norm(f, R)
        wr = f.sb("wr", [P, C, E0])
        br = f.sb("br", [P, E0])
        bo = f.sb("bo", [E0, D])
        lg = f.sb("lg", [P, TPI, E0])
        mx = f.sb("mx", [P, TPI])
        gt = f.sb("gt", [E0, TPI, P])
        pl = f.ps("pl", [P, 512])
        pg = f.ps("pg", [P, 512])
        po = f.ps("po", [P, 2, 512])
        s_w, s_l, s_m, s_e, s_gt, s_gc, s_o, s_a, s_xr, s_c = (
            f.sem(n) for n in ("w", "l", "m", "e", "gt", "gc", "o", "a", "xr2", "c"))
        s_g = [f.sem(f"g{k}") for k in range(5)]
        with nc.Block() as block:
            @block.sync
            def _(s):
                s.dma_start(wr[:, :, :], rows(A.f0_wr)).then_inc(s_w, 16)
                s.dma_start(br[:, :], spread(A.f0_br)).then_inc(s_w, 16)
                s.dma_start(bo[:, :], A.f0_bo).then_inc(s_w, 16)

            @block.vector
            def _(v):
                v.wait_ge(s_w, 48)
                with v.Fori(0, ITER) as i:
                    nm.vector(v, i)
                    v.wait_ge(s_l, TPI * i + TPI)
                    v.tensor_tensor(lg[:, :, :], pl[:, 0:TPI * E0].rearrange("p (t e) -> p t e", e=E0),
                                    br[:, :].unsqueeze(1).to_broadcast([P, TPI, E0]), ALU.add).then_inc(s_g[0], 1)
                    v.wait_ge(s_g[0], i + 1)
                    v.tensor_reduce(mx[:, :], lg[:, :, :], AXX, ALU.max).then_inc(s_g[1], 1)
                    v.wait_ge(s_g[1], i + 1)
                    v.tensor_tensor(lg[:, :, :], lg[:, :, :], mx[:, :].unsqueeze(2).to_broadcast([P, TPI, E0]),
                                    ALU.subtract).then_inc(s_m, 1)
                    v.wait_ge(s_e, i + 1)
                    v.tensor_reduce(mx[:, :], lg[:, :, :], AXX, ALU.add).then_inc(s_g[2], 1)
                    v.wait_ge(s_g[2], i + 1)
                    v.reciprocal(mx[:, :], mx[:, :]).then_inc(s_g[3], 1)
                    v.wait_ge(s_g[3], i + 1)
                    v.tensor_tensor(R.gate[:, bass.ds(TPI * i, TPI), 0:E0], lg[:, :, :],
                                    mx[:, :].unsqueeze(2).to_broadcast([P, TPI, E0]), ALU.mult).then_inc(s_c, 1)
                    v.tensor_tensor(lg[:, :, :], lg[:, :, :], mx[:, :].unsqueeze(2).to_broadcast([P, TPI, E0]),
                                    ALU.mult).then_inc(s_g[4], 1)
                    for j in range(TPI):
                        v.wait_ge(s_o, TPI * i + j + 1)
                        xj = xtile(R, TPI * i + j)
                        v.tensor_tensor(xj, xj, po[:, j % 2, 0:D], ALU.add).then_inc(s_a, 1)

            @block.scalar
            def _(a):
                with a.Fori(0, ITER) as i:
                    nm.scalar_root(a, i)
                    a.wait_ge(s_l, TPI * i)
                    for j in range(TPI):
                        nm.scalar_copy(a, i, j)
                    a.wait_ge(s_m, i + 1)
                    a.activation(lg[:, :, :], lg[:, :, :], ACT.Exp).then_inc(s_e, 1)
                    for j in range(TPI):
                        a.wait_ge(s_gt, TPI * i + j + 1)
                        a.activation(gt[:, j], pg[0:E0, (j % 4) * P:(j % 4 + 1) * P], ACT.Copy).then_inc(s_gc, 1)

            @block.tensor
            def _(t):
                t.wait_ge(s_w, 48)
                with t.Fori(0, ITER) as i:
                    nm.tensor(t, i, 0)
                    t.wait_ge(s_g[0], i)
                    for j in range(TPI):
                        if j + 1 < TPI:
                            nm.tensor(t, i, j + 1)
                        t.wait_ge(nm.s_xt, TPI * i + j + 1)
                        for c in range(C):
                            mm = t.matmul(pl[:, j * E0:(j + 1) * E0], nm.xt[:, j, c], wr[:, c, :], start=(c == 0),
                                          stop=(c == C - 1))
                        mm.then_inc(s_l, 1)
                    t.wait_ge(s_g[4], i + 1)
                    for j in range(TPI):
                        t.wait_ge(s_gc, TPI * i + (j - 3 if j >= 4 else 0))
                        t.transpose(pg[0:E0, (j % 4) * P:(j % 4 + 1) * P], lg[:, j], R.ident[:, :]).then_inc(s_gt, 1)
                        t.wait_ge(s_gc, TPI * i + j + 1)
                        t.wait_ge(s_a, TPI * i + (j - 1 if j >= 2 else 0))
                        t.matmul(po[:, j % 2, 0:D], gt[:, j], bo[:, :], start=True, stop=True).then_inc(s_o, 1)


def experts0(nc, R, A):
    with Phase(nc, "exp0") as f:
        w1 = f.sb("w1", [P, E0, C, D])
        w2 = f.sb("w2", [P, E0, C, D])
        wo = f.sb("wo", [P, E0, C, D])
        bn = f.sb("bn", [P, 2, 5, E0 * C])
        scale = f.sb("scale", [P, 2, E0 * C])
        shift = f.sb("shift", [P, 2, E0 * C])
        h1 = f.sb("h1", [P, C, TOK])
        h2 = f.sb("h2", [P, C, TOK])
        ph = f.ps("ph", [P, 4, 512])
        po = f.ps("po", [P, 4, 512])
        s_w, s_b, s_st, s_v, s_rt, s_ready, s_h, s_g, s_o, s_a, s_l2 = (
            f.sem(n) for n in ("w", "b", "st", "v", "rt", "ready", "h", "g", "o", "a", "l2"))
        ix = f.sb("ix", [P, 2, GROUP8], U32)
        rec = f.sb("rec", [P, 2, GROUP8, 2], I32)
        s_seen = f.sem("seen")
        s_ix, s_sc = f.sem("ix"), [f.sem(f"sc{k}") for k in range(2)]
        with nc.Block() as block:
            @block.gpsimd
            def _(g):
                with g.Fori(0, FB // (2 * GROUP8)) as i:
                    for b in range(2):
                        g.wait_ge(s_sc[b], 16 * GROUP8 * i)
                        q = 2 * i + b
                        g.tensor_copy(ix[:, b], R.fpos[:, bass.ds(GROUP8 * q, GROUP8)]).then_inc(s_ix, 1)
                        g.tensor_copy(rec[:, b].rearrange("p t k -> p (t k)"),
                                      R.frec[:, bass.ds(GROUP8 * q, GROUP8), :].rearrange("p t k -> p (t k)"))\
                            .then_inc(s_ix, 1)
                        g.wait_ge(s_ix, 4 * i + 2 * b + 2)
                        g.sem_inc(s_seen, 1)
                        for u in range(GROUP8):
                            g.indirect_dma_start(R.fsorted, bass.IndirectOffsetOnAxis(ix[:, b, u:u + 1], 0),
                                                 rec[:, b, u], None).then_inc(s_sc[b], 16)
                for b in range(2):
                    g.wait_ge(s_sc[b], 16 * FB // 2)

            @block.sync
            def _(s):
                s.dma_start(bn[:, :, :, :], A.f0_bn).then_inc(s_b, 16)
                for wt, wd in ((w1, A.f0_w1), (w2, A.f0_w2), (wo, A.f0_wo)):
                    for e in range(E0):
                        s.dma_start(wt[:, e], rows(wd[e])).then_inc(s_w, 16)

            @block.tensor
            def _(t):
                t.wait_ge(s_w, 16 * 3 * E0)
                with t.Fori(0, ITER) as i:
                    base = 8 * E0 * i

                    def layer(e, l):
                        k = 2 * e + l
                        for fb in range(C):
                            for h in range(2):
                                n = 2 * fb + h
                                t.wait_ge(s_g, base + (4 * (k - 1) + n + 1 if k else 0))
                                for c in range(C):
                                    x = R.XT[:, c, bass.ds(i * TOK + h * HALF, HALF)] if l == 0 else \
                                        h1[:, c, h * HALF:(h + 1) * HALF]
                                    w = (w1, w2)[l][:, e, c, fb * P:(fb + 1) * P]
                                    mm = t.matmul(ph[:, n, 0:HALF], w, x, start=(c == 0), stop=(c == C - 1))
                                mm.then_inc(s_h, 1)

                    layer(0, 0)
                    for e in range(E0):
                        t.wait_ge(s_g, base + 8 * e + 4)
                        layer(e, 1)
                        if e + 1 < E0:
                            layer(e + 1, 0)
                        t.wait_ge(s_g, base + 8 * e + 8)
                        for j in range(TPI):
                            n = TPI * e + j
                            t.wait_ge(s_a, TPI * E0 * i + max(n - 3, 0))
                            for c in range(C):
                                mm = t.matmul(po[:, n % 4, 0:D], h2[:, c, j * P:(j + 1) * P], wo[:, e, c, :],
                                              start=(c == 0), stop=(c == C - 1))
                            mm.then_inc(s_o, 1)

            @block.vector
            def _(v):
                st = Steps(v, s_st)
                v.wait_ge(s_b, 16)
                st.then(v.tensor_scalar(scale[:, :, :], bn[:, :, 4, :], BN_EPS, None, ALU.add))
                v.sem_inc(s_v, 1)
                v.wait_ge(s_rt, 1)
                st.then(v.reciprocal(scale[:, :, :], scale[:, :, :]))
                st.then(v.tensor_tensor(scale[:, :, :], scale[:, :, :], bn[:, :, 1, :], ALU.mult))
                st.then(v.tensor_tensor(shift[:, :, :], bn[:, :, 0, :], bn[:, :, 3, :], ALU.subtract))
                st.then(v.tensor_tensor(shift[:, :, :], shift[:, :, :], scale[:, :, :], ALU.mult))
                st.then(v.tensor_tensor(shift[:, :, :], shift[:, :, :], bn[:, :, 2, :], ALU.add))
                v.sem_inc(s_ready, 1)
                with v.Fori(0, ITER) as i:
                    for e in range(E0):
                        for j in range(TPI):
                            n = TPI * e + j
                            v.wait_ge(s_o, TPI * E0 * i + n + 1)
                            v.wait_ge(s_a, TPI * E0 * i + max(n - 6, 0))
                            xj = xtile(R, TPI * i + j)
                            g = R.gate[:, bass.ds(TPI * i + j, 1), e:e + 1].rearrange("p a b -> p (a b)")
                            v.scalar_tensor_tensor(xj, po[:, n % 4, 0:D], g, xj, ALU.mult, ALU.add).then_inc(s_a, 1)

            @block.scalar
            def _(a):
                a.wait_ge(s_v, 1)
                a.activation(scale[:, :, :], scale[:, :, :], ACT.Sqrt).then_inc(s_rt, 1)
                a.wait_ge(s_ready, 1)
                with a.Fori(0, ITER) as i:
                    for e in range(E0):
                        for l in range(2):
                            k = 2 * e + l
                            if l:
                                a.wait_ge(s_o, TPI * E0 * i + TPI * e)
                            for fb in range(C):
                                for h in range(2):
                                    n = 2 * fb + h
                                    a.wait_ge(s_h, 8 * E0 * i + 4 * k + n + 1)
                                    a.activation((h1, h2)[l][:, fb, h * HALF:(h + 1) * HALF], ph[:, n, 0:HALF],
                                                 ACT.Relu, bias=shift[:, l, C * e + fb:C * e + fb + 1],
                                                 scale=scale[:, l, C * e + fb:C * e + fb + 1]).then_inc(s_g, 1)



def finish1(nc, R, A):
    with Phase(nc, "fin1") as f:
        bias = f.sb("bias", [1, 2, D])
        den = f.sb("den", [P, W, GH])
        xt = f.sb("xt", [P, TPI, C, P])
        po = f.ps("po", [P, 2, 512])
        s_w, s_st, s_x, s_o, s_m, s_b, s_a = (f.sem(n) for n in ("w", "st", "x", "o", "m", "b", "a"))
        with nc.Block() as block:
            @block.sync
            def _(s):
                s.dma_start(bias[:, 0, :], A.gat_bias).then_inc(s_w, 16)
                s.dma_start(bias[:, 1, :], A.m1_bout).then_inc(s_w, 16)

            @block.scalar
            def _(a):
                with a.Fori(0, ITER) as i:
                    a.wait_ge(s_o, TPI * i)
                    for j in range(TPI):
                        a.activation(xt[:, j], R.XT[:, :, bass.ds((TPI * i + j) * P, P)], ACT.Copy).then_inc(s_x, 1)

            @block.tensor
            def _(t):
                t.wait_ge(s_w, 32)
                with t.Fori(0, ITER) as i:
                    for j in range(TPI):
                        t.wait_ge(s_x, TPI * i + j + 1)
                        t.wait_ge(s_b, TPI * i + (j - 1 if j >= 2 else 0))
                        for k in range(2):
                            t.matmul(po[:, j % 2, 0:D], R.ones[0:1, :], bias[0:1, k, :], start=(k == 0), stop=False)
                        for c in range(C):
                            mm = t.matmul(po[:, j % 2, 0:D], xt[:, j, c], R.weff[:, c, :], start=False,
                                          stop=(c == C - 1))
                        mm.then_inc(s_o, 1)

            @block.vector
            def _(v):
                st = Steps(v, s_st)
                st.then(v.tensor_scalar(den[:, :, :], R.gat[:, :, GH * GC:GROW], 1e-30, None, ALU.max))
                st.then(v.reciprocal(den[:, :, :], den[:, :, :]))
                with v.Fori(0, ITER) as i:
                    for j in range(TPI):
                        n = TPI * i + j
                        a3 = R.gat[:, bass.ds(n, 1), 0:GH * GC].rearrange("p a (h c) -> p (a h) c", c=GC)
                        a2 = R.gat[:, bass.ds(n, 1), 0:GH * GC].rearrange("p a d -> p (a d)")
                        d3 = den[:, bass.ds(n, 1), :].rearrange("p a h -> p (a h)").unsqueeze(2).to_broadcast([P, GH, GC])
                        v.tensor_tensor(a3, a3, d3, ALU.mult).then_inc(s_m, 1)
                        xj = xtile(R, n)
                        v.wait_ge(s_o, n + 1)
                        v.tensor_tensor(xj, xj, po[:, j % 2, 0:D], ALU.add).then_inc(s_b, 1)
                        v.wait_ge(s_m, n + 1)
                        v.wait_ge(s_b, n + 1)
                        v.tensor_tensor(xj, xj, a2, ALU.add).then_inc(s_a, 1)



def router_table(nc, R, A):
    FX = FH * FC
    EXT = FX + 2 * FH
    with Phase(nc, "rtab") as f:
        nm = Norm(f, R)
        w = f.sb("w", [P, C, EXT])
        att = f.sb("att", [P, 2, FX])
        wa = f.sb("wa", [P, FX])
        tabt = f.sb("tabt", [P, W, FROW])
        gm = f.sb("gm", [P, FH])
        pl = f.ps("pl", [P, 512])
        s_w, s_st, s_l, s_e, s_t, s_ready, s_o, s_red = (
            f.sem(n) for n in ("w_", "st", "l", "e", "t", "ready", "o", "red"))
        with nc.Block() as block:
            @block.sync
            def _(s):
                s.dma_start(w[:, :, 0:FX], rows(A.r_w)).then_inc(s_w, 16)
                for k, row in enumerate((A.r_src, A.r_dst)):
                    s.dma_start(att[:, k, :], spread(row)).then_inc(s_w, 16)
                s.wait_ge(s_t, 1)
                s.dma_start(R.tabr.rearrange("(t p) d -> p t d", p=P), tabt[:, :, :]).then_inc(s_o, 16)
                s.wait_ge(s_o, 16)

            @block.vector
            def _(v):
                st = Steps(v, s_st)
                v.wait_ge(s_w, 48)
                for c in range(C):
                    for k in range(2):
                        st.then(v.tensor_tensor(wa[:, :], w[:, c, 0:FX], att[:, k, :], ALU.mult))
                        o = FX + k * FH
                        st.then(v.tensor_reduce(w[:, c, o:o + FH], wa[:, :].rearrange("p (h c) -> p h c", h=FH), AXX,
                                                ALU.add))
                v.sem_inc(s_ready, 1)
                with v.Fori(0, ITER) as i:
                    nm.vector(v, i)
                    v.wait_ge(s_l, TPI * i + TPI)
                    v.tensor_copy(R.rext[:, bass.ds(TPI * i, TPI), :],
                                  pl[:, 0:TPI * EXT].rearrange("p (t e) -> p t e", e=EXT)).then_inc(s_e, 1)
                v.wait_ge(s_e, ITER)
                st.then(v.tensor_copy(tabt[:, :, :], R.rext[:, :, 0:FROW]))
                v.sem_inc(s_t, 1)
                st.then(v.tensor_copy(R.rdst[:, :, :], R.rext[:, :, FROW:EXT]))
                st.then(v.tensor_reduce(gm[:, :], R.rext[:, :, FX:FROW].rearrange("p t h -> p h t"), AXX, ALU.max))
                v.sem_inc(s_red, 1)

            @block.gpsimd
            def _(g):
                g.wait_ge(s_red, 1)
                g.partition_all_reduce(R.rmax[:, :], gm[:, :], P, bass.bass_isa.ReduceOp.max)

            @block.scalar
            def _(a):
                with a.Fori(0, ITER) as i:
                    nm.scalar_root(a, i)
                    a.wait_ge(s_l, TPI * i)
                    for j in range(TPI):
                        nm.scalar_copy(a, i, j)

            @block.tensor
            def _(t):
                t.wait_ge(s_ready, 1)
                with t.Fori(0, ITER) as i:
                    nm.tensor(t, i, 0)
                    t.wait_ge(s_e, i)
                    for j in range(TPI):
                        if j + 1 < TPI:
                            nm.tensor(t, i, j + 1)
                        t.wait_ge(nm.s_xt, TPI * i + j + 1)
                        for c in range(C):
                            mm = t.matmul(pl[:, j * EXT:(j + 1) * EXT], nm.xt[:, j, c], w[:, c, :], start=(c == 0),
                                          stop=(c == C - 1))
                        mm.then_inc(s_l, 1)


def router_gates(nc, R, A):
    FX = FH * FC
    K = E1
    with Phase(nc, "rgate") as f:
        z = f.sb("z", [P, W, FH])
        t16 = f.sb("t16", [P, W, FX])
        a = f.sb("a", [P, W, FX])
        m = f.sb("m", [P, W])
        r = f.sb("r", [P, W])
        bg = f.sb("bg", [P, 3, FX])
        sc = f.sb("sc", [P, W, K])
        rank = f.sb("rank", [P, W, K])
        gt = f.sb("gt", [P, W])
        s_w, s_st, s_go, s_back = (f.sem(n) for n in ("w", "st", "go", "back"))
        with nc.Block() as block:
            @block.sync
            def _(s):
                for k, row in enumerate((A.r_b, A.r_gam, A.r_bet)):
                    s.dma_start(bg[:, k, :], spread(row)).then_inc(s_w, 16)

            @block.scalar
            def _(s):
                s.wait_ge(s_go, 1)
                s.activation(r[:, :], r[:, :], ACT.Sqrt).then_inc(s_back, 1)
                s.wait_ge(s_go, 2)
                s.activation(sc[:, :, :], sc[:, :, :], ACT.Exp).then_inc(s_back, 1)

            @block.vector
            def _(v):
                st = Steps(v, s_st)

                def wide(t, n):
                    return t.unsqueeze(2).to_broadcast([P, W, n])

                for k in (2, 1):
                    st.then(v.tensor_tensor(R.racc[:, :, 0:FROW], R.racc[:, :, 0:FROW],
                                            R.racc[:, :, k * FROW:(k + 1) * FROW], ALU.add))
                st.then(v.tensor_scalar(z[:, :, :], R.racc[:, :, FX:FROW], 1e-30, None, ALU.max))
                st.then(v.reciprocal(z[:, :, :], z[:, :, :]))
                for h in range(FH):
                    c = slice(h * FC, (h + 1) * FC)
                    st.then(v.tensor_tensor(a[:, :, c], R.racc[:, :, c], wide(z[:, :, h], FC), ALU.mult))
                v.wait_ge(s_w, 48)

                def row(k):
                    return bg[:, k, :].unsqueeze(1).to_broadcast([P, W, FX])

                st.then(v.tensor_tensor(a[:, :, :], a[:, :, :], row(0), ALU.add))
                st.then(v.tensor_reduce(m[:, :], a[:, :, :], AXX, ALU.add))
                st.then(v.tensor_scalar(m[:, :], m[:, :], 1.0 / FX, None, ALU.mult))
                st.then(v.tensor_tensor(a[:, :, :], a[:, :, :], wide(m[:, :], FX), ALU.subtract))
                st.then(v.tensor_tensor(t16[:, :, :], a[:, :, :], a[:, :, :], ALU.mult))
                st.then(v.tensor_reduce(r[:, :], t16[:, :, :], AXX, ALU.add))
                st.then(v.tensor_scalar(r[:, :], r[:, :], 1.0 / FX, LN_EPS, ALU.mult, ALU.add))
                v.sem_inc(s_go, 1)
                v.wait_ge(s_back, 1)
                st.then(v.reciprocal(r[:, :], r[:, :]))
                st.then(v.tensor_tensor(a[:, :, :], a[:, :, :], wide(r[:, :], FX), ALU.mult))
                st.then(v.tensor_tensor(a[:, :, :], a[:, :, :], row(1), ALU.mult))
                st.then(v.tensor_tensor(a[:, :, :], a[:, :, :], row(2), ALU.add))
                st.then(v.tensor_reduce(sc[:, :, :], a[:, :, :].rearrange("p t (h c) -> p t c h", c=FC), AXX, ALU.add))
                st.then(v.tensor_scalar(sc[:, :, :], sc[:, :, :], 1.0 / FH, None, ALU.mult))
                st.then(v.memset(rank[:, :, :], 0.0))
                for k in range(K):
                    for o in range(K):
                        if o != k:
                            st.then(v.tensor_tensor(gt[:, :], sc[:, :, o], sc[:, :, k],
                                                    ALU.is_ge if o < k else ALU.is_gt))
                            st.then(v.tensor_tensor(rank[:, :, k], rank[:, :, k], gt[:, :], ALU.add))
                st.then(v.tensor_scalar(rank[:, :, :], rank[:, :, :], 1.5, None, ALU.is_lt))
                st.then(v.tensor_reduce(m[:, :], sc[:, :, :], AXX, ALU.max))
                st.then(v.tensor_tensor(sc[:, :, :], sc[:, :, :], wide(m[:, :], K), ALU.subtract))
                v.sem_inc(s_go, 1)
                v.wait_ge(s_back, 2)
                st.then(v.tensor_tensor(sc[:, :, :], sc[:, :, :], rank[:, :, :], ALU.mult))
                st.then(v.tensor_reduce(m[:, :], sc[:, :, :], AXX, ALU.add))
                st.then(v.reciprocal(m[:, :], m[:, :]))
                st.then(v.tensor_tensor(R.gate[:, :, 0:K], sc[:, :, :], wide(m[:, :], K), ALU.mult))



class Experts1:
    PRODUCTS = ((("h", 0),), (("y", 0), ("h", 1)), (("y", 1), ("h", 2)), (("y", 2),))
    BANK = {("h", 0): 0, ("y", 0): 1, ("h", 1): 2, ("y", 1): 0, ("h", 2): 1, ("y", 2): 2}
    TAKEN = ((), (("h", 0),), (("y", 0), ("h", 1)), (("y", 1), ("h", 2)), (("y", 2),))
    HB = HID1 // P
    PER = E1 - 1
    def __init__(self, nc, R, A):
        self.nc, self.R, self.A = nc, R, A

    def pieces(self):
        PER = self.PER
        full, rest = divmod(W, PER)
        assert NBUF == PER + 1 and rest > 0
        return [(0, W, [(e, 1, 0) for e in range(PER)]),
                (W, W + full, [(PER, PER, k - PER * W) for k in range(PER)]),
                (W + full, W + full + 1, [(PER, PER, k - PER * W) for k in range(rest)])]

    def stages(self, Q):
        st, last = [], []
        for lo, hi, now in self.pieces():
            st.append((lo, lo + 1, (now, last)))
            if hi > lo + 1:
                st.append((lo + 1, hi, (now, now)))
            last = now
        assert hi < Q
        st.append((hi, hi + 1, ([], last)))
        if hi + 1 < Q:
            st.append((hi + 1, Q, None))
        return st

    def place(self, f):
        self.w1 = f.sb("w1", [P, E1, C, HID1])
        self.w2 = f.sb("w2", [P, E1, self.HB, D])
        self.b1 = f.sb("b1", [P, E1, self.HB])
        self.b2 = f.sb("b2", [P, E1, D])
        self.pre = f.sb("pre", [P, self.PER, HID1])
        self.hid = f.sb("hid", [P, self.PER, HID1])
        self.y = f.sb("y", [P, self.PER, D])
        self.px = f.ps("px", [P, self.PER, 512])
        self.s_w, self.s_b, self.s_h, self.s_pre, self.s_g, self.s_o, self.s_y = (
            f.sem(n) for n in ("xw", "xb", "xh", "xpre", "xg", "xo", "xy"))
        self.s_out = [f.sem(f"xout{k}") for k in range(self.PER)]

    def pool_start(self, g):
        pass

    def vector_start(self, v):
        pass

    def tensor_start(self, t):
        t.sem_inc(self.s_y, 2 * self.PER)
        t.sem_inc(self.s_o, self.PER)
        t.wait_ge(self.s_w, 16 * 2 * E1)

    def tensor(self, t, i, b, work):
        now, last = work
        PER = self.PER
        for what, k in self.PRODUCTS[b]:
            if k >= len(now if what == "h" else last):
                continue
            bank = self.px[:, self.BANK[what, k]]
            if what == "h":
                e, mul, off = now[k]
                t.wait_ge(self.s_y, PER * i + 2 + k)
                for fb in range(self.HB):
                    for c in range(C):
                        mm = t.matmul(bank[:, fb * P:(fb + 1) * P], self.w1[:, e, c, fb * P:(fb + 1) * P],
                                      self.R.XT[:, c, bass.ds((mul * i + off) * P, P)], start=(c == 0),
                                      stop=(c == C - 1))
                mm.then_inc(self.s_h, 1)
            else:
                if k == 0:
                    t.wait_ge(self.s_g, i)
                elif now[k - 1:]:
                    t.wait_ge(self.s_pre, PER * i + k)
                t.wait_ge(self.s_y, PER * i + k + 1)
                for c in range(self.HB):
                    mm = t.matmul(bank[:, 0:D], self.hid[:, k, c * P:(c + 1) * P], self.w2[:, last[k][0], c, :],
                                  start=(c == 0), stop=(c == self.HB - 1))
                mm.then_inc(self.s_o, 1)

    def scalar(self, a, i, b, work):
        n = len(work[1])
        if b == 0 and n:
            a.wait_ge(self.s_pre, self.PER * (i - 1) + n)
            a.wait_ge(self.s_o, self.PER * i)
            a.activation(self.hid[:, 0:n], self.pre[:, 0:n], ACT.Gelu).then_inc(self.s_g, 1)

    def vector(self, v, i, step, work):
        now, last = work
        for what, k in self.TAKEN[step]:
            if k >= len(now if what == "h" else last):
                continue
            bank = self.px[:, self.BANK[what, k]]
            if what == "h":
                v.wait_ge(self.s_h, self.PER * i + k + 1)
                if last:
                    v.wait_ge(self.s_g, i)
                b1 = self.b1[:, now[k][0]].unsqueeze(2).to_broadcast([P, self.HB, P])
                v.tensor_tensor(self.pre[:, k].rearrange("p (f t) -> p f t", t=P),
                                bank.rearrange("p (f t) -> p f t", t=P), b1, ALU.add).then_inc(self.s_pre, 1)
            else:
                v.wait_ge(self.s_o, self.PER * i + k + 1)
                v.wait_ge(self.s_out[k], 16 * i)
                v.tensor_tensor(self.y[:, k], bank[:, 0:D], self.b2[:, last[k][0]], ALU.add).then_inc(self.s_y, 1)

    def sync(self, s):
        s.dma_start(self.b1[:, :, :], self.A.f1_b1).then_inc(self.s_b, 16)
        for e in range(E1):
            s.dma_start(self.b2[:, e], spread(self.A.f1_b2[e])).then_inc(self.s_b, 16)
        s.wait_ge(self.s_b, 16 * (1 + E1))
        for e in range(E1):
            s.dma_start(self.w1[:, e], rows(self.A.f1_w1[e])).then_inc(self.s_w, 16)
            s.dma_start(self.w2[:, e], rows(self.A.f1_w2[e])).then_inc(self.s_w, 16)
        for k in range(self.PER):
            s.sem_inc(self.s_out[k], 16)

        for lo, hi, now in self.pieces():
            with s.Fori(lo, hi) as i:
                for k in range(len(now)):
                    n = self.PER * i + k
                    s.wait_ge(self.s_y, n + 2 * self.PER + 1)
                    s.dma_start(self.R.ydram[:, bass.ds(n, 1), :].rearrange("p a d -> p (a d)"), self.y[:, k])\
                        .then_inc(self.s_out[k], 16)
        for k in range(self.PER):
            s.wait_ge(self.s_out[k], 16 * (1 + sum(hi - lo for lo, hi, now in self.pieces() if k < len(now))))


def combine1(nc, R, A, out):
    PER = E1 - 1
    with Phase(nc, "exp1") as f:
        ya = f.sb("ya", [P, 2, PER * TPI, D])
        yb = f.sb("yb", [P, 2, TPI, D])
        s_a, s_out = f.sem("a"), f.sem("out")
        s_in = [f.sem(f"in{h}") for h in range(2)]
        with nc.Block() as block:
            @block.sync
            def _(s):
                for i in range(ITER + 1):
                    if i < ITER:
                        if i >= 2:
                            s.wait_ge(s_a, TPI * E1 * (i - 1))
                        s.dma_start(ya[:, i % 2], R.ydram[:, PER * TPI * i:PER * TPI * (i + 1), :])\
                            .then_inc(s_in[i % 2], 16)
                        o = PER * W + TPI * i
                        s.dma_start(yb[:, i % 2], R.ydram[:, o:o + TPI, :]).then_inc(s_in[i % 2], 16)
                    if i >= 1:
                        s.wait_ge(s_a, TPI * E1 * i)
                        o = TPI * (i - 1)
                        n = min(TPI, W - 1 - o)
                        s.dma_start(out[o * P:(o + n) * P, :].rearrange("(t p) d -> p t d", p=P),
                                    R.X[:, o:o + n, :]).then_inc(s_out, 16)
                s.dma_start(out[(W - 1) * P:N, :], R.X[0:N - (W - 1) * P, W - 1, :]).then_inc(s_out, 16)
                s.wait_ge(s_out, 16 * (ITER + 1))

            @block.vector
            def _(v):
                for i in range(ITER):
                    v.wait_ge(s_in[i % 2], 32 * (i // 2 + 1))
                    for e in range(E1):
                        for j in range(TPI):
                            t = TPI * i + j
                            n = TPI * E1 * i + TPI * e + j
                            if e:
                                v.wait_ge(s_a, n - TPI + 1)
                            y = ya[:, i % 2, PER * j + e] if e < PER else yb[:, i % 2, j]
                            v.scalar_tensor_tensor(R.X[:, t], y, R.gate[:, t, e:e + 1], R.X[:, t], ALU.mult, ALU.add)\
                                .then_inc(s_a, 1)



class Shared:
    pass


def build(nc, A, out):
    R = Shared()
    R.tab0 = nc.dram_tensor("tab0", [NP, GCN], F32).ap()
    R.tab1 = nc.dram_tensor("tab1", [NP, GROW], F32).ap()
    R.tabr = nc.dram_tensor("tabr", [NP, FROW], F32).ap()
    R.fsorted = nc.dram_tensor("fsorted", [FE, 2], I32).ap()
    R.ydram = nc.dram_tensor("ydram", [P, E1 * W, D], F32).ap()
    R.wdram = nc.dram_tensor("wdram", [16 * P], I32).ap()
    GT, FT = -(-(GSLOTS + TURN) // P) * P, -(-(FSLOTS + TURN) // P) * P
    with Phase(nc, "all") as f:
        R.ident = f.sb("ident", [P, P])
        R.identb = f.sb("identb", [P, P], BF16)
        R.iota = f.sb("iota", [P, P])
        R.ones = f.sb("ones", [P, P])
        R.mask = f.sb("mask", [P, W])
        R.X = f.sb("X", [P, W, D])
        R.XT = f.sb("XT", [P, C, NP])
        R.weff = f.sb("weff", [P, C, D])
        R.beff = f.sb("beff", [P, C])
        R.kvsum = f.sb("kvsum", [P, 512])
        R.fstart = f.sb("fstart", [P, W])
        R.gmax = f.sb("gmax", [P, GH])
        R.gmaxa = f.sb("gmaxa", [P, GH])
        R.gate = f.sb("gate", [P, W, E0])
        constants(nc, R)
        with Phase(nc, "graph") as g:
            R.gstart = g.sb("gstart", [P, W])
            R.nsrc = g.sb("nsrc", [P, W])
            R.adst = g.sb("adst", [P, W, GH])
            R.gsrc = g.sb("gsrc", [P, GT])
            R.gdst = g.sb("gdst", [P, GT])
            R.gwin = g.sb("gwin", [1, GT], I32)
            R.gwinn = g.sb("gwinn", [1, GT], I32)
            with Phase(nc, "fedge") as fe:
                R.frec = fe.sb("frec", [P, FB, 2], I32)
                R.fpos = fe.sb("fpos", [P, FB])
                degrees(nc, R, A)
                slot_tables(nc, R, "gslot", R.gstart, A.grec, GB, GT, R.gsrc, R.gdst, R.gwin, R.gwinn)
                kv_phase(nc, R, A, 0)
                fold0(nc, R, A)
                with Phase(nc, "gcn") as h:
                    R.gcn = h.sb("sum", [P, W, GCN + 1])
                    clear(nc, R.gcn[:, :, :])
                    edges(nc, R, "gcne", R.tab0, GSLOTS, R.gsrc, R.gdst, R.gwin, R.gwinn, R.gcn,
                          beside=Layer0Work(nc, R, A))
                    gcn_finish(nc, R, A)
                gates0(nc, R, A)
                experts0(nc, R, A)
            kv_phase(nc, R, A, 1)
            fold1(nc, R, A)
            with Phase(nc, "gat") as h:
                R.gat = h.sb("sum", [P, W, GROW])
                gat3 = h.sb("adst3", [P, W, 3 * GH], BF16)
                loops(nc, R, "gloop", R.tab1, R.gat, GH, GC, R.adst, gat3, R.gmaxa)
                edges(nc, R, "gate", R.tab1, GSLOTS, R.gsrc, R.gdst, R.gwin, R.gwinn, R.gat, GH, GC, gat3, R.gmaxa)
                finish1(nc, R, A)
        with Phase(nc, "router") as g:
            R.rsrc = g.sb("rsrc", [P, FT])
            R.rdrel = g.sb("rdrel", [P, FT])
            R.rwin = g.sb("rwin", [1, FT], I32)
            R.rwinn = g.sb("rwinn", [1, FT], I32)
            R.rext = g.sb("rext", [P, W, FROW + FH])
            R.rdst = g.sb("rdst", [P, W, FH])
            R.rmax = g.sb("rmax", [P, FH])
            R.racc = g.sb("racc", [P, W, 3 * FROW])
            rdst3 = g.sb("rdst3", [P, W, 3 * FH], BF16)
            router_table(nc, R, A)
            slot_tables(nc, R, "fslot", R.fstart, R.fsorted.rearrange("(b e) k -> b (e k)", e=P), FB, FT, R.rsrc,
                        R.rdrel, R.rwin, R.rwinn)
            loops(nc, R, "rloop", R.tabr, R.racc, FH, FC, R.rdst, rdst3, R.rmax)
            edges(nc, R, "rtr", R.tabr, FSLOTS, R.rsrc, R.rdrel, R.rwin, R.rwinn, R.racc, FH, FC, rdst3, R.rmax,
                  split=True, beside=Experts1(nc, R, A))
            router_gates(nc, R, A)
            combine1(nc, R, A, out)


def kernel(**inputs):
    import numpy as np
    import concourse.bacc as bacc
    from concourse.bass_utils import run_bass_kernel_spmd as run

    g = {k: np.asarray(v) for k, v in inputs.items()}
    pad = np.full(GB * P - GE, PAD_NODE, np.int32)
    src, dst = np.concatenate([g["src"], pad]), np.concatenate([g["dst"], pad])
    qkv0 = g["L0_mix_w_qkv"].reshape(D, HEADS, 3, HC0)
    bqkv0 = g["L0_mix_b_qkv"].reshape(HEADS, 3, HC0)
    qkv1 = g["L1_mix_w_qkv"]
    inner = HEADS * HC1

    def cols(b):
        return b.reshape(-1, P).T

    bn = [[g[f"L0_ffn_{n}{k}"].reshape(E0 * C, P).T for n in ("b", "g", "be", "m", "v")] for k in (1, 2)]
    given = dict(
        x=g["x"],
        gsrc_t=src.reshape(GB, P).T, gdst_t=dst.reshape(GB, P).T,
        grec=np.stack([src, dst], -1).reshape(GB, 2 * P),
        ffn_edges=g["L1_ffn_edge_index"].T.reshape(P, FB, 2),
        gcn_w=g["L0_gnn_W_gcn"], gcn_b=g["L0_gnn_b_gcn"], gcn_wout=g["L0_gnn_W_out"], gcn_bout=g["L0_gnn_b_out"][None],
        m0_kv=np.concatenate([qkv0[:, :, 1].reshape(D, D), qkv0[:, :, 2].reshape(D, D)], 1),
        m0_wqt=qkv0[:, :, 0].reshape(D, D).T,
        m0_bkv=np.concatenate([bqkv0[:, 1].reshape(D), bqkv0[:, 2].reshape(D)]),
        m0_bq_t=cols(bqkv0[:, 0].reshape(D)),
        m0_gam=np.stack([g["L0_mix_kln_g"], g["L0_mix_vln_g"]]), m0_bet=np.stack([g["L0_mix_kln_b"], g["L0_mix_vln_b"]]),
        m0_w1=g["L0_mix_w1"], m0_b1_t=cols(g["L0_mix_b1"]), m0_w2=g["L0_mix_w2"], m0_b2=g["L0_mix_b2"][None],
        f0_wr=g["L0_ffn_Wr"], f0_br=g["L0_ffn_br"], f0_w1=g["L0_ffn_W1"], f0_w2=g["L0_ffn_W2"], f0_wo=g["L0_ffn_Wo"],
        f0_bo=g["L0_ffn_bo"], f0_bn=np.stack([np.stack(k, 1) for k in bn], 1),
        gat_w=g["L1_gnn_W"], gat_src=g["L1_gnn_att_src"].reshape(-1), gat_dst=g["L1_gnn_att_dst"].reshape(-1),
        gat_bias=g["L1_gnn_bias"][None],
        m1_kv=qkv1[:, inner:], m1_wqt=qkv1[:, :inner].T, m1_wout=g["L1_mix_w_out"], m1_bout=g["L1_mix_b_out"][None],
        r_w=g["L1_ffn_W_gat"], r_src=g["L1_ffn_att_src"].reshape(-1), r_dst=g["L1_ffn_att_dst"].reshape(-1),
        r_b=g["L1_ffn_b_gat"], r_gam=g["L1_ffn_ln_gamma"], r_bet=g["L1_ffn_ln_beta"],
        f1_w1=g["L1_ffn_W1"], f1_b1=g["L1_ffn_b1"].reshape(E1, -1, P).transpose(2, 0, 1), f1_w2=g["L1_ffn_W2"],
        f1_b2=g["L1_ffn_b2"],
    )
    nc = bacc.Bacc("TRN2", target_bir_lowering=False, num_devices=1)
    arrays, A = {}, Shared()
    for name, a in given.items():
        a = np.ascontiguousarray(a)
        arrays[f"in_{name}"] = a
        A.__dict__[name] = nc.dram_tensor(f"in_{name}", a.shape, mybir.dt.from_np(a.dtype), kind="ExternalInput").ap()
    out = nc.dram_tensor("out", [N, D], F32, kind="ExternalOutput").ap()
    build(nc, A, out)
    r = run(nc, [arrays], core_ids=[0])
    return r.results[0]["out"]
```

```python
from contextlib import ExitStack

import concourse.bass as bass
from concourse import mybir

F32 = mybir.dt.float32
BF16 = mybir.dt.bfloat16
I32 = mybir.dt.int32
U32 = mybir.dt.uint32
ALU = mybir.AluOpType
ACT = mybir.ActivationFunctionType
AXX = mybir.AxisListType.X
ENG = mybir.EngineType

P = 128
N = 6250
D = 256
C = D // P
W = -(-N // P)
NP = W * P
TPI = 7
ITER = W // TPI
TOK = TPI * P
HALF = TOK // 2
assert W % TPI == 0 and HALF <= 512

HEADS = 8
HC0 = 32
HC1 = 64
GCN = 64
GH, GC = 8, 32
GROW = GH * GC + GH
E0, E1 = 8, 4
HID1 = 512
FH, FC = 4, 4
FROW = FH * FC + FH
LN_EPS = 1e-5
BN_EPS = 1e-3

GE = 50000 * 2 + N
GB = 832
FE = 131072
FB = FE // P
PAD_NODE = 8192
GROUP = 4
NBUF = 4
TURN = NBUF * GROUP
GROUP8 = 8
GSLOTS = -(-(GB + W - 1) // TURN) * TURN
FSLOTS = -(-(FB + W - 1) // TURN) * TURN
SCATTERS = FB // (2 * GROUP8)
SCATTERG = 4
SCATTER0 = 8
assert GB * P >= GE


class Phase:

    def __init__(self, nc, tag):
        self.nc, self.tag, self.ctx, self.sems = nc, tag, ExitStack(), []

    def __enter__(self):
        return self

    def __exit__(self, *a):
        if self.sems:
            self.nc.clear_and_free_semaphores(self.sems)
            self.nc.all_engine_barrier()
        self.ctx.close()

    def sb(self, name, shape, dt=F32):
        return self.ctx.enter_context(self.nc.sbuf_tensor(f"{self.tag}_{name}", shape, dt))

    def ps(self, name, shape, dt=F32):
        return self.ctx.enter_context(self.nc.psum_tensor(f"{self.tag}_{name}", shape, dt))

    def sem(self, name):
        self.sems.append(self.nc.alloc_semaphore(f"{self.tag}_{name}"))
        return self.sems[-1]


class Steps:

    def __init__(self, eng, sem, start=0):
        self.eng, self.sem, self.n = eng, sem, start

    def then(self, ins):
        ins.then_inc(self.sem, 1)
        self.n += 1
        self.eng.wait_ge(self.sem, self.n)


def rows(ap):
    return ap.rearrange("(c p) n -> p c n", p=P)


def spread(ap, n=P):
    return ap.partition_broadcast(n)



def constants(nc, R):
    with Phase(nc, "cst") as f:
        made = f.sem("made")
        row_i = f.sb("row_i", [P, P], I32)
        with nc.Block() as block:
            @block.gpsimd
            def _(g):
                st = Steps(g, made)
                st.then(g.memset(R.ident[:, :], 0.0))
                st.then(g.affine_select(out=R.ident[:, :], in_=R.ident[:, :], compare_op=ALU.not_equal, fill=1.0,
                                        base=0, pattern=[[-1, P]], channel_multiplier=1))
                st.then(g.tensor_copy(R.identb[:, :], R.ident[:, :]))
                st.then(g.iota(row_i[:, :], pattern=[[1, P]], base=0, channel_multiplier=0))
                st.then(g.tensor_copy(R.iota[:, :], row_i[:, :]))
                st.then(g.memset(R.ones[:, :], 1.0))
                st.then(g.memset(R.mask[:, :], 1.0))
                st.then(g.affine_select(out=R.mask[:, W - 1:W], in_=R.mask[:, W - 1:W], compare_op=ALU.is_ge, fill=0.0,
                                        base=N - (W - 1) * P - 1, pattern=[[0, 1]], channel_multiplier=-1))



def degrees(nc, R, A):
    BAT = 16
    TURNS = GB // (2 * BAT)
    with Phase(nc, "deg") as f:
        si = f.sb("si", [P, GB], I32)
        di = f.sb("di", [P, GB], I32)
        part = f.sb("part", [P, GB], I32)
        lo = f.sb("lo", [P, GB], BF16)
        hi = f.sb("hi", [P, GB], BF16)
        count = f.sb("count", [P, P, BAT], BF16)
        dstw = f.sb("dstw", [P, GB], BF16)
        junk = f.sb("junk", [P, GB], BF16)
        cnt = f.sb("cnt", [P, W])
        ohlo = f.sb("ohlo", [P, 2, P, BAT], BF16)
        ohhi = f.sb("ohhi", [P, 2, W, BAT], BF16)
        deg = f.ps("deg", [P, 512])
        total = f.ps("total", [P, 512])
        zero = f.sb("zero", [P, P], BF16)
        loaded, step, hot, used, zeroed, counted, summed, rooted = (
            f.sem(n) for n in ("loaded", "step", "hot", "used", "zeroed", "counted", "summed", "rooted"))
        std = f.sb("std", [P, W])
        with nc.Block() as block:
            @block.sync
            def _(s):
                s.dma_start(si[:, :], A.gsrc_t).then_inc(loaded, 16)
                s.dma_start(di[:, :], A.gdst_t).then_inc(loaded, 16)

            @block.vector
            def _(v):
                st = Steps(v, step)
                v.memset(zero[:, :], 0.0).then_inc(zeroed, 1)
                st.then(v.tensor_copy(count[:, :, :], R.iota[:, :].unsqueeze(2).to_broadcast([P, P, BAT])))
                v.wait_ge(loaded, 32)
                st.then(v.tensor_scalar(part[:, :], si[:, :], P - 1, None, ALU.bitwise_and))
                st.then(v.tensor_copy(lo[:, :], part[:, :]))
                st.then(v.tensor_scalar(part[:, :], si[:, :], 7, None, ALU.arith_shift_right))
                st.then(v.tensor_copy(hi[:, :], part[:, :]))
                st.then(v.tensor_scalar(part[:, :], di[:, :], 7, None, ALU.arith_shift_right))
                st.then(v.tensor_copy(dstw[:, :], part[:, :]))
                with v.Fori(0, TURNS) as i:
                    for g in range(2):
                        v.wait_ge(used, 2 * i)
                        col = (2 * i + g) * BAT
                        v.tensor_tensor(ohlo[:, g], count[:, :, :],
                                        lo[:, bass.ds(col, BAT)].unsqueeze(1).to_broadcast([P, P, BAT]),
                                        ALU.is_equal).then_inc(hot, 1)
                        v.tensor_tensor(ohhi[:, g], count[:, 0:W, :],
                                        hi[:, bass.ds(col, BAT)].unsqueeze(1).to_broadcast([P, W, BAT]),
                                        ALU.is_equal).then_inc(hot, 1)
                for w in range(W):
                    st.then(v.tensor_scalar(junk[:, :], dstw[:, :], float(w), None, ALU.is_lt, ALU.add,
                                            accum_out=cnt[:, w:w + 1]))
                v.sem_inc(counted, 1)
                v.wait_ge(summed, 1)
                st.then(v.tensor_copy(R.gstart[:, :], total[:, 0:W]))
                st.then(v.tensor_scalar(std[:, :], deg[:, 0:W], 1.0, None, ALU.max))
                v.sem_inc(counted, 1)
                v.wait_ge(rooted, 1)
                v.reciprocal(R.nsrc[:, :], std[:, :])

            @block.scalar
            def _(a):
                a.wait_ge(counted, 2)
                a.activation(std[:, :], std[:, :], ACT.Sqrt).then_inc(rooted, 1)

            @block.tensor
            def _(t):
                t.wait_ge(zeroed, 1)
                t.matmul(deg[:, 0:W], zero[:, :], zero[:, 0:W], start=True, stop=False, skip_group_check=True)
                with t.Fori(0, TURNS) as i:
                    for g in range(2):
                        t.wait_ge(hot, 4 * i + 2 * g + 2)
                        for b in range(BAT):
                            mm = t.matmul(deg[:, 0:W], ohlo[:, g, :, b], ohhi[:, g, :, b], start=False, stop=False,
                                          skip_group_check=True)
                        mm.then_inc(used, 1)
                t.wait_ge(counted, 1)
                t.matmul(total[:, 0:W], R.ones[:, :], cnt[:, :], start=True, stop=True).then_inc(summed, 1)



def slot_tables(nc, R, tag, start, rec, nblocks, nslots, src_ix, dst_rel, wtab, wnext):
    J = -(-nslots // P)
    with Phase(nc, tag) as f:
        si = f.sb("si", [P, W], I32)
        sf = f.sb("sf", [P, W])
        iw = f.sb("iw", [P, W], I32)
        slot_i = f.sb("slot_i", [P, J], I32)
        slot = f.sb("slot", [P, J])
        cmp = f.sb("cmp", [P, J, W - 1])
        win = f.sb("win", [P, J])
        blk = f.sb("blk", [P, J])
        off = f.sb("off", [P, J])
        blk_i = f.sb("blk_i", [P, J], U32)
        win_i = f.sb("win_i", [P, J], I32)
        edge = f.sb("edge", [P, J, P, 2], I32)
        srcf = f.sb("srcf", [P, J, P])
        dstf = f.sb("dstf", [P, J, P])
        pt = f.ps("pt", [P, 4, 512])
        made, step, tabbed, gathered, split, turned, put, wout, win_done = (
            f.sem(n) for n in ("made", "step", "tabbed", "gathered", "split", "turned", "put", "wout", "win_done"))
        gath = [f.sem(f"gath{j}") for j in range(J)]
        with nc.Block() as block:
            @block.gpsimd
            def _(g):
                g.iota(slot_i[:, :], pattern=[[P, J]], base=0, channel_multiplier=1).then_inc(made, 1)
                g.iota(iw[:, :], pattern=[[1, W]], base=0, channel_multiplier=0).then_inc(made, 1)
                g.wait_ge(tabbed, 1)
                for j in range(J):
                    g.indirect_dma_start(edge[:, j].rearrange("p e k -> p (e k)"), None, rec,
                                         bass.IndirectOffsetOnAxis(blk_i[:, j:j + 1], 0)).then_inc(gath[j], 16)

            @block.vector
            def _(v):
                st = Steps(v, step)
                v.wait_ge(made, 2)
                st.then(v.tensor_copy(slot[:, :], slot_i[:, :]))
                st.then(v.tensor_copy(si[:, :], start[:, :]))
                st.then(v.tensor_scalar(si[:, :], si[:, :], 7, None, ALU.arith_shift_right))
                st.then(v.tensor_tensor(sf[:, :], si[:, :], iw[:, :], ALU.add))
                st.then(v.tensor_tensor(cmp[:, :, :], sf[:, 1:W].unsqueeze(1).to_broadcast([P, J, W - 1]),
                                        slot[:, :].unsqueeze(2).to_broadcast([P, J, W - 1]), ALU.is_le))
                st.then(v.tensor_reduce(win[:, :], cmp[:, :, :], AXX, ALU.add))
                st.then(v.tensor_tensor(blk[:, :], slot[:, :], win[:, :], ALU.subtract))
                st.then(v.tensor_scalar(blk_i[:, :], blk[:, :], float(nblocks - 1), None, ALU.min))
                st.then(v.tensor_copy(win_i[:, :], win[:, :]))
                st.then(v.tensor_scalar(off[:, :], blk[:, :], float(nblocks), -float(1 << 22), ALU.is_ge, ALU.mult))
                st.then(v.scalar_tensor_tensor(off[:, :], win[:, :], float(P), off[:, :], ALU.mult, ALU.add))
                v.sem_inc(tabbed, 1)
                for j in range(J):
                    v.wait_ge(gath[j], 16)
                    v.tensor_scalar(srcf[:, j], edge[:, j, :, 0], float(N - 1), None, ALU.min).then_inc(split, 1)
                    v.tensor_scalar(dstf[:, j], edge[:, j, :, 1], off[:, j:j + 1], None,
                                    ALU.subtract).then_inc(split, 1)
                for j in range(J):
                    v.wait_ge(turned, j + 1)
                    v.tensor_copy(src_ix[:, j * P:(j + 1) * P], pt[:, 2 * (j % 2), 0:P]).then_inc(put, 1)
                    v.tensor_copy(dst_rel[:, j * P:(j + 1) * P], pt[:, 2 * (j % 2) + 1, 0:P]).then_inc(put, 1)

            @block.tensor
            def _(t):
                for j in range(J):
                    t.wait_ge(split, 2 * (j + 1))
                    if j >= 2:
                        t.wait_ge(put, 2 * (j - 1))
                    t.transpose(pt[:, 2 * (j % 2), 0:P], srcf[:, j], R.ident[:, :])
                    t.transpose(pt[:, 2 * (j % 2) + 1, 0:P], dstf[:, j], R.ident[:, :]).then_inc(turned, 1)

            @block.sync
            def _(s):
                s.wait_ge(tabbed, 1)
                with nc.allow_non_contiguous_dma(reason="one number per slot, once"):
                    s.dma_start(R.wdram[0:J * P].rearrange("(j p) -> p j", p=P), win_i[:, :]).then_inc(wout, 16)
                s.wait_ge(wout, 16)
                s.dma_start(wtab[0:1, :], R.wdram[0:J * P].unsqueeze(0)).then_inc(wout, 16)
                s.dma_start(wnext[0:1, 0:J * P - 2 * GROUP], R.wdram[2 * GROUP:J * P].unsqueeze(0)).then_inc(wout, 16)
                s.wait_ge(wout, 48)



class Norm:

    def __init__(self, f, R):
        self.R = R
        self.stats = f.sb("stats", [P, TPI, 6])
        self.mv = f.sb("mv", [P, TPI, 2])
        self.var = f.sb("var", [P, TPI])
        self.std = f.sb("std", [P, TPI])
        self.rstd = f.sb("rstd", [P, TPI])
        self.xn = f.sb("xn", [P, TPI, D])
        self.xt = f.sb("xt", [P, TPI, C, P])
        self.pt = f.ps("pt", [P, 2, 512])
        self.s_stat, self.s_mv, self.s_var, self.s_std, self.s_rstd = (
            f.sem(n) for n in ("stat", "mv", "var", "std", "rstd"))
        self.s_seen = f.sem("seen")
        self.s_xn, self.s_tp, self.s_xt, self.s_xr = (f.sem(n) for n in ("xn", "tp", "xt", "xr"))

    def statistics(self, v, i):
        for j in range(TPI):
            self.tile_statistics(v, i, j)
        self.aggregate(v, i)

    def tile_statistics(self, v, i, j):
        v.bn_stats(self.stats[:, j], xtile(self.R, TPI * i + j)).then_inc(self.s_stat, 1)

    def aggregate(self, v, i):
        v.wait_ge(self.s_stat, TPI * i + TPI)
        v.sem_inc(self.s_seen, 1)
        for j in range(TPI):
            v.bn_aggr(self.mv[:, j], self.stats[:, j]).then_inc(self.s_mv, 1)
        v.wait_ge(self.s_mv, TPI * i + TPI)
        v.tensor_scalar(self.var[:, :], self.mv[:, :, 1], LN_EPS, None, ALU.add).then_inc(self.s_var, 1)

    def normalise(self, v, i):
        R = self.R
        v.wait_ge(self.s_std, i + 1)
        v.reciprocal(self.rstd[:, :], self.std[:, :]).then_inc(self.s_rstd, 1)
        v.wait_ge(self.s_rstd, i + 1)
        v.wait_ge(self.s_tp, TPI * i)
        for j in range(TPI):
            v.tensor_scalar(self.xn[:, j], xtile(R, TPI * i + j), self.mv[:, j, 0:1], self.rstd[:, j:j + 1],
                            ALU.subtract, ALU.mult).then_inc(self.s_xn, 1)

    @staticmethod
    def turns(engine, turn):
        with engine.Fori(0, ITER - 1) as i:
            turn(i, True)
        turn(ITER - 1, False)

    def scalar_root(self, a, i):
        a.wait_ge(self.s_var, i + 1)
        a.activation(self.std[:, :], self.var[:, :], ACT.Sqrt).then_inc(self.s_std, 1)

    def scalar_copy(self, a, i, j):
        a.wait_ge(self.s_tp, TPI * i + j + 1)
        src = self.pt[:, j % 2, 0:C * P].rearrange("p (c t) -> p c t", c=C)
        a.activation(self.xt[:, j], src, ACT.Copy).then_inc(self.s_xt, 1)
        a.activation(self.R.XT[:, :, bass.ds((TPI * i + j) * P, P)], src, ACT.Copy).then_inc(self.s_xr, 1)

    def tensor(self, t, i, j):
        t.wait_ge(self.s_xn, TPI * i + j + 1)
        t.wait_ge(self.s_xr, TPI * i + (j - 1 if j >= 2 else 0))
        for c in range(C):
            mm = t.transpose(self.pt[:, j % 2, c * P:(c + 1) * P], self.xn[:, j, c * P:(c + 1) * P], self.R.ident[:, :])
        mm.then_inc(self.s_tp, 1)


def kv_phase(nc, R, A, L):
    first = L == 0
    hd = HC0 if first else HC1
    G = 2 * HEADS
    KV = G * hd
    NB_KV = KV // 512
    EXT = GCN if first else GH * GC + 2 * GH
    TAB = GCN if first else GROW
    PAIRS = KV // 2 // P
    wkv_d, ext_d, tab_d = (A.m0_kv, A.gcn_w, R.tab0) if first else (A.m1_kv, A.gat_w, R.tab1)
    with Phase(nc, f"kv{L}") as f:
        nm = Norm(f, R)
        wkv = f.sb("wkv", [P, C, KV])
        wext = f.sb("wext", [P, C, EXT])
        gsum = f.sb("gsum", [P, C, G])
        kc = f.sb("kc", [P, TPI, KV])
        sq = f.sb("sq", [P, KV])
        ssum = f.sb("ssum", [P, TPI, G])
        sstd = f.sb("sstd", [P, TPI, G])
        srs = f.sb("srs", [P, TPI, G])
        ext = f.sb("ext", [P, TPI, EXT])
        tabt = f.sb("tabt", [P, TPI, TAB])
        zero = f.sb("zero", [P, 512], BF16)
        if first:
            bias = f.sb("bias", [P, KV])
            bsum = f.sb("bsum", [P, G])
            gam = f.sb("gam", [P, KV])
            bet = f.sb("bet", [P, KV])
            blast = f.sb("blast", [P, KV])
        else:
            att = f.sb("att", [P, 2, GH * GC])
            wa = f.sb("wa", [P, GH * GC])
        pkv = f.ps("pkv", [P, 4 // NB_KV if NB_KV > 1 else 2, NB_KV, 512])
        pext = f.ps("pext", [P, 512])
        pacc = f.ps("pacc", [P, 512])
        s_w, s_st, s_z, s_ready, s_x = (f.sem(n) for n in ("w", "st", "z", "ready", "x"))
        s_kvp, s_kc, s_sq, s_red, s_ve, s_sd, s_r2, s_rm = (
            f.sem(n) for n in ("kvp", "kc", "sq", "red", "ve", "sd", "r2", "rm"))
        s_k1, s_k2, s_k3, s_kv, s_ep, s_ec, s_tab, s_tab_d, s_out, s_acc, s_gm = (
            f.sem(n) for n in ("k1", "k2", "k3", "kv", "ep", "ec", "tab", "tabd", "out", "acc", "gm"))
        s_xa = f.sem("xa")
        s_kdone = s_k3 if first else s_k1
        loads = 6 if first else 4
        with nc.Block() as block:
            @block.sync
            def _(s):
                s.dma_start(wkv[:, :, :], rows(wkv_d)).then_inc(s_w, 16)
                s.dma_start(wext[:, :, 0:ext_d.shape[1]], rows(ext_d)).then_inc(s_w, 16)
                if first:
                    s.dma_start(bias[:, :], spread(A.m0_bkv)).then_inc(s_w, 16)
                    for tile, row in ((gam, A.m0_gam), (bet, A.m0_bet)):
                        for k in range(2):
                            s.dma_start(tile[:, k * KV // 2:k * KV // 2 + hd], spread(row[k])).then_inc(s_w, 16)
                    s.wait_ge(s_z, 2)
                    full = W - 1
                    s.dma_start(R.X[:, 0:full, :], A.x[0:full * P, :].rearrange("(t p) d -> p t d", p=P))\
                        .then_inc(s_x, 16)
                    s.dma_start(R.X[0:N - full * P, full, :], A.x[full * P:N, :]).then_inc(s_x, 16)
                else:
                    for k, row in enumerate((A.gat_src, A.gat_dst)):
                        s.dma_start(att[:, k, :], spread(row)).then_inc(s_w, 16)
                with s.Fori(0, ITER) as i:
                    s.wait_ge(s_tab, i + 1)
                    s.dma_start(tab_d[bass.ds(i * TOK, TOK), :].rearrange("(t p) d -> p t d", p=P), tabt[:, :, :])\
                        .then_inc(s_out, 16)
                s.wait_ge(s_out, 16 * ITER)

            if first:
                @block.gpsimd
                def _(g):
                    def turn(i, more):
                        for j in range(TPI):
                            g.wait_ge(nm.s_xn, TPI * i + j + 1)
                            xj = xtile(R, TPI * i + j)
                            g.tensor_tensor(xj, xj, nm.xn[:, j], ALU.add).then_inc(s_xa, 1)
                        for j in range(TPI):
                            n = TPI * i + j
                            g.wait_ge(s_k1, n + 1)
                            g.tensor_tensor(kc[:, j], kc[:, j], gam[:, :], ALU.mult).then_inc(s_k2, 1)
                            g.wait_ge(s_k2, n + 1)
                            shift = bet if more or j + 1 < TPI else blast
                            g.tensor_tensor(kc[:, j], kc[:, j], shift[:, :], ALU.add).then_inc(s_k3, 1)

                    g.wait_ge(s_ready, 1)
                    nm.turns(g, turn)

            @block.vector
            def _(v):
                st = Steps(v, s_st)
                v.memset(zero[:, :], 0.0).then_inc(s_z, 1)
                if first:
                    v.memset(R.X[:, W - 1, :], 0.0).then_inc(s_z, 1)
                v.wait_ge(s_w, 16 * (7 if first else 4))
                if first:
                    for tile in (gam, bet):
                        for k in range(2):
                            o = k * KV // 2
                            for m in (1, 2, 4):
                                st.then(v.tensor_copy(tile[:, o + m * hd:o + 2 * m * hd], tile[:, o:o + m * hd]))
                for c in range(C):
                    v3 = wkv[:, c, :].rearrange("p (g e) -> p g e", g=G)
                    st.then(v.tensor_reduce(gsum[:, c, :], v3, AXX, ALU.add))
                    st.then(v.tensor_scalar(gsum[:, c, :], gsum[:, c, :], 1.0 / hd, None, ALU.mult))
                    st.then(v.tensor_tensor(v3, v3, gsum[:, c, :].unsqueeze(2).to_broadcast([P, G, hd]), ALU.subtract))
                if first:
                    st.then(v.tensor_scalar(blast[:, :], bet[:, :], R.mask[:, W - 1:W], None, ALU.mult))
                    b3 = bias[:, :].rearrange("p (g e) -> p g e", g=G)
                    st.then(v.tensor_reduce(bsum[:, :], b3, AXX, ALU.add))
                    st.then(v.tensor_scalar(bsum[:, :], bsum[:, :], 1.0 / hd, None, ALU.mult))
                    st.then(v.tensor_tensor(b3, b3, bsum[:, :].unsqueeze(2).to_broadcast([P, G, hd]), ALU.subtract))
                    v.wait_ge(s_x, 32)
                else:
                    for c in range(C):
                        for k in range(2):
                            st.then(v.tensor_tensor(wa[:, :], wext[:, c, 0:GH * GC], att[:, k, :], ALU.mult))
                            o = GH * GC + k * GH
                            st.then(v.tensor_reduce(wext[:, c, o:o + GH],
                                                    wa[:, :].rearrange("p (h c) -> p h c", h=GH), AXX, ALU.add))
                    st.then(v.memset(R.gmax[:, :], -3.0e38))
                v.sem_inc(s_ready, 1)
                nm.statistics(v, 0)
                nm.normalise(v, 0)

                def turn(i, more):
                    def weigh(j):
                        n = TPI * i + j
                        v.wait_ge(s_sd, n + 1)
                        v.reciprocal(srs[:, j], sstd[:, j]).then_inc(s_r2, 1)
                        v.wait_ge(s_r2, n + 1)
                        v.tensor_tensor(srs[:, j], srs[:, j], R.mask[:, bass.ds(n, 1)].to_broadcast([P, G]),
                                        ALU.mult).then_inc(s_rm, 1)
                        v.wait_ge(s_rm, n + 1)
                        k3 = kc[:, j].rearrange("p (g e) -> p g e", g=G)
                        v.tensor_tensor(k3, k3, srs[:, j].unsqueeze(2).to_broadcast([P, G, hd]),
                                        ALU.mult).then_inc(s_k1, 1)

                    if first:
                        v.wait_ge(s_kv, i)
                    for j in range(TPI):
                        if first:
                            v.wait_ge(s_kvp, TPI * i + j + 1)
                            v.tensor_tensor(kc[:, j], pkv[:, j % 2].rearrange("p b n -> p (b n)"), bias[:, :],
                                            ALU.add).then_inc(s_kc, 1)
                        if more:
                            nm.tile_statistics(v, i + 1, j)
                        if j >= 2:
                            weigh(j - 2)
                        v.wait_ge(s_sq, TPI * i + j + 1)
                        v.tensor_reduce(ssum[:, j], sq[:, :].rearrange("p (g e) -> p g e", g=G), AXX,
                                        ALU.add).then_inc(s_red, 1)
                        v.wait_ge(s_red, TPI * i + j + 1)
                        v.tensor_scalar(ssum[:, j], ssum[:, j], 1.0 / hd, LN_EPS, ALU.mult, ALU.add).then_inc(s_ve, 1)
                    if more:
                        nm.aggregate(v, i + 1)
                    weigh(TPI - 2)
                    weigh(TPI - 1)
                    if more:
                        if first:
                            v.wait_ge(s_xa, TPI * i + TPI)
                        nm.normalise(v, i + 1)
                    v.wait_ge(s_ec, TPI * i + TPI)
                    v.wait_ge(s_out, 16 * i)
                    if first:
                        v.tensor_tensor(tabt[:, :, :], ext[:, :, :],
                                        R.nsrc[:, bass.ds(TPI * i, TPI)].unsqueeze(2).to_broadcast([P, TPI, GCN]),
                                        ALU.mult).then_inc(s_tab, 1)
                    else:
                        v.tensor_copy(tabt[:, :, :], ext[:, :, 0:TAB]).then_inc(s_tab, 1)
                        v.tensor_copy(R.adst[:, bass.ds(TPI * i, TPI), :], ext[:, :, TAB:EXT]).then_inc(s_tab_d, 1)
                        for j in range(TPI):
                            v.tensor_tensor(R.gmax[:, :], R.gmax[:, :], ext[:, j, GH * GC:TAB],
                                            ALU.max).then_inc(s_gm, 1)
                            v.wait_ge(s_gm, TPI * i + j + 1)

                nm.turns(v, turn)
                v.wait_ge(s_acc, 1)
                v.tensor_copy(R.kvsum[:, 0:PAIRS * P], pacc[:, 0:PAIRS * P])

            def evac(a, i, j):
                a.wait_ge(s_ep, TPI * i + j + 1)
                a.activation(ext[:, j], pext[:, 0:EXT], ACT.Copy).then_inc(s_ec, 1)
                if not first:
                    if j == 0:
                        a.wait_ge(s_kv, i)
                    a.wait_ge(s_kvp, TPI * i + j + 1)
                    a.activation(kc[:, j], pkv[:, j % 2].rearrange("p b n -> p (b n)"), ACT.Copy).then_inc(s_kc, 1)
                a.wait_ge(s_kc, TPI * i + j + 1)
                a.wait_ge(s_red, TPI * i + j)
                a.activation(sq[:, :], kc[:, j], ACT.Square).then_inc(s_sq, 1)

            @block.scalar
            def _(a):
                nm.scalar_root(a, 0)

                def root(i, j):
                    a.wait_ge(s_ve, TPI * i + j + 1)
                    a.activation(sstd[:, j], ssum[:, j], ACT.Sqrt).then_inc(s_sd, 1)

                def turn(i, more):
                    for j in range(TPI):
                        if j == 0:
                            a.wait_ge(s_ep, TPI * i)
                            a.wait_ge(s_tab, i)
                            if not first:
                                a.wait_ge(s_gm, TPI * i)
                                a.wait_ge(s_tab_d, i)
                        nm.scalar_copy(a, i, j)
                        if j >= 1:
                            evac(a, i, j - 1)
                        if j >= 2:
                            root(i, j - 2)
                    evac(a, i, TPI - 1)
                    root(i, TPI - 2)
                    root(i, TPI - 1)
                    if more:
                        nm.scalar_root(a, i + 1)

                nm.turns(a, turn)

            @block.tensor
            def _(t):
                t.wait_ge(s_z, 1)
                t.matmul(pacc[:, 0:PAIRS * P], zero[:, 0:P], zero[:, 0:PAIRS * P], start=True, stop=False, skip_group_check=True)
                t.wait_ge(s_ready, 1)
                with t.Fori(0, ITER) as i:
                    def outer(j):
                        t.wait_ge(s_kdone, TPI * i + j + 1)
                        for b in range(PAIRS):
                            k = kc[:, j, b * P:(b + 1) * P]
                            u = kc[:, j, KV // 2 + b * P:KV // 2 + (b + 1) * P]
                            if not first:
                                k, u = u, k
                            mm = t.matmul(pacc[:, b * P:(b + 1) * P], k, u, start=False, stop=False,
                                          skip_group_check=True)
                        return mm

                    nm.tensor(t, i, 0)
                    for j in range(TPI):
                        if j + 1 < TPI:
                            nm.tensor(t, i, j + 1)
                        t.wait_ge(nm.s_xt, TPI * i + j + 1)
                        t.wait_ge(s_kc, TPI * i + (j - 1 if j >= 2 else 0))
                        for b in range(NB_KV):
                            for c in range(C):
                                mm = t.matmul(pkv[:, j % 2, b], nm.xt[:, j, c], wkv[:, c, b * 512:(b + 1) * 512],
                                              start=(c == 0), stop=(c == C - 1))
                        mm.then_inc(s_kvp, 1)
                        t.wait_ge(s_ec, TPI * i + j)
                        for c in range(C):
                            mm = t.matmul(pext[:, 0:EXT], nm.xt[:, j, c], wext[:, c, :], start=(c == 0),
                                          stop=(c == C - 1))
                        mm.then_inc(s_ep, 1)
                        if j >= 3:
                            outer(j - 3)
                    for j in range(TPI - 3, TPI):
                        mm = outer(j)
                    mm.then_inc(s_kv, 1)
                t.wait_ge(s_kv, ITER)
                t.sem_inc(s_acc, 1)



def block_mask(g, st, tile, width):
    st.then(g.memset(tile[:, :], 1.0))
    v = tile[:, :].rearrange("p (g e) -> p g e", e=width)
    n = P // width
    st.then(g.affine_select(out=v, in_=v, compare_op=ALU.is_ge, fill=0.0, base=0,
                            pattern=[[-width, n], [0, width]], channel_multiplier=1))
    st.then(g.affine_select(out=v, in_=v, compare_op=ALU.is_ge, fill=0.0, base=width - 1,
                            pattern=[[width, n], [0, width]], channel_multiplier=-1))


def fold0(nc, R, A):
    with Phase(nc, "fold0") as f:
        diag = f.sb("diag", [P, P])
        bd = f.sb("bd", [P, C, P])
        wqt = f.sb("wqt", [P, C, D])
        w1 = f.sb("w1", [P, C, D])
        bq = f.sb("bq", [P, C])
        b1 = f.sb("b1", [P, C])
        rwt = f.sb("rwt", [P, C, D])
        bk = f.sb("bk", [P, C])
        pr = f.ps("pr", [P, C, 512])
        pb = f.ps("pb", [P, 512])
        pw = f.ps("pw", [P, C, 512])
        loaded, made, step, masked, mixed, copied, folded = (
            f.sem(n) for n in ("loaded", "made", "step", "masked", "mixed", "copied", "folded"))
        with nc.Block() as block:
            @block.sync
            def _(s):
                s.dma_start(wqt[:, :, :], rows(A.m0_wqt)).then_inc(loaded, 16)
                s.dma_start(w1[:, :, :], rows(A.m0_w1)).then_inc(loaded, 16)
                s.dma_start(bq[:, :], A.m0_bq_t).then_inc(loaded, 16)
                s.dma_start(b1[:, :], A.m0_b1_t).then_inc(loaded, 16)

            @block.gpsimd
            def _(g):
                block_mask(g, Steps(g, made), diag, HC0)

            @block.vector
            def _(v):
                st = Steps(v, step)
                v.wait_ge(made, 3)
                for k in range(C):
                    v.scalar_tensor_tensor(bd[:, k, :], R.kvsum[:, k * P:(k + 1) * P], 1.0 / N, diag[:, :], ALU.mult,
                                           ALU.mult).then_inc(masked, 1)
                v.wait_ge(mixed, 1)
                for k in range(C):
                    st.then(v.tensor_copy(rwt[:, k, :], pr[:, k, 0:D]))
                    st.then(v.tensor_tensor(rwt[:, k, k * P:(k + 1) * P], rwt[:, k, k * P:(k + 1) * P], R.ident[:, :],
                                            ALU.add))
                st.then(v.tensor_copy(bk[:, :], pb[:, 0:C]))
                v.sem_inc(copied, 1)
                v.wait_ge(folded, 1)
                v.tensor_copy(R.weff[:, :, :], pw[:, :, 0:D])
                v.wait_ge(loaded, 64)
                v.tensor_tensor(R.beff[:, :], pb[:, 64:64 + C], b1[:, :], ALU.add)

            @block.tensor
            def _(t):
                t.wait_ge(loaded, 64)
                t.wait_ge(masked, C)
                for k in range(C):
                    t.matmul(pr[:, k, 0:D], bd[:, k, :], wqt[:, k, :], start=True, stop=True)
                for k in range(C):
                    mm = t.matmul(pb[:, k:k + 1], bd[:, k, :], bq[:, k:k + 1], start=True, stop=True)
                mm.then_inc(mixed, 1)
                t.wait_ge(copied, 1)
                for m in range(C):
                    for k in range(C):
                        t.matmul(pw[:, m, 0:D], rwt[:, k, m * P:(m + 1) * P], w1[:, k, :], start=(k == 0),
                                 stop=(k == C - 1))
                for m in range(C):
                    for k in range(C):
                        mm = t.matmul(pb[:, 64 + m:65 + m], w1[:, k, m * P:(m + 1) * P], bk[:, k:k + 1],
                                      start=(k == 0), stop=(k == C - 1))
                mm.then_inc(folded, 1)


def fold1(nc, R, A):
    K = HEADS * HC1 // P
    with Phase(nc, "fold1") as f:
        diag = f.sb("diag", [P, P])
        bd = f.sb("bd", [P, K, P])
        wqt = f.sb("wqt", [P, K, D])
        wout = f.sb("wout", [P, K, D])
        m1 = f.sb("m1", [P, K, D])
        pm = f.ps("pm", [P, K, 512])
        pw = f.ps("pw", [P, C, 512])
        loaded, made, masked, mixed, copied, folded, red = (
            f.sem(n) for n in ("loaded", "made", "masked", "mixed", "copied", "folded", "red"))
        with nc.Block() as block:
            @block.sync
            def _(s):
                s.dma_start(wqt[:, :, :], rows(A.m1_wqt)).then_inc(loaded, 16)
                s.dma_start(wout[:, :, :], rows(A.m1_wout)).then_inc(loaded, 16)

            @block.gpsimd
            def _(g):
                block_mask(g, Steps(g, made), diag, HC1)
                g.partition_all_reduce(R.gmaxa[:, :], R.gmax[:, :], P, bass.bass_isa.ReduceOp.max).then_inc(red, 1)

            @block.vector
            def _(v):
                v.wait_ge(made, 3)
                for k in range(K):
                    v.scalar_tensor_tensor(bd[:, k, :], R.kvsum[:, k * P:(k + 1) * P], 1.0 / N, diag[:, :], ALU.mult,
                                           ALU.mult).then_inc(masked, 1)
                v.wait_ge(mixed, 1)
                v.tensor_copy(m1[:, :, :], pm[:, :, 0:D]).then_inc(copied, 1)
                v.wait_ge(folded, 1)
                v.tensor_copy(R.weff[:, :, :], pw[:, :, 0:D])

            @block.tensor
            def _(t):
                t.wait_ge(loaded, 32)
                t.wait_ge(masked, K)
                for k in range(K):
                    mm = t.matmul(pm[:, k, 0:D], bd[:, k, :], wout[:, k, :], start=True, stop=True)
                mm.then_inc(mixed, 1)
                t.wait_ge(copied, 1)
                for m in range(C):
                    for k in range(K):
                        mm = t.matmul(pw[:, m, 0:D], wqt[:, k, m * P:(m + 1) * P], m1[:, k, :], start=(k == 0),
                                      stop=(k == K - 1))
                mm.then_inc(folded, 1)



def xtile(R, n):
    return R.X[:, bass.ds(n, 1), :].rearrange("p a d -> p (a d)")



class Layer0Work:
    WINS = W + 1
    HALFW = WINS // 2

    def __init__(self, nc, R, A):
        self.nc, self.R, self.A = nc, R, A

    def stages(self, Q):
        H = self.HALFW
        assert 2 * H == self.WINS and H + 1 < W < 2 * H + 1 < Q
        return [(0, H, "count mix"), (H, H + 1, "sum mix"), (H + 1, W, "rank mix"), (W, 2 * H + 1, "rank"),
                (2 * H + 1, 2 * H + 2, "end"), (2 * H + 2, Q, None)]

    def place(self, f):
        self.w2 = f.sb("w2", [P, C, D])
        self.b2 = f.sb("b2", [1, D])
        self.hid = f.sb("hid", [P, C, P])
        self.ph = f.ps("ph", [P, 512])
        self.py = f.ps("py", [P, 512])
        self.s_w, self.s_h, self.s_g, self.s_o, self.s_a = (f.sem(n) for n in ("mw", "mh", "mg", "mo", "ma"))
        self.wdst = f.sb("wdst", [P, FB], I32)
        self.win = f.sb("win", [P, FB])
        self.hit = f.sb("hit", [P, FB])
        self.rank = f.sb("rank", [P, FB])
        self.one = f.sb("one", [P, FB])
        self.pos = f.sb("pos", [P, FB])
        self.tot = f.sb("tot", [P, self.WINS])
        self.tri = f.sb("tri", [P, P])
        self.start = f.sb("start", [P, self.WINS + 1])
        self.base = f.sb("base", [P, self.WINS])
        self.scanin = f.sb("scanin", [P, self.WINS + 1])
        self.wcol = f.sb("wcol", [P, 1])
        self.bcol = f.sb("bcol", [P, 1])
        self.psum = f.ps("psum", [P, 2, 64])
        self.s_load, self.s_tri, self.s_step, self.s_cnt, self.s_rank, self.s_counted, self.s_summed, self.s_seen = (
            f.sem(n) for n in ("pload", "ptri", "pstep", "pcnt", "prank", "pcounted", "psummed", "pseen"))

    def sync(self, s):
        s.dma_start(self.R.frec[:, :, :], self.A.ffn_edges).then_inc(self.s_load, 16)
        s.dma_start(self.w2[:, :, :], rows(self.A.m0_w2)).then_inc(self.s_w, 16)
        s.dma_start(self.b2[:, :], self.A.m0_b2).then_inc(self.s_w, 16)

    def pool_start(self, g):
        g.memset(self.tri[:, :], 1.0).then_inc(self.s_tri, 1)
        g.wait_ge(self.s_tri, 1)
        g.affine_select(out=self.tri[:, :], in_=self.tri[:, :], compare_op=ALU.is_gt, fill=0.0,
                        base=0, pattern=[[1, P]], channel_multiplier=-1).then_inc(self.s_tri, 1)

    def tensor_start(self, t):
        t.sem_inc(self.s_g, 1)
        t.sem_inc(self.s_a, 1)
        t.wait_ge(self.s_w, 32)
        t.wait_ge(self.s_tri, 2)

    def vector_start(self, v):
        st = self.st = Steps(v, self.s_step)
        v.wait_ge(self.s_load, 16)
        st.then(v.tensor_scalar(self.wdst[:, :], self.R.frec[:, :, 1], 7, None, ALU.arith_shift_right))
        st.then(v.tensor_scalar(self.win[:, :], self.wdst[:, :], float(W), None, ALU.min))
        st.then(v.memset(self.one[:, :], 1.0))
        st.then(v.memset(self.pos[:, :], 0.0))

    def tensor(self, t, i, b, work):
        if "mix" in work and b == 0:
            t.wait_ge(self.s_g, i + 1)
            for fb in range(C):
                for c in range(C):
                    mm = t.matmul(self.ph[:, fb * P:(fb + 1) * P], self.R.weff[:, c, fb * P:(fb + 1) * P],
                                  self.R.XT[:, c, bass.ds(i * P, P)], start=(c == 0), stop=(c == C - 1))
            mm.then_inc(self.s_h, 1)
        if "mix" in work and b == 2:
            t.wait_ge(self.s_g, i + 2)
            t.wait_ge(self.s_a, i + 1)
            t.matmul(self.py[:, 0:D], self.R.ones[0:1, :], self.b2[0:1, :], start=True, stop=False)
            for c in range(C):
                mm = t.matmul(self.py[:, 0:D], self.hid[:, c], self.w2[:, c, :], start=False, stop=(c == C - 1))
            mm.then_inc(self.s_o, 1)
        if "sum" in work and b == 1:
            t.wait_ge(self.s_counted, 1)
            t.matmul(self.psum[:, 0, 0:self.WINS], self.tri[:, :], self.tot[:, :], start=True, stop=True)
            t.matmul(self.psum[:, 1, 0:self.WINS], self.R.ones[:, :], self.tot[:, :], start=True, stop=True)\
                .then_inc(self.s_summed, 1)

    def scalar(self, a, i, b, work):
        if "mix" in work and b == 1:
            a.wait_ge(self.s_h, i + 1)
            for fb in range(C):
                ins = a.activation(self.hid[:, fb], self.ph[:, fb * P:(fb + 1) * P], ACT.Gelu,
                                   bias=self.R.beff[:, fb:fb + 1])
            ins.then_inc(self.s_g, 1)

    def vector(self, v, i, step, work):
        if "mix" in work and step == 3:
            v.wait_ge(self.s_o, i + 1)
            xi = xtile(self.R, i)
            v.tensor_tensor(xi, xi, self.py[:, 0:D], ALU.add).then_inc(self.s_a, 1)
        h = step // 2
        if "count" in work and step in (0, 2):
            n = 4 * i + 2 * h
            w = 2 * i + h
            v.tensor_copy(self.wcol[:, :], self.R.iota[:, bass.ds(w, 1)]).then_inc(self.s_cnt, 1)
            v.wait_ge(self.s_cnt, n + 1)
            v.tensor_scalar(self.hit[:, :], self.win[:, :], self.wcol[:, 0:1], None, ALU.is_equal, ALU.add,
                            accum_out=self.tot[:, bass.ds(w, 1)]).then_inc(self.s_cnt, 1)
            v.wait_ge(self.s_cnt, n + 2)
        if "sum" in work and step == 0:
            v.sem_inc(self.s_counted, 1)
        if "sum" in work and step == 2:
            st = self.st
            v.wait_ge(self.s_summed, 1)
            st.then(v.memset(self.scanin[:, :], 0.0))
            st.then(v.tensor_copy(self.scanin[:, 1:], self.psum[:, 1, 0:self.WINS]))
            st.then(v.tensor_tensor_scan(self.start[:, :], self.one[:, 0:self.WINS + 1], self.scanin[:, :], 0.0,
                                         ALU.mult, ALU.add))
            st.then(v.tensor_copy(self.R.fstart[:, :], self.start[:, 0:W]))
            st.then(v.tensor_tensor(self.base[:, :], self.start[:, 0:self.WINS], self.psum[:, 0, 0:self.WINS],
                                    ALU.add))
        if "rank" in work and step in (0, 2):
            n = 10 * (i - self.HALFW - 1) + 5 * h
            w = 2 * (i - self.HALFW - 1) + h
            v.tensor_copy(self.wcol[:, :], self.R.iota[:, bass.ds(w, 1)]).then_inc(self.s_rank, 1)
            v.tensor_copy(self.bcol[:, :], self.base[:, bass.ds(w, 1)]).then_inc(self.s_rank, 1)
            v.wait_ge(self.s_rank, n + 2)
            v.tensor_scalar(self.hit[:, :], self.win[:, :], self.wcol[:, 0:1], None, ALU.is_equal)\
                .then_inc(self.s_rank, 1)
            v.wait_ge(self.s_rank, n + 3)
            v.tensor_tensor_scan(self.rank[:, :], self.one[:, :], self.hit[:, :], self.bcol[:, 0:1], ALU.mult,
                                 ALU.add).then_inc(self.s_rank, 1)
            v.wait_ge(self.s_rank, n + 4)
            v.sem_inc(self.s_seen, 1)
            v.copy_predicated(self.pos[:, :], self.hit[:, :].bitcast(I32), self.rank[:, :]).then_inc(self.s_rank, 1)
            v.wait_ge(self.s_rank, n + 5)
        if "end" in work and step == 0:
            self.st.then(v.tensor_scalar(self.R.fpos[:, :], self.pos[:, :], 1.0, None, ALU.subtract))



def edges(nc, R, tag, table, nslots, src_ix, dst_rel, wtab, wnext, acc, heads=0, width=0, adst3=None, gmax=None,
          split=False, beside=None):
    FEAT = heads * width
    ROW = table.shape[1]
    F = ROW if split else acc.shape[2]
    SUM = acc.shape[2]
    Q = nslots // TURN
    with Phase(nc, tag) as f:
        rowsb = f.sb("rows", [P, NBUF, GROUP, F])
        ix = f.sb("ix", [P, NBUF, GROUP], U32)
        hot = None if split else f.sb("hot", [P, NBUF, GROUP, P])
        po = f.ps("po", [P, 2 if split else GROUP, 512])
        s_rows = [f.sem(f"rows{b}") for b in range(NBUF)]
        s_ix, s_hot, s_sum, s_acc, s_one, s_seen = (f.sem(n) for n in ("ix", "hot", "sum", "acc", "one", "seen"))
        ACREDIT = 2 * GROUP if split else GROUP
        if heads:
            hott = f.sb("hott", [P, 2, GROUP, P], BF16)
            adw = f.sb("adw", [P, 2, GROUP, 3 * heads], BF16)
            ad = f.sb("ad", [P, GROUP, heads])
            s_adsum, s_hb = f.sem("adsum"), f.sem("hb")
            hotb = f.sb("hotb", [P, NBUF if split else 2, P, GROUP], BF16)
            count = f.sb("count", [P, P, GROUP], BF16)
            s_count = f.sem("count")
            z = f.sb("z", [P, GROUP, heads])
            lz = f.sb("lz", [P, GROUP, heads])
            zm = f.sb("zm", [P, GROUP, heads])
            lm = f.sb("lm", [P, GROUP, heads])
            ptt = f.ps("ptt", [P, GROUP * P], BF16)
            pad = f.ps("pad", [P, 2, 512])
            s_tp, s_tt, s_adw, s_ad, s_z, s_zm, s_lz, s_lm, s_d, s_ex, s_msg = (
                f.sem(n) for n in ("tp", "tt", "adw", "ad", "z", "zm", "lz", "lm", "d", "ex", "msg"))

        if split:
            parts = f.sb("parts", [P, 2, GROUP, 3, F], BF16)
            s_part = f.sem("part")

        def bank(b, u):
            return po[:, b % 2, u * SUM:(u + 1) * SUM] if split else po[:, u, 0:SUM]

        stages = beside.stages(Q) if beside else [(0, Q, None)]
        if beside:
            beside.place(f)

        def turns(engine, turn):
            for lo, hi, work in stages:
                if hi - lo == 1:
                    turn(lo, work)
                else:
                    with engine.Fori(lo, hi) as i:
                        turn(i, work)

        def windows(engine, at, n):
            _, ws = nc.values_load_multi_w_load_instructions(
                at, engines=(engine,), min_val=0, max_val=W - 1,
                skip_runtime_bounds_check_because="a count of at most W - 1 windows")
            assert len(ws) == n
            return ws

        with nc.Block() as block:
            @block.gpsimd
            def _(g):
                def gather(b, copied):
                    g.wait_ge(s_ix, copied)
                    g.sem_inc(s_seen, 1)
                    for u in range(GROUP):
                        g.indirect_dma_start(rowsb[:, b, u, 0:ROW], None, table,
                                             bass.IndirectOffsetOnAxis(ix[:, b, u:u + 1], 0)).then_inc(s_rows[b], 16)

                if beside:
                    beside.pool_start(g)
                with g.Fori(0, Q) as i:
                    for b in range(NBUF):
                        gather(b, NBUF * i + b + 1)
                if heads:
                    gather(0, NBUF * Q + 1)

            @block.scalar
            def _(a):
                def indices(q, b):
                    a.activation(ix[:, b], src_ix[:, bass.ds(GROUP * q, GROUP)], ACT.Copy).then_inc(s_ix, 1)

                def window_scores(par, ws):
                    for u in range(GROUP):
                        ins = a.activation(adw[:, par, u], adst3[:, bass.ds(ws[u], 1), :].rearrange("p a h -> p (a h)"),
                                           ACT.Copy)
                    ins.then_inc(s_adw, 1)

                def whole_hot(q, b):
                    if not split:
                        a.wait_ge(s_hot, q + 1)
                        a.activation(hot[:, b], hotb[:, b % 2].rearrange("p e u -> p u e"), ACT.Copy).then_inc(s_hb, 1)

                def turned(q, par):
                    a.wait_ge(s_tp, q + 1)
                    a.activation(hott[:, par], ptt[:, :].rearrange("p (u e) -> p u e", u=GROUP), ACT.Copy)\
                        .then_inc(s_tt, 1)

                def weight(q, b):
                    a.wait_ge(s_d, q + 1)
                    a.activation(rowsb[:, b, :, FEAT:FEAT + heads], z[:, :, :], ACT.Exp).then_inc(s_ex, 1)

                for b in range(NBUF):
                    indices(b, b)
                if heads:
                    ws = windows(ENG.Activation, wtab[0:1, 0:2 * GROUP], 2 * GROUP)
                    for q in range(3):
                        if q < 2:
                            window_scores(q, ws[q * GROUP:(q + 1) * GROUP])
                        whole_hot(q, q)
                        turned(q, q % 2)
                    weight(0, 0)
                def turn(i, work):
                    if heads:
                        ws = windows(ENG.Activation, wnext[0:1, bass.ds(TURN * i, TURN)], TURN)
                    for b in range(NBUF):
                        q = NBUF * i + b
                        if heads:
                            a.wait_ge(s_ad, q + 1)
                            window_scores(b % 2, ws[b * GROUP:(b + 1) * GROUP])
                            weight(q + 1, (b + 1) % NBUF)
                            whole_hot(q + 3, (b + 3) % NBUF)
                        if work:
                            beside.scalar(a, i, b, work)
                        if heads:
                            turned(q + 3, (b + 1) % 2)
                        a.wait_ge(s_sum, GROUP * q + GROUP)
                        indices(q + NBUF, b)

                turns(a, turn)

            @block.vector
            def _(v):
                def one_hot(q, b, ahead=True):
                    dst = dst_rel[:, bass.ds(GROUP * q, GROUP)]
                    if not heads:
                        v.tensor_tensor(hot[:, b], R.iota[:, :].unsqueeze(1).to_broadcast([P, GROUP, P]),
                                        dst.unsqueeze(2).to_broadcast([P, GROUP, P]), ALU.is_equal).then_inc(s_hot, 1)
                        return
                    if not split and ahead:
                        v.wait_ge(s_tp, q - 1)
                        v.wait_ge(s_hb, q - 1)
                    v.tensor_tensor(hotb[:, b if split else b % 2], count[:, :, :],
                                    dst.unsqueeze(1).to_broadcast([P, P, GROUP]), ALU.is_equal).then_inc(s_hot, 1)

                def exponents(q, b, gathered):
                    v.wait_ge(s_ad, q + 1)
                    v.tensor_reduce(ad[:, :, :], pad[:, b % 2, 0:GROUP * 3 * heads]
                                    .rearrange("p (u k h) -> p u h k", k=3, h=heads), AXX, ALU.add).then_inc(s_adsum, 1)
                    v.wait_ge(s_adsum, q + 1)
                    v.tensor_tensor(zm[:, :, :], ad[:, :, :], gmax[:, :].unsqueeze(1).to_broadcast([P, GROUP, heads]),
                                    ALU.add).then_inc(s_zm, 1)
                    v.wait_ge(s_rows[b], gathered)
                    v.tensor_tensor(z[:, :, :], ad[:, :, :], rowsb[:, b, :, FEAT:FEAT + heads], ALU.add).then_inc(s_z, 1)
                    v.wait_ge(s_zm, q + 1)
                    v.scalar_tensor_tensor(lm[:, :, :], zm[:, :, :], 0.2, zm[:, :, :], ALU.mult, ALU.max)\
                        .then_inc(s_lm, 1)
                    v.wait_ge(s_z, q + 1)
                    v.scalar_tensor_tensor(lz[:, :, :], z[:, :, :], 0.2, z[:, :, :], ALU.mult, ALU.max)\
                        .then_inc(s_lz, 1)
                    v.wait_ge(s_lm, q + 1)
                    v.wait_ge(s_lz, q + 1)
                    v.tensor_tensor(z[:, :, :], lz[:, :, :], lm[:, :, :], ALU.subtract).then_inc(s_d, 1)

                def cut(q, b):
                    m, part = rowsb[:, b], parts[:, b % 2]
                    v.wait_ge(s_part, 4 * q + 1)
                    v.tensor_copy(part[:, :, 0], m).then_inc(s_part, 1)
                    v.wait_ge(s_part, 4 * q + 2)
                    v.tensor_tensor(m, m, part[:, :, 0], ALU.subtract).then_inc(s_part, 1)
                    v.wait_ge(s_part, 4 * q + 3)
                    v.tensor_copy(part[:, :, 1], m).then_inc(s_part, 1)
                    v.wait_ge(s_part, 4 * q + 4)
                    v.tensor_tensor(part[:, :, 2], m, part[:, :, 1], ALU.subtract).then_inc(s_msg, 1)

                def message(q, b):
                    v.wait_ge(s_ex, q + 1)
                    m = rowsb[:, b, :, 0:FEAT].rearrange("p u (h c) -> p u h c", h=heads)
                    v.tensor_tensor(m, m, rowsb[:, b, :, FEAT:FEAT + heads].unsqueeze(3)
                                    .to_broadcast([P, GROUP, heads, width]), ALU.mult)\
                        .then_inc(s_part if split else s_msg, 1)
                    if split:
                        cut(q, b)

                if F > ROW:
                    v.memset(rowsb[:, :, :, ROW:F], 1.0).then_inc(s_one, 1)
                if heads:
                    v.tensor_copy(count[:, :, :], R.iota[:, :].unsqueeze(2).to_broadcast([P, P, GROUP]))\
                        .then_inc(s_count, 1)
                    v.wait_ge(s_count, 1)
                one_hot(0, 0, False)
                one_hot(1, 1, False)
                one_hot(2, 2)
                if heads:
                    exponents(0, 0, 16 * GROUP)
                    message(0, 0)
                if beside:
                    beside.vector_start(v)

                def turn(i, work):
                    wt = windows(ENG.DVE, wtab[0:1, bass.ds(TURN * i, TURN)], TURN)
                    for b in range(NBUF):
                        q = NBUF * i + b
                        if heads:
                            exponents(q + 1, (b + 1) % NBUF, 16 * GROUP * (i + 1 + (b + 1) // NBUF))
                        one_hot(q + 3, (b + 3) % NBUF)
                        if work:
                            beside.vector(v, i, b, work)
                        for u in range(GROUP):
                            if heads and u == GROUP // 2:
                                message(q + 1, (b + 1) % NBUF)
                            v.wait_ge(s_sum, GROUP * q + (GROUP if split else u + 1))
                            v.wait_ge(s_acc, GROUP * q + u + ACREDIT)
                            aw = acc[:, bass.ds(wt[b * GROUP + u], 1), :].rearrange("p a d -> p (a d)")
                            v.tensor_tensor(aw, aw, bank(b, u), ALU.add).then_inc(s_acc, 1)
                    if work:
                        beside.vector(v, i, NBUF, work)

                turns(v, turn)

            @block.tensor
            def _(t):
                def turn_hot(q, b):
                    t.wait_ge(s_hot, q + 1)
                    for u in range(GROUP):
                        mm = t.transpose(ptt[:, u * P:(u + 1) * P], hotb[:, b if split else b % 2, :, u],
                                         R.identb[:, :])
                    mm.then_inc(s_tp, 1)

                def scores(q, b):
                    t.wait_ge(s_tt, q + 1)
                    t.wait_ge(s_adw, q + 1)
                    for u in range(GROUP):
                        o = u * 3 * heads
                        mm = t.matmul(pad[:, b % 2, o:o + 3 * heads], hott[:, b % 2, u], adw[:, b % 2, u], start=True,
                                      stop=True)
                    mm.then_inc(s_ad, 1)

                t.sem_inc(s_acc, ACREDIT)
                if F > ROW:
                    t.wait_ge(s_one, 1)
                if heads:
                    turn_hot(0, 0)
                    scores(0, 0)
                    turn_hot(1, 1)
                    scores(1, 1)
                    turn_hot(2, 2)
                if beside:
                    beside.tensor_start(t)

                def turn(i, work):
                    for b in range(NBUF):
                        q = NBUF * i + b
                        if heads:
                            t.wait_ge(s_msg, q + 1)
                            if not split:
                                t.wait_ge(s_hb, q + 1)
                        else:
                            t.wait_ge(s_hot, q + 1)
                            t.wait_ge(s_rows[b], 16 * GROUP * i + 16 * GROUP)
                        for u in range(GROUP):
                            if heads and u == GROUP // 2:
                                scores(q + 2, (b + 2) % NBUF)
                            t.wait_ge(s_acc, GROUP * q + (GROUP if split else u + 1))
                            w = parts[:, b % 2, u].rearrange("p k f -> p (k f)") if split else rowsb[:, b, u, :]
                            one = hotb[:, b, :, u] if split else hot[:, b, u]
                            t.matmul(bank(b, u), one, w, start=True, stop=True).then_inc(s_sum, 1)
                        if heads:
                            turn_hot(q + 3, (b + 3) % NBUF)
                        if work:
                            beside.tensor(t, i, b, work)

                turns(t, turn)

            @block.sync
            def _(s):
                if beside:
                    beside.sync(s)


def loops(nc, R, tag, table, acc, heads, width, adst, adst3, gmax):
    ROW = table.shape[1]
    FEAT = heads * width
    with Phase(nc, tag) as f:
        z = f.sb("z", [P, W, heads])
        zm = f.sb("zm", [P, W, heads])
        s_in, s_st, s_go, s_ex = (f.sem(n) for n in ("in", "st", "go", "ex"))
        with nc.Block() as block:
            @block.sync
            def _(s):
                s.dma_start(acc[:, :, 0:ROW], table.rearrange("(t p) d -> p t d", p=P)).then_inc(s_in, 16)

            @block.vector
            def _(v):
                st = Steps(v, s_st)
                if acc.shape[2] > ROW:
                    v.memset(acc[:, :, ROW:], 0.0)
                st.then(v.tensor_copy(z[:, :, :], adst[:, :, :]))
                for k in range(3):
                    part = adst3[:, :, k * heads:(k + 1) * heads]
                    st.then(v.tensor_copy(part, z[:, :, :]))
                    if k < 2:
                        st.then(v.tensor_tensor(z[:, :, :], z[:, :, :], part, ALU.subtract))
                st.then(v.tensor_tensor(zm[:, :, :], adst[:, :, :], gmax[:, :].unsqueeze(1).to_broadcast([P, W, heads]),
                                        ALU.add))
                st.then(v.scalar_tensor_tensor(zm[:, :, :], zm[:, :, :], 0.2, zm[:, :, :], ALU.mult, ALU.max))
                v.wait_ge(s_in, 16)
                st.then(v.tensor_tensor(z[:, :, :], acc[:, :, FEAT:FEAT + heads], adst[:, :, :], ALU.add))
                st.then(v.scalar_tensor_tensor(z[:, :, :], z[:, :, :], 0.2, z[:, :, :], ALU.mult, ALU.max))
                st.then(v.tensor_tensor(z[:, :, :], z[:, :, :], zm[:, :, :], ALU.subtract))
                v.sem_inc(s_go, 1)
                v.wait_ge(s_ex, 1)
                a4 = acc[:, :, 0:FEAT].rearrange("p t (h c) -> p t h c", h=heads)
                v.tensor_tensor(a4, a4, acc[:, :, FEAT:FEAT + heads].unsqueeze(3).to_broadcast([P, W, heads, width]),
                                ALU.mult)

            @block.scalar
            def _(a):
                a.wait_ge(s_go, 1)
                a.activation(acc[:, :, FEAT:FEAT + heads], z[:, :, :], ACT.Exp).then_inc(s_ex, 1)


def clear(nc, tile):
    with nc.Block() as block:
        @block.vector
        def _(v):
            v.memset(tile, 0.0)



class Scatter:

    def __init__(self, f, R):
        self.R = R
        self.ix = f.sb("ix", [P, 2, GROUP8], U32)
        self.rec = f.sb("rec", [P, 2, GROUP8, 2], I32)
        self.s_seen, self.s_ix, self.s_sc = f.sem("scseen"), f.sem("scix"), [f.sem(f"sc{k}") for k in range(2)]

    def run(self, g, first, end):
        with g.Fori(0, end - first) as i:
            for b in range(2):
                g.wait_ge(self.s_sc[b], 16 * GROUP8 * i)
                q = 2 * (first + i) + b
                g.tensor_copy(self.ix[:, b], self.R.fpos[:, bass.ds(GROUP8 * q, GROUP8)]).then_inc(self.s_ix, 1)
                g.tensor_copy(self.rec[:, b].rearrange("p t k -> p (t k)"),
                              self.R.frec[:, bass.ds(GROUP8 * q, GROUP8), :].rearrange("p t k -> p (t k)"))\
                    .then_inc(self.s_ix, 1)
                g.wait_ge(self.s_ix, 4 * i + 2 * b + 2)
                g.sem_inc(self.s_seen, 1)
                for u in range(GROUP8):
                    g.indirect_dma_start(self.R.fsorted, bass.IndirectOffsetOnAxis(self.ix[:, b, u:u + 1], 0),
                                         self.rec[:, b, u], None).then_inc(self.s_sc[b], 16)
        for b in range(2):
            g.wait_ge(self.s_sc[b], 16 * GROUP8 * (end - first))


def gcn_finish(nc, R, A):
    with Phase(nc, "gcnf") as f:
        wout = f.sb("wout", [GCN + 1, D])
        bg = f.sb("bg", [P, GCN])
        nd = f.sb("nd", [P, W])
        h = f.sb("h", [P, TPI, GCN + 1])
        ht = f.sb("ht", [GCN + 1, TPI, P])
        pt = f.ps("pt", [P, 2, 512])
        po = f.ps("po", [P, 2, 512])
        s_w, s_st, s_sq, s_rt, s_ready, s_h, s_t, s_c, s_o, s_a, s_m = (
            f.sem(n) for n in ("w", "st", "sq", "rt", "ready", "h", "t", "c", "o", "a", "m"))
        scatter = Scatter(f, R)
        with nc.Block() as block:
            @block.gpsimd
            def _(g):
                scatter.run(g, 0, SCATTERG)

            @block.sync
            def _(s):
                s.dma_start(wout[0:GCN, :], A.gcn_wout).then_inc(s_w, 16)
                s.dma_start(wout[GCN:GCN + 1, :], A.gcn_bout).then_inc(s_w, 16)
                s.dma_start(bg[:, :], spread(A.gcn_b)).then_inc(s_w, 16)

            @block.vector
            def _(v):
                st = Steps(v, s_st)
                st.then(v.tensor_scalar(nd[:, :], R.gcn[:, :, GCN], 1.0, None, ALU.max))
                v.sem_inc(s_sq, 1)
                v.memset(h[:, :, GCN:GCN + 1], 1.0).then_inc(s_m, 1)
                v.wait_ge(s_rt, 1)
                st.then(v.reciprocal(nd[:, :], nd[:, :]))
                g3 = R.gcn[:, :, 0:GCN]
                v.wait_ge(s_w, 48)
                st.then(v.tensor_tensor(g3, g3, nd[:, :].unsqueeze(2).to_broadcast([P, W, GCN]), ALU.mult))
                st.then(v.tensor_tensor(g3, g3, bg[:, :].unsqueeze(1).to_broadcast([P, W, GCN]), ALU.add))
                with v.Fori(0, ITER) as i:
                    v.wait_ge(s_t, TPI * i)
                    v.tensor_scalar(h[:, :, 0:GCN], R.gcn[:, bass.ds(TPI * i, TPI), 0:GCN], 0.0, None, ALU.max)\
                        .then_inc(s_h, 1)
                    for j in range(TPI):
                        v.wait_ge(s_o, TPI * i + j + 1)
                        xj = xtile(R, TPI * i + j)
                        v.tensor_tensor(xj, xj, po[:, j % 2, 0:D], ALU.add).then_inc(s_a, 1)

            @block.scalar
            def _(a):
                a.wait_ge(s_sq, 1)
                a.activation(nd[:, :], nd[:, :], ACT.Sqrt).then_inc(s_rt, 1)
                with a.Fori(0, ITER) as i:
                    a.wait_ge(s_o, TPI * i)
                    for j in range(TPI):
                        a.wait_ge(s_t, TPI * i + j + 1)
                        a.activation(ht[:, j], pt[0:GCN + 1, j % 2, 0:P], ACT.Copy).then_inc(s_c, 1)

            @block.tensor
            def _(t):
                t.wait_ge(s_w, 48)
                t.wait_ge(s_m, 1)
                with t.Fori(0, ITER) as i:
                    def turn_tile(j):
                        t.wait_ge(s_c, TPI * i + (j - 1 if j >= 2 else 0))
                        t.transpose(pt[0:GCN + 1, j % 2, 0:P], h[:, j], R.ident[:, :]).then_inc(s_t, 1)

                    t.wait_ge(s_h, i + 1)
                    turn_tile(0)
                    for j in range(TPI):
                        if j + 1 < TPI:
                            turn_tile(j + 1)
                        t.wait_ge(s_c, TPI * i + j + 1)
                        t.wait_ge(s_a, TPI * i + (j - 1 if j >= 2 else 0))
                        t.matmul(po[:, j % 2, 0:D], ht[:, j], wout[:, :], start=True, stop=True).then_inc(s_o, 1)



def gates0(nc, R, A):
    with Phase(nc, "gate0") as f:
        nm = Norm(f, R)
        wr = f.sb("wr", [P, C, E0])
        br = f.sb("br", [P, E0])
        lg = f.sb("lg", [P, W, E0])
        mx = f.sb("mx", [P, W])
        pl = f.ps("pl", [P, 512])
        s_w, s_st, s_l, s_g, s_m, s_e = (f.sem(n) for n in ("w", "st", "l", "g", "m", "e"))
        scatter = Scatter(f, R)
        with nc.Block() as block:
            @block.gpsimd
            def _(g):
                scatter.run(g, SCATTERG, SCATTER0)

            @block.sync
            def _(s):
                s.dma_start(wr[:, :, :], rows(A.f0_wr)).then_inc(s_w, 16)
                s.dma_start(br[:, :], spread(A.f0_br)).then_inc(s_w, 16)

            @block.vector
            def _(v):
                v.wait_ge(s_w, 32)
                nm.statistics(v, 0)
                nm.normalise(v, 0)

                def turn(i, more):
                    if more:
                        nm.statistics(v, i + 1)
                        nm.normalise(v, i + 1)
                    v.wait_ge(s_l, TPI * i + TPI)
                    v.tensor_tensor(lg[:, bass.ds(TPI * i, TPI), :],
                                    pl[:, 0:TPI * E0].rearrange("p (t e) -> p t e", e=E0),
                                    br[:, :].unsqueeze(1).to_broadcast([P, TPI, E0]), ALU.add).then_inc(s_g, 1)

                nm.turns(v, turn)
                st = Steps(v, s_st)
                wide = mx[:, :].unsqueeze(2).to_broadcast([P, W, E0])
                v.wait_ge(s_g, ITER)
                st.then(v.tensor_reduce(mx[:, :], lg[:, :, :], AXX, ALU.max))
                st.then(v.tensor_tensor(lg[:, :, :], lg[:, :, :], wide, ALU.subtract))
                v.sem_inc(s_m, 1)
                v.wait_ge(s_e, 1)
                st.then(v.tensor_reduce(mx[:, :], lg[:, :, :], AXX, ALU.add))
                st.then(v.reciprocal(mx[:, :], mx[:, :]))
                st.then(v.tensor_tensor(R.gate[:, :, 0:E0], lg[:, :, :], wide, ALU.mult))

            @block.scalar
            def _(a):
                nm.scalar_root(a, 0)

                def turn(i, more):
                    a.wait_ge(s_l, TPI * i)
                    for j in range(TPI):
                        nm.scalar_copy(a, i, j)
                        if more and j == TPI // 2:
                            nm.scalar_root(a, i + 1)

                nm.turns(a, turn)
                a.wait_ge(s_m, 1)
                a.activation(lg[:, :, :], lg[:, :, :], ACT.Exp).then_inc(s_e, 1)

            @block.tensor
            def _(t):
                t.wait_ge(s_w, 32)
                with t.Fori(0, ITER) as i:
                    nm.tensor(t, i, 0)
                    t.wait_ge(s_g, i)
                    for j in range(TPI):
                        if j + 1 < TPI:
                            nm.tensor(t, i, j + 1)
                        t.wait_ge(nm.s_xt, TPI * i + j + 1)
                        for c in range(C):
                            mm = t.matmul(pl[:, j * E0:(j + 1) * E0], nm.xt[:, j, c], wr[:, c, :], start=(c == 0),
                                          stop=(c == C - 1))
                        mm.then_inc(s_l, 1)


def experts0(nc, R, A):
    with Phase(nc, "exp0") as f:
        bo = f.sb("bo", [P, E0, D])
        s_bo = f.sem("bo")
        w1 = f.sb("w1", [P, E0, C, D])
        w2 = f.sb("w2", [P, E0, C, D])
        wo = f.sb("wo", [P, E0, C, D])
        bn = f.sb("bn", [P, 2, 5, E0 * C])
        scale = f.sb("scale", [P, 2, E0 * C])
        shift = f.sb("shift", [P, 2, E0 * C])
        h1 = f.sb("h1", [P, C, TOK])
        h2 = f.sb("h2", [P, C, TOK])
        ph = f.ps("ph", [P, 4, 512])
        po = f.ps("po", [P, 4, 512])
        s_w = [f.sem(f"w{e}") for e in range(E0)]
        s_b, s_st, s_v, s_rt, s_ready, s_h, s_g, s_o, s_a, s_l2 = (
            f.sem(n) for n in ("b", "st", "v", "rt", "ready", "h", "g", "o", "a", "l2"))
        scatter = Scatter(f, R)
        with nc.Block() as block:
            @block.gpsimd
            def _(g):
                scatter.run(g, SCATTER0, SCATTERS)

            @block.sync
            def _(s):
                s.dma_start(bn[:, :, :, :], A.f0_bn).then_inc(s_b, 16)
                for e in range(E0):
                    s.dma_start(bo[:, e], spread(A.f0_bo[e])).then_inc(s_b, 16)
                for e in range(E0):
                    for wt, wd in ((w1, A.f0_w1), (w2, A.f0_w2), (wo, A.f0_wo)):
                        s.dma_start(wt[:, e], rows(wd[e])).then_inc(s_w[e], 16)

            @block.tensor
            def _(t):
                with t.Fori(0, ITER) as i:
                    base = 8 * E0 * i

                    def layer(e, l):
                        t.wait_ge(s_w[e], 16 * 3)
                        k = 2 * e + l
                        for fb in range(C):
                            for h in range(2):
                                n = 2 * fb + h
                                t.wait_ge(s_g, base + (4 * (k - 1) + n + 1 if k else 0))
                                for c in range(C):
                                    x = R.XT[:, c, bass.ds(i * TOK + h * HALF, HALF)] if l == 0 else \
                                        h1[:, c, h * HALF:(h + 1) * HALF]
                                    w = (w1, w2)[l][:, e, c, fb * P:(fb + 1) * P]
                                    mm = t.matmul(ph[:, n, 0:HALF], w, x, start=(c == 0), stop=(c == C - 1))
                                mm.then_inc(s_h, 1)

                    layer(0, 0)
                    for e in range(E0):
                        t.wait_ge(s_g, base + 8 * e + 4)
                        layer(e, 1)
                        if e + 1 < E0:
                            layer(e + 1, 0)
                        t.wait_ge(s_g, base + 8 * e + 8)
                        for j in range(TPI):
                            n = TPI * e + j
                            t.wait_ge(s_a, TPI * E0 * i + max(n - 3, 0))
                            for c in range(C):
                                mm = t.matmul(po[:, n % 4, 0:D], h2[:, c, j * P:(j + 1) * P], wo[:, e, c, :],
                                              start=(c == 0), stop=(c == C - 1))
                            mm.then_inc(s_o, 1)

            @block.vector
            def _(v):
                st = Steps(v, s_st)
                v.wait_ge(s_b, 16 * (1 + E0))
                st.then(v.tensor_scalar(scale[:, :, :], bn[:, :, 4, :], BN_EPS, None, ALU.add))
                v.sem_inc(s_v, 1)
                v.wait_ge(s_rt, 1)
                st.then(v.reciprocal(scale[:, :, :], scale[:, :, :]))
                st.then(v.tensor_tensor(scale[:, :, :], scale[:, :, :], bn[:, :, 1, :], ALU.mult))
                st.then(v.tensor_tensor(shift[:, :, :], bn[:, :, 0, :], bn[:, :, 3, :], ALU.subtract))
                st.then(v.tensor_tensor(shift[:, :, :], shift[:, :, :], scale[:, :, :], ALU.mult))
                st.then(v.tensor_tensor(shift[:, :, :], shift[:, :, :], bn[:, :, 2, :], ALU.add))
                v.sem_inc(s_ready, 1)
                with v.Fori(0, ITER) as i:
                    for e in range(E0):
                        gates = [R.gate[:, bass.ds(TPI * i + j, 1), e:e + 1].rearrange("p a b -> p (a b)")
                                 for j in range(TPI)]
                        for j in range(TPI):
                            n = TPI * e + j
                            v.wait_ge(s_a, TPI * E0 * i + max(n - 6, 0))
                            xj = xtile(R, TPI * i + j)
                            v.scalar_tensor_tensor(xj, bo[:, e], gates[j], xj, ALU.mult, ALU.add).then_inc(s_bo, 1)
                        for j in range(TPI):
                            n = TPI * e + j
                            v.wait_ge(s_o, TPI * E0 * i + n + 1)
                            v.wait_ge(s_bo, TPI * E0 * i + n + 1)
                            xj = xtile(R, TPI * i + j)
                            g = gates[j]
                            v.scalar_tensor_tensor(xj, po[:, n % 4, 0:D], g, xj, ALU.mult, ALU.add).then_inc(s_a, 1)

            @block.scalar
            def _(a):
                a.wait_ge(s_v, 1)
                a.activation(scale[:, :, :], scale[:, :, :], ACT.Sqrt).then_inc(s_rt, 1)
                a.wait_ge(s_ready, 1)
                with a.Fori(0, ITER) as i:
                    for e in range(E0):
                        for l in range(2):
                            k = 2 * e + l
                            if l:
                                a.wait_ge(s_o, TPI * E0 * i + TPI * e)
                            for fb in range(C):
                                for h in range(2):
                                    n = 2 * fb + h
                                    a.wait_ge(s_h, 8 * E0 * i + 4 * k + n + 1)
                                    a.activation((h1, h2)[l][:, fb, h * HALF:(h + 1) * HALF], ph[:, n, 0:HALF],
                                                 ACT.Relu, bias=shift[:, l, C * e + fb:C * e + fb + 1],
                                                 scale=scale[:, l, C * e + fb:C * e + fb + 1]).then_inc(s_g, 1)



def finish1(nc, R, A):
    with Phase(nc, "fin1") as f:
        bias = f.sb("bias", [P, 2, D])
        den = f.sb("den", [P, W, GH])
        xt = f.sb("xt", [P, TPI, C, P])
        po = f.ps("po", [P, 2, 512])
        s_w, s_st, s_x, s_o, s_m, s_b, s_a, s_m2 = (f.sem(n) for n in ("w", "st", "x", "o", "m", "b", "a", "m2"))
        with nc.Block() as block:
            @block.sync
            def _(s):
                s.dma_start(bias[:, 0, :], spread(A.gat_bias[0])).then_inc(s_w, 16)
                s.dma_start(bias[:, 1, :], spread(A.m1_bout[0])).then_inc(s_w, 16)

            @block.scalar
            def _(a):
                with a.Fori(0, ITER) as i:
                    a.wait_ge(s_o, TPI * i)
                    for j in range(TPI):
                        a.activation(xt[:, j], R.XT[:, :, bass.ds((TPI * i + j) * P, P)], ACT.Copy).then_inc(s_x, 1)

            @block.tensor
            def _(t):
                with t.Fori(0, ITER) as i:
                    for j in range(TPI):
                        t.wait_ge(s_x, TPI * i + j + 1)
                        t.wait_ge(s_b, TPI * i + (j - 1 if j >= 2 else 0))
                        for c in range(C):
                            mm = t.matmul(po[:, j % 2, 0:D], xt[:, j, c], R.weff[:, c, :], start=(c == 0),
                                          stop=(c == C - 1))
                        mm.then_inc(s_o, 1)

            @block.vector
            def _(v):
                st = Steps(v, s_st)
                st.then(v.tensor_scalar(den[:, :, :], R.gat[:, :, GH * GC:GROW], 1e-30, None, ALU.max))
                st.then(v.reciprocal(den[:, :, :], den[:, :, :]))
                v.wait_ge(s_w, 32)
                st.then(v.tensor_tensor(bias[:, 0], bias[:, 0], bias[:, 1], ALU.add))
                with v.Fori(0, ITER) as i:
                    for j in range(TPI):
                        n = TPI * i + j
                        a3 = R.gat[:, bass.ds(n, 1), 0:GH * GC].rearrange("p a (h c) -> p (a h) c", c=GC)
                        a2 = R.gat[:, bass.ds(n, 1), 0:GH * GC].rearrange("p a d -> p (a d)")
                        d3 = den[:, bass.ds(n, 1), :].rearrange("p a h -> p (a h)").unsqueeze(2).to_broadcast([P, GH, GC])
                        v.tensor_tensor(a3, a3, d3, ALU.mult).then_inc(s_m, 1)
                        xj = xtile(R, n)
                        v.wait_ge(s_o, n + 1)
                        v.tensor_tensor(xj, xj, po[:, j % 2, 0:D], ALU.add).then_inc(s_b, 1)
                        v.wait_ge(s_m, n + 1)
                        v.tensor_tensor(a2, a2, bias[:, 0], ALU.add).then_inc(s_m2, 1)
                        v.wait_ge(s_m2, n + 1)
                        v.wait_ge(s_b, n + 1)
                        v.tensor_tensor(xj, xj, a2, ALU.add).then_inc(s_a, 1)



def router_table(nc, R, A):
    FX = FH * FC
    EXT = FX + 2 * FH
    with Phase(nc, "rtab") as f:
        nm = Norm(f, R)
        w = f.sb("w", [P, C, EXT])
        att = f.sb("att", [P, 2, FX])
        wa = f.sb("wa", [P, FX])
        tabt = f.sb("tabt", [P, W, FROW])
        gm = f.sb("gm", [P, FH])
        pl = f.ps("pl", [P, 512])
        s_w, s_st, s_l, s_e, s_t, s_ready, s_o, s_red = (
            f.sem(n) for n in ("w_", "st", "l", "e", "t", "ready", "o", "red"))
        with nc.Block() as block:
            @block.sync
            def _(s):
                s.dma_start(w[:, :, 0:FX], rows(A.r_w)).then_inc(s_w, 16)
                for k, row in enumerate((A.r_src, A.r_dst)):
                    s.dma_start(att[:, k, :], spread(row)).then_inc(s_w, 16)
                s.wait_ge(s_t, 1)
                s.dma_start(R.tabr.rearrange("(t p) d -> p t d", p=P), tabt[:, :, :]).then_inc(s_o, 16)
                s.wait_ge(s_o, 16)

            @block.vector
            def _(v):
                st = Steps(v, s_st)
                v.wait_ge(s_w, 48)
                for c in range(C):
                    for k in range(2):
                        st.then(v.tensor_tensor(wa[:, :], w[:, c, 0:FX], att[:, k, :], ALU.mult))
                        o = FX + k * FH
                        st.then(v.tensor_reduce(w[:, c, o:o + FH], wa[:, :].rearrange("p (h c) -> p h c", h=FH), AXX,
                                                ALU.add))
                v.sem_inc(s_ready, 1)
                nm.statistics(v, 0)
                nm.normalise(v, 0)

                def turn(i, more):
                    if more:
                        nm.statistics(v, i + 1)
                        nm.normalise(v, i + 1)
                    v.wait_ge(s_l, TPI * i + TPI)
                    v.tensor_copy(R.rext[:, bass.ds(TPI * i, TPI), :],
                                  pl[:, 0:TPI * EXT].rearrange("p (t e) -> p t e", e=EXT)).then_inc(s_e, 1)

                nm.turns(v, turn)
                v.wait_ge(s_e, ITER)
                st.then(v.tensor_copy(tabt[:, :, :], R.rext[:, :, 0:FROW]))
                v.sem_inc(s_t, 1)
                st.then(v.tensor_copy(R.rdst[:, :, :], R.rext[:, :, FROW:EXT]))
                st.then(v.tensor_reduce(gm[:, :], R.rext[:, :, FX:FROW].rearrange("p t h -> p h t"), AXX, ALU.max))
                v.sem_inc(s_red, 1)

            @block.gpsimd
            def _(g):
                g.wait_ge(s_red, 1)
                g.partition_all_reduce(R.rmax[:, :], gm[:, :], P, bass.bass_isa.ReduceOp.max)

            @block.scalar
            def _(a):
                nm.scalar_root(a, 0)

                def turn(i, more):
                    a.wait_ge(s_l, TPI * i)
                    for j in range(TPI):
                        nm.scalar_copy(a, i, j)
                        if more and j == TPI // 2:
                            nm.scalar_root(a, i + 1)

                nm.turns(a, turn)

            @block.tensor
            def _(t):
                t.wait_ge(s_ready, 1)
                with t.Fori(0, ITER) as i:
                    nm.tensor(t, i, 0)
                    t.wait_ge(s_e, i)
                    for j in range(TPI):
                        if j + 1 < TPI:
                            nm.tensor(t, i, j + 1)
                        t.wait_ge(nm.s_xt, TPI * i + j + 1)
                        for c in range(C):
                            mm = t.matmul(pl[:, j * EXT:(j + 1) * EXT], nm.xt[:, j, c], w[:, c, :], start=(c == 0),
                                          stop=(c == C - 1))
                        mm.then_inc(s_l, 1)


def router_gates(nc, R, A):
    FX = FH * FC
    K = E1
    with Phase(nc, "rgate") as f:
        z = f.sb("z", [P, W, FH])
        t16 = f.sb("t16", [P, W, FX])
        a = f.sb("a", [P, W, FX])
        m = f.sb("m", [P, W])
        r = f.sb("r", [P, W])
        bg = f.sb("bg", [P, 3, FX])
        sc = f.sb("sc", [P, W, K])
        rank = f.sb("rank", [P, W, K])
        gt = f.sb("gt", [P, W])
        s_w, s_st, s_go, s_back = (f.sem(n) for n in ("w", "st", "go", "back"))
        with nc.Block() as block:
            @block.sync
            def _(s):
                for k, row in enumerate((A.r_b, A.r_gam, A.r_bet)):
                    s.dma_start(bg[:, k, :], spread(row)).then_inc(s_w, 16)

            @block.scalar
            def _(s):
                s.wait_ge(s_go, 1)
                s.activation(r[:, :], r[:, :], ACT.Sqrt).then_inc(s_back, 1)
                s.wait_ge(s_go, 2)
                s.activation(sc[:, :, :], sc[:, :, :], ACT.Exp).then_inc(s_back, 1)

            @block.vector
            def _(v):
                st = Steps(v, s_st)

                def wide(t, n):
                    return t.unsqueeze(2).to_broadcast([P, W, n])

                for k in (2, 1):
                    st.then(v.tensor_tensor(R.racc[:, :, 0:FROW], R.racc[:, :, 0:FROW],
                                            R.racc[:, :, k * FROW:(k + 1) * FROW], ALU.add))
                st.then(v.tensor_scalar(z[:, :, :], R.racc[:, :, FX:FROW], 1e-30, None, ALU.max))
                st.then(v.reciprocal(z[:, :, :], z[:, :, :]))
                for h in range(FH):
                    c = slice(h * FC, (h + 1) * FC)
                    st.then(v.tensor_tensor(a[:, :, c], R.racc[:, :, c], wide(z[:, :, h], FC), ALU.mult))
                v.wait_ge(s_w, 48)

                def row(k):
                    return bg[:, k, :].unsqueeze(1).to_broadcast([P, W, FX])

                st.then(v.tensor_tensor(a[:, :, :], a[:, :, :], row(0), ALU.add))
                st.then(v.tensor_reduce(m[:, :], a[:, :, :], AXX, ALU.add))
                st.then(v.tensor_scalar(m[:, :], m[:, :], 1.0 / FX, None, ALU.mult))
                st.then(v.tensor_tensor(a[:, :, :], a[:, :, :], wide(m[:, :], FX), ALU.subtract))
                st.then(v.tensor_tensor(t16[:, :, :], a[:, :, :], a[:, :, :], ALU.mult))
                st.then(v.tensor_reduce(r[:, :], t16[:, :, :], AXX, ALU.add))
                st.then(v.tensor_scalar(r[:, :], r[:, :], 1.0 / FX, LN_EPS, ALU.mult, ALU.add))
                v.sem_inc(s_go, 1)
                v.wait_ge(s_back, 1)
                st.then(v.reciprocal(r[:, :], r[:, :]))
                st.then(v.tensor_tensor(a[:, :, :], a[:, :, :], wide(r[:, :], FX), ALU.mult))
                st.then(v.tensor_tensor(a[:, :, :], a[:, :, :], row(1), ALU.mult))
                st.then(v.tensor_tensor(a[:, :, :], a[:, :, :], row(2), ALU.add))
                st.then(v.tensor_reduce(sc[:, :, :], a[:, :, :].rearrange("p t (h c) -> p t c h", c=FC), AXX, ALU.add))
                st.then(v.tensor_scalar(sc[:, :, :], sc[:, :, :], 1.0 / FH, None, ALU.mult))
                st.then(v.memset(rank[:, :, :], 0.0))
                for k in range(K):
                    for o in range(K):
                        if o != k:
                            st.then(v.tensor_tensor(gt[:, :], sc[:, :, o], sc[:, :, k],
                                                    ALU.is_ge if o < k else ALU.is_gt))
                            st.then(v.tensor_tensor(rank[:, :, k], rank[:, :, k], gt[:, :], ALU.add))
                st.then(v.tensor_scalar(rank[:, :, :], rank[:, :, :], 1.5, None, ALU.is_lt))
                st.then(v.tensor_reduce(m[:, :], sc[:, :, :], AXX, ALU.max))
                st.then(v.tensor_tensor(sc[:, :, :], sc[:, :, :], wide(m[:, :], K), ALU.subtract))
                v.sem_inc(s_go, 1)
                v.wait_ge(s_back, 2)
                st.then(v.tensor_tensor(sc[:, :, :], sc[:, :, :], rank[:, :, :], ALU.mult))
                st.then(v.tensor_reduce(m[:, :], sc[:, :, :], AXX, ALU.add))
                st.then(v.reciprocal(m[:, :], m[:, :]))
                st.then(v.tensor_tensor(R.gate[:, :, 0:K], sc[:, :, :], wide(m[:, :], K), ALU.mult))



class Experts1:
    PRODUCTS = ((("h", 0),), (("y", 0), ("h", 1)), (("y", 1), ("h", 2)), (("y", 2),))
    BANK = {("h", 0): 0, ("y", 0): 1, ("h", 1): 2, ("y", 1): 0, ("h", 2): 1, ("y", 2): 2}
    TAKEN = ((), (("h", 0),), (("y", 0), ("h", 1)), (("y", 1), ("h", 2)), (("y", 2),))
    HB = HID1 // P
    PER = E1 - 1
    def __init__(self, nc, R, A):
        self.nc, self.R, self.A = nc, R, A

    def pieces(self):
        PER = self.PER
        full, rest = divmod(W, PER)
        assert NBUF == PER + 1 and rest > 0
        return [(0, W, [(e, 1, 0) for e in range(PER)]),
                (W, W + full, [(PER, PER, k - PER * W) for k in range(PER)]),
                (W + full, W + full + 1, [(PER, PER, k - PER * W) for k in range(rest)])]

    def stages(self, Q):
        st, last = [], []
        for lo, hi, now in self.pieces():
            st.append((lo, lo + 1, (now, last)))
            if hi > lo + 1:
                st.append((lo + 1, hi, (now, now)))
            last = now
        assert hi < Q
        st.append((hi, hi + 1, ([], last)))
        if hi + 1 < Q:
            st.append((hi + 1, Q, None))
        return st

    def place(self, f):
        self.w1 = f.sb("w1", [P, E1, C, HID1])
        self.w2 = f.sb("w2", [P, E1, self.HB, D])
        self.b1 = f.sb("b1", [P, E1, self.HB])
        self.b2 = f.sb("b2", [P, E1, D])
        self.pre = f.sb("pre", [P, self.PER, HID1])
        self.hid = f.sb("hid", [P, self.PER, HID1])
        self.y = f.sb("y", [P, self.PER, D])
        self.px = f.ps("px", [P, self.PER, 512])
        self.s_w = [f.sem(f"xw{e}") for e in range(E1)]
        self.s_b, self.s_h, self.s_pre, self.s_g, self.s_o, self.s_y = (
            f.sem(n) for n in ("xb", "xh", "xpre", "xg", "xo", "xy"))
        self.s_out = [f.sem(f"xout{k}") for k in range(self.PER)]

    def pool_start(self, g):
        pass

    def vector_start(self, v):
        pass

    def tensor_start(self, t):
        t.sem_inc(self.s_y, 2 * self.PER)
        t.sem_inc(self.s_o, self.PER)

    def tensor(self, t, i, b, work):
        now, last = work
        PER = self.PER
        for what, k in self.PRODUCTS[b]:
            if k >= len(now if what == "h" else last):
                continue
            bank = self.px[:, self.BANK[what, k]]
            if what == "h":
                e, mul, off = now[k]
                t.wait_ge(self.s_w[e], 32)
                t.wait_ge(self.s_y, PER * i + 2 + k)
                for fb in range(self.HB):
                    for c in range(C):
                        mm = t.matmul(bank[:, fb * P:(fb + 1) * P], self.w1[:, e, c, fb * P:(fb + 1) * P],
                                      self.R.XT[:, c, bass.ds((mul * i + off) * P, P)], start=(c == 0),
                                      stop=(c == C - 1))
                mm.then_inc(self.s_h, 1)
            else:
                if k == 0:
                    t.wait_ge(self.s_g, i)
                elif now[k - 1:]:
                    t.wait_ge(self.s_pre, PER * i + k)
                t.wait_ge(self.s_y, PER * i + k + 1)
                for c in range(self.HB):
                    mm = t.matmul(bank[:, 0:D], self.hid[:, k, c * P:(c + 1) * P], self.w2[:, last[k][0], c, :],
                                  start=(c == 0), stop=(c == self.HB - 1))
                mm.then_inc(self.s_o, 1)

    def scalar(self, a, i, b, work):
        n = len(work[1])
        if b == 0 and n:
            a.wait_ge(self.s_pre, self.PER * (i - 1) + n)
            a.wait_ge(self.s_o, self.PER * i)
            a.activation(self.hid[:, 0:n], self.pre[:, 0:n], ACT.Gelu).then_inc(self.s_g, 1)

    def vector(self, v, i, step, work):
        now, last = work
        for what, k in self.TAKEN[step]:
            if k >= len(now if what == "h" else last):
                continue
            bank = self.px[:, self.BANK[what, k]]
            if what == "h":
                v.wait_ge(self.s_h, self.PER * i + k + 1)
                if last:
                    v.wait_ge(self.s_g, i)
                b1 = self.b1[:, now[k][0]].unsqueeze(2).to_broadcast([P, self.HB, P])
                v.tensor_tensor(self.pre[:, k].rearrange("p (f t) -> p f t", t=P),
                                bank.rearrange("p (f t) -> p f t", t=P), b1, ALU.add).then_inc(self.s_pre, 1)
            else:
                v.wait_ge(self.s_o, self.PER * i + k + 1)
                v.wait_ge(self.s_out[k], 16 * i)
                v.tensor_tensor(self.y[:, k], bank[:, 0:D], self.b2[:, last[k][0]], ALU.add).then_inc(self.s_y, 1)

    def sync(self, s):
        s.dma_start(self.b1[:, :, :], self.A.f1_b1).then_inc(self.s_b, 16)
        for e in range(E1):
            s.dma_start(self.b2[:, e], spread(self.A.f1_b2[e])).then_inc(self.s_b, 16)
        s.wait_ge(self.s_b, 16 * (1 + E1))
        for e in range(E1):
            s.dma_start(self.w1[:, e], rows(self.A.f1_w1[e])).then_inc(self.s_w[e], 16)
            s.dma_start(self.w2[:, e], rows(self.A.f1_w2[e])).then_inc(self.s_w[e], 16)
        for k in range(self.PER):
            s.sem_inc(self.s_out[k], 16)

        for lo, hi, now in self.pieces():
            with s.Fori(lo, hi) as i:
                for k in range(len(now)):
                    n = self.PER * i + k
                    s.wait_ge(self.s_y, n + 2 * self.PER + 1)
                    s.dma_start(self.R.ydram[:, bass.ds(n, 1), :].rearrange("p a d -> p (a d)"), self.y[:, k])\
                        .then_inc(self.s_out[k], 16)
        for k in range(self.PER):
            s.wait_ge(self.s_out[k], 16 * (1 + sum(hi - lo for lo, hi, now in self.pieces() if k < len(now))))


def combine1(nc, R, A, out):
    PER = E1 - 1
    with Phase(nc, "exp1") as f:
        ya = f.sb("ya", [P, 2, PER * TPI, D])
        yb = f.sb("yb", [P, 2, TPI, D])
        s_a, s_out = f.sem("a"), f.sem("out")
        s_in = [f.sem(f"in{h}") for h in range(2)]
        with nc.Block() as block:
            @block.sync
            def _(s):
                for i in range(ITER + 1):
                    if i < ITER:
                        if i >= 2:
                            s.wait_ge(s_a, TPI * E1 * (i - 1))
                        s.dma_start(ya[:, i % 2], R.ydram[:, PER * TPI * i:PER * TPI * (i + 1), :])\
                            .then_inc(s_in[i % 2], 16)
                        o = PER * W + TPI * i
                        s.dma_start(yb[:, i % 2], R.ydram[:, o:o + TPI, :]).then_inc(s_in[i % 2], 16)
                    if i >= 1:
                        s.wait_ge(s_a, TPI * E1 * i)
                        o = TPI * (i - 1)
                        n = min(TPI, W - 1 - o)
                        s.dma_start(out[o * P:(o + n) * P, :].rearrange("(t p) d -> p t d", p=P),
                                    R.X[:, o:o + n, :]).then_inc(s_out, 16)
                s.dma_start(out[(W - 1) * P:N, :], R.X[0:N - (W - 1) * P, W - 1, :]).then_inc(s_out, 16)
                s.wait_ge(s_out, 16 * (ITER + 1))

            @block.vector
            def _(v):
                for i in range(ITER):
                    v.wait_ge(s_in[i % 2], 32 * (i // 2 + 1))
                    for e in range(E1):
                        for j in range(TPI):
                            t = TPI * i + j
                            n = TPI * E1 * i + TPI * e + j
                            if e:
                                v.wait_ge(s_a, n - TPI + 1)
                            y = ya[:, i % 2, PER * j + e] if e < PER else yb[:, i % 2, j]
                            v.scalar_tensor_tensor(R.X[:, t], y, R.gate[:, t, e:e + 1], R.X[:, t], ALU.mult, ALU.add)\
                                .then_inc(s_a, 1)



class Shared:
    pass


def build(nc, A, out):
    R = Shared()
    R.tab0 = nc.dram_tensor("tab0", [NP, GCN], F32).ap()
    R.tab1 = nc.dram_tensor("tab1", [NP, GROW], F32).ap()
    R.tabr = nc.dram_tensor("tabr", [NP, FROW], F32).ap()
    R.fsorted = nc.dram_tensor("fsorted", [FE, 2], I32).ap()
    R.ydram = nc.dram_tensor("ydram", [P, E1 * W, D], F32).ap()
    R.wdram = nc.dram_tensor("wdram", [16 * P], I32).ap()
    GT, FT = -(-(GSLOTS + TURN) // P) * P, -(-(FSLOTS + TURN) // P) * P
    with Phase(nc, "all") as f:
        R.ident = f.sb("ident", [P, P])
        R.identb = f.sb("identb", [P, P], BF16)
        R.iota = f.sb("iota", [P, P])
        R.ones = f.sb("ones", [P, P])
        R.mask = f.sb("mask", [P, W])
        R.X = f.sb("X", [P, W, D])
        R.XT = f.sb("XT", [P, C, NP])
        R.weff = f.sb("weff", [P, C, D])
        R.beff = f.sb("beff", [P, C])
        R.kvsum = f.sb("kvsum", [P, 512])
        R.fstart = f.sb("fstart", [P, W])
        R.gmax = f.sb("gmax", [P, GH])
        R.gmaxa = f.sb("gmaxa", [P, GH])
        R.gate = f.sb("gate", [P, W, E0])
        constants(nc, R)
        with Phase(nc, "graph") as g:
            R.gstart = g.sb("gstart", [P, W])
            R.nsrc = g.sb("nsrc", [P, W])
            R.adst = g.sb("adst", [P, W, GH])
            R.gsrc = g.sb("gsrc", [P, GT])
            R.gdst = g.sb("gdst", [P, GT], BF16)
            R.gwin = g.sb("gwin", [1, GT], I32)
            R.gwinn = g.sb("gwinn", [1, GT], I32)
            with Phase(nc, "fedge") as fe:
                R.frec = fe.sb("frec", [P, FB, 2], I32)
                R.fpos = fe.sb("fpos", [P, FB])
                degrees(nc, R, A)
                slot_tables(nc, R, "gslot", R.gstart, A.grec, GB, GT, R.gsrc, R.gdst, R.gwin, R.gwinn)
                kv_phase(nc, R, A, 0)
                fold0(nc, R, A)
                with Phase(nc, "gcn") as h:
                    R.gcn = h.sb("sum", [P, W, GCN + 1])
                    clear(nc, R.gcn[:, :, :])
                    edges(nc, R, "gcne", R.tab0, GSLOTS, R.gsrc, R.gdst, R.gwin, R.gwinn, R.gcn,
                          beside=Layer0Work(nc, R, A))
                    gcn_finish(nc, R, A)
                gates0(nc, R, A)
                experts0(nc, R, A)
            kv_phase(nc, R, A, 1)
            fold1(nc, R, A)
            with Phase(nc, "gat") as h:
                R.gat = h.sb("sum", [P, W, GROW])
                gat3 = h.sb("adst3", [P, W, 3 * GH], BF16)
                loops(nc, R, "gloop", R.tab1, R.gat, GH, GC, R.adst, gat3, R.gmaxa)
                edges(nc, R, "gate", R.tab1, GSLOTS, R.gsrc, R.gdst, R.gwin, R.gwinn, R.gat, GH, GC, gat3, R.gmaxa)
                finish1(nc, R, A)
        with Phase(nc, "router") as g:
            R.rsrc = g.sb("rsrc", [P, FT])
            R.rdrel = g.sb("rdrel", [P, FT], BF16)
            R.rwin = g.sb("rwin", [1, FT], I32)
            R.rwinn = g.sb("rwinn", [1, FT], I32)
            R.rext = g.sb("rext", [P, W, FROW + FH])
            R.rdst = g.sb("rdst", [P, W, FH])
            R.rmax = g.sb("rmax", [P, FH])
            R.racc = g.sb("racc", [P, W, 3 * FROW])
            rdst3 = g.sb("rdst3", [P, W, 3 * FH], BF16)
            router_table(nc, R, A)
            slot_tables(nc, R, "fslot", R.fstart, R.fsorted.rearrange("(b e) k -> b (e k)", e=P), FB, FT, R.rsrc,
                        R.rdrel, R.rwin, R.rwinn)
            loops(nc, R, "rloop", R.tabr, R.racc, FH, FC, R.rdst, rdst3, R.rmax)
            edges(nc, R, "rtr", R.tabr, FSLOTS, R.rsrc, R.rdrel, R.rwin, R.rwinn, R.racc, FH, FC, rdst3, R.rmax,
                  split=True, beside=Experts1(nc, R, A))
            router_gates(nc, R, A)
            combine1(nc, R, A, out)


def kernel(**inputs):
    import numpy as np
    import concourse.bacc as bacc
    from concourse.bass_utils import run_bass_kernel_spmd as run

    g = {k: np.asarray(v) for k, v in inputs.items()}
    pad = np.full(GB * P - GE, PAD_NODE, np.int32)
    src, dst = np.concatenate([g["src"], pad]), np.concatenate([g["dst"], pad])
    qkv0 = g["L0_mix_w_qkv"].reshape(D, HEADS, 3, HC0)
    bqkv0 = g["L0_mix_b_qkv"].reshape(HEADS, 3, HC0)
    qkv1 = g["L1_mix_w_qkv"]
    inner = HEADS * HC1

    def cols(b):
        return b.reshape(-1, P).T

    bn = [[g[f"L0_ffn_{n}{k}"].reshape(E0 * C, P).T for n in ("b", "g", "be", "m", "v")] for k in (1, 2)]
    given = dict(
        x=g["x"],
        gsrc_t=src.reshape(GB, P).T, gdst_t=dst.reshape(GB, P).T,
        grec=np.stack([src, dst], -1).reshape(GB, 2 * P),
        ffn_edges=g["L1_ffn_edge_index"].T.reshape(P, FB, 2),
        gcn_w=g["L0_gnn_W_gcn"], gcn_b=g["L0_gnn_b_gcn"], gcn_wout=g["L0_gnn_W_out"], gcn_bout=g["L0_gnn_b_out"][None],
        m0_kv=np.concatenate([qkv0[:, :, 1].reshape(D, D), qkv0[:, :, 2].reshape(D, D)], 1),
        m0_wqt=qkv0[:, :, 0].reshape(D, D).T,
        m0_bkv=np.concatenate([bqkv0[:, 1].reshape(D), bqkv0[:, 2].reshape(D)]),
        m0_bq_t=cols(bqkv0[:, 0].reshape(D)),
        m0_gam=np.stack([g["L0_mix_kln_g"], g["L0_mix_vln_g"]]), m0_bet=np.stack([g["L0_mix_kln_b"], g["L0_mix_vln_b"]]),
        m0_w1=g["L0_mix_w1"], m0_b1_t=cols(g["L0_mix_b1"]), m0_w2=g["L0_mix_w2"], m0_b2=g["L0_mix_b2"][None],
        f0_wr=g["L0_ffn_Wr"], f0_br=g["L0_ffn_br"], f0_w1=g["L0_ffn_W1"], f0_w2=g["L0_ffn_W2"], f0_wo=g["L0_ffn_Wo"],
        f0_bo=g["L0_ffn_bo"], f0_bn=np.stack([np.stack(k, 1) for k in bn], 1),
        gat_w=g["L1_gnn_W"], gat_src=g["L1_gnn_att_src"].reshape(-1), gat_dst=g["L1_gnn_att_dst"].reshape(-1),
        gat_bias=g["L1_gnn_bias"][None],
        m1_kv=qkv1[:, inner:], m1_wqt=qkv1[:, :inner].T, m1_wout=g["L1_mix_w_out"], m1_bout=g["L1_mix_b_out"][None],
        r_w=g["L1_ffn_W_gat"], r_src=g["L1_ffn_att_src"].reshape(-1), r_dst=g["L1_ffn_att_dst"].reshape(-1),
        r_b=g["L1_ffn_b_gat"], r_gam=g["L1_ffn_ln_gamma"], r_bet=g["L1_ffn_ln_beta"],
        f1_w1=g["L1_ffn_W1"], f1_b1=g["L1_ffn_b1"].reshape(E1, -1, P).transpose(2, 0, 1), f1_w2=g["L1_ffn_W2"],
        f1_b2=g["L1_ffn_b2"],
    )
    nc = bacc.Bacc("TRN2", target_bir_lowering=False, num_devices=1)
    arrays, A = {}, Shared()
    for name, a in given.items():
        a = np.ascontiguousarray(a)
        arrays[f"in_{name}"] = a
        A.__dict__[name] = nc.dram_tensor(f"in_{name}", a.shape, mybir.dt.from_np(a.dtype), kind="ExternalInput").ap()
    out = nc.dram_tensor("out", [N, D], F32, kind="ExternalOutput").ap()
    build(nc, A, out)
    r = run(nc, [arrays], core_ids=[0])
    return r.results[0]["out"]
```
